# Optimizing a Trainium2 kernel written in Bass

```python
import numpy as np
import jax
import jax.numpy as jnp

def _softmax(x, axis=-1):
    return jax.nn.softmax(x, axis=axis)

def _gelu(x):
    return jax.nn.gelu(x, approximate=True)

def _silu(x):
    return jax.nn.silu(x)

def _sigmoid(x):
    return jax.nn.sigmoid(x)

def _layernorm(x, axis=-1, eps=1e-05):
    m = jnp.mean(x, axis=axis, keepdims=True)
    v = jnp.var(x, axis=axis, keepdims=True)
    return (x - m) / jnp.sqrt(v + eps)

def _scatter_add(tgt, idx, src, axis=0):
    return tgt.at[idx].add(src)

def _segment_sum(src, seg, n):
    return jax.ops.segment_sum(src, seg, n)
kernel_name = 'mk_gnn_resnorm_d4_gnn_r8_39497f'

def setup_inputs(seed: int=0):
    np.random.seed(seed)
    _w = jnp.asarray

    def _rec_inputs():
        import jax
        import jax.numpy as jnp
        _gk = jax.random.key(seed)
        x = -0.000202 + 1 * jax.random.normal(jax.random.fold_in(_gk, 1), (12500, 64), jnp.float32)
        src = jax.random.randint(jax.random.fold_in(_gk, 2), (200000,), 0, 12500, jnp.int32)
        dst = jax.random.randint(jax.random.fold_in(_gk, 3), (200000,), 0, 12500, jnp.int32)
        _o = jnp.argsort(dst, stable=True)
        src = src[_o]
        dst = dst[_o]
        edge_attr_16 = 0.000196303 + 1.00016 * jax.random.normal(jax.random.fold_in(_gk, 12), (200000, 16), jnp.float32)
        edge_attr_32 = -5.16925e-05 + 1.00005 * jax.random.normal(jax.random.fold_in(_gk, 13), (200000, 32), jnp.float32)
        edge_weight = jax.random.uniform(jax.random.fold_in(_gk, 15), (200000,), jnp.float32, 0.0, 0.999999)
        return (x, src, dst, edge_attr_16, edge_attr_32, edge_weight)
    x, src, dst, edge_attr_16, edge_attr_32, edge_weight = _rec_inputs()

    def _L0_gnn_setup():
        import jax, jax.numpy as jnp
        import numpy as np
        N_NODES = 12500
        N_EDGES = 200000
        D_FEAT = 64
        key = jax.random.key(seed)
        k1, k2, k3 = jax.random.split(key, 3)
        x = jax.random.normal(k1, (N_NODES, D_FEAT), dtype=jnp.float32)
        edge_index = jax.random.randint(k2, (2, N_EDGES), 0, N_NODES, dtype=jnp.int64)
        edge_attr = jax.random.uniform(k3, (N_EDGES,), dtype=jnp.float32)
        return {'x': x, 'edge_index': edge_index, 'edge_attr': edge_attr}
    _L0_gnn_all = _L0_gnn_setup()
    _L0_gnn_in = {k: v for k, v in _L0_gnn_all.items() if k in ()}
    del _L0_gnn_all

    def _L1_gnn_setup():
        import jax, jax.numpy as jnp
        import numpy as np
        N_NODES = 12500
        N_EDGES = 400000
        EDGE_OUT = 32
        HID = 128
        NODE_OUT = 64
        N_GRAPHS = 16
        key = jax.random.key(seed)
        ks = jax.random.split(key, 9)
        x = jax.random.normal(ks[0], (N_NODES, 64), dtype=jnp.float32)
        edge_index = jax.random.randint(ks[1], (2, N_EDGES), 0, N_NODES, dtype=jnp.int64)
        edge_attr = jax.random.normal(ks[2], (N_EDGES, EDGE_OUT), dtype=jnp.float32)
        u = jax.random.normal(ks[3], (N_GRAPHS, 1), dtype=jnp.float32)
        batch = jnp.sort(jax.random.randint(ks[4], (N_NODES,), 0, N_GRAPHS, dtype=jnp.int64))
        d_in = 3 * EDGE_OUT + 1
        W1 = jax.random.normal(ks[5], (d_in, HID), dtype=jnp.float32) / np.sqrt(d_in)
        b1 = jnp.zeros((HID,), dtype=jnp.float32)
        W2 = jax.random.normal(ks[6], (HID, NODE_OUT), dtype=jnp.float32) / np.sqrt(HID)
        b2 = jnp.zeros((NODE_OUT,), dtype=jnp.float32)
        return {'x': x, 'edge_index': edge_index, 'edge_attr': edge_attr, 'u': u, 'batch': batch, 'W1': W1, 'b1': b1, 'W2': W2, 'b2': b2}
    _L1_gnn_all = _L1_gnn_setup()
    _L1_gnn_in = {k: v for k, v in _L1_gnn_all.items() if k in ('u', 'W1', 'b1', 'W2', 'b2')}
    del _L1_gnn_all

    def _L2_gnn_setup():
        import jax, jax.numpy as jnp
        import numpy as np
        N_NODES = 12500

        def gcn_conv(x, edge_index, W, b, num_nodes):
            src = jnp.concatenate([edge_index[0], jnp.arange(num_nodes, dtype=edge_index.dtype)])
            dst = jnp.concatenate([edge_index[1], jnp.arange(num_nodes, dtype=edge_index.dtype)])
            deg = jax.ops.segment_sum(jnp.ones_like(dst, dtype=x.dtype), dst, num_segments=num_nodes)
            dinv = jnp.where(deg > 0, jax.lax.rsqrt(deg), 0.0)
            norm = dinv[src] * dinv[dst]
            h = x @ W
            msg = h[src] * norm[:, None]
            out = jax.ops.segment_sum(msg, dst, num_segments=num_nodes)
            return out + b
        key = jax.random.key(seed)
        k1, k2, k3, k4, k5, k6 = jax.random.split(key, 6)
        d_in, d_hid, d_out = (64, 64, 64)
        x = jax.random.normal(k1, (N_NODES, d_in), dtype=jnp.float32)
        edge_index = jax.random.randint(k2, (2, 125000), 0, N_NODES, dtype=jnp.int64)
        W1 = jax.random.normal(k3, (d_in, d_hid), dtype=jnp.float32) / np.sqrt(d_in)
        b1 = jnp.zeros((d_hid,), dtype=jnp.float32)
        W2 = jax.random.normal(k4, (d_hid, d_out), dtype=jnp.float32) / np.sqrt(d_hid)
        b2 = jnp.zeros((d_out,), dtype=jnp.float32)
        return {'x': x, 'edge_index': edge_index, 'W1': W1, 'b1': b1, 'W2': W2, 'b2': b2}
    _L2_gnn_all = _L2_gnn_setup()
    _L2_gnn_in = {k: v for k, v in _L2_gnn_all.items() if k in ('W1', 'b1', 'W2', 'b2')}
    del _L2_gnn_all

    def _L3_gnn_setup():
        import jax, jax.numpy as jnp
        import numpy as np
        N, E = (12500, 200000)
        IN_DIM, OUT_DIM, EDGE_DIM, H = (64, 64, 16, 4)
        HD = OUT_DIM // H
        NEG_SLOPE = 0.2
        EPS_SOFTMAX = 1e-08
        EPS_LN = 1e-05
        key = jax.random.key(seed)
        ks = jax.random.split(key, 8)
        return {'x': jax.random.normal(ks[0], (N, IN_DIM), jnp.float32), 'edge_index': jax.random.randint(ks[1], (2, E), 0, N, jnp.int64 if jax.config.jax_enable_x64 else jnp.int32), 'edge_attr': jax.random.normal(ks[2], (E, EDGE_DIM), jnp.float32), 'W_node': jax.random.normal(ks[3], (IN_DIM, OUT_DIM), jnp.float32) / np.sqrt(IN_DIM), 'W_edge': jax.random.normal(ks[4], (EDGE_DIM, H), jnp.float32) / np.sqrt(EDGE_DIM), 'attn_src': jax.random.normal(ks[5], (H, HD), jnp.float32), 'attn_dst': jax.random.normal(ks[6], (H, HD), jnp.float32), 'ln_gamma': jnp.ones((OUT_DIM,), jnp.float32), 'ln_beta': jnp.zeros((OUT_DIM,), jnp.float32)}
    _L3_gnn_all = _L3_gnn_setup()
    _L3_gnn_in = {k: v for k, v in _L3_gnn_all.items() if k in ('W_node', 'W_edge', 'attn_src', 'attn_dst', 'ln_gamma', 'ln_beta')}
    del _L3_gnn_all
    return {'x': x, 'src': src, 'dst': dst, 'edge_attr_16': edge_attr_16, 'edge_attr_32': edge_attr_32, 'edge_weight': edge_weight, 'L1_gnn_u': _L1_gnn_in['u'], 'L1_gnn_W1': _L1_gnn_in['W1'], 'L1_gnn_b1': _L1_gnn_in['b1'], 'L1_gnn_W2': _L1_gnn_in['W2'], 'L1_gnn_b2': _L1_gnn_in['b2'], 'L2_gnn_W1': _L2_gnn_in['W1'], 'L2_gnn_b1': _L2_gnn_in['b1'], 'L2_gnn_W2': _L2_gnn_in['W2'], 'L2_gnn_b2': _L2_gnn_in['b2'], 'L3_gnn_W_node': _L3_gnn_in['W_node'], 'L3_gnn_W_edge': _L3_gnn_in['W_edge'], 'L3_gnn_attn_src': _L3_gnn_in['attn_src'], 'L3_gnn_attn_dst': _L3_gnn_in['attn_dst'], 'L3_gnn_ln_gamma': _L3_gnn_in['ln_gamma'], 'L3_gnn_ln_beta': _L3_gnn_in['ln_beta']}

def reference(x, src, dst, edge_attr_16, edge_attr_32, edge_weight, L1_gnn_u, L1_gnn_W1, L1_gnn_b1, L1_gnn_W2, L1_gnn_b2, L2_gnn_W1, L2_gnn_b1, L2_gnn_W2, L2_gnn_b2, L3_gnn_W_node, L3_gnn_W_edge, L3_gnn_attn_src, L3_gnn_attn_dst, L3_gnn_ln_gamma, L3_gnn_ln_beta):
    import jax
    import jax.numpy as jnp

    def _L0_gnn_ref(x, edge_index, edge_attr):
        import jax, jax.numpy as jnp
        import numpy as np
        N_NODES = 12500
        N_EDGES = 200000
        D_FEAT = 64
        row, col = (edge_index[0], edge_index[1])
        B = jnp.exp(-edge_attr)
        msgs = B[:, None] * x[col]
        out = jax.ops.segment_sum(msgs, row, num_segments=N_NODES)
        return out

    def _L1_gnn_ref(x, edge_index, edge_attr, u, batch, W1, b1, W2, b2):
        import jax, jax.numpy as jnp
        import numpy as np
        N_NODES = 12500
        N_EDGES = 400000
        EDGE_OUT = 32
        HID = 128
        NODE_OUT = 64
        N_GRAPHS = 16
        N = x.shape[0]
        row = edge_index[0]
        seg_sum = jax.ops.segment_sum(edge_attr, row, num_segments=N)
        seg_max = jax.ops.segment_max(edge_attr, row, num_segments=N)
        cnt = jax.ops.segment_sum(jnp.ones((edge_attr.shape[0], 1), edge_attr.dtype), row, num_segments=N)
        seg_mean = seg_sum / jnp.maximum(cnt, 1.0)
        seg_max = jnp.where(cnt > 0, seg_max, 0.0)
        h = jnp.concatenate([seg_sum, seg_max, seg_mean, u[batch]], axis=1)
        h = jax.nn.relu(h @ W1 + b1)
        return h @ W2 + b2

    def _L2_gnn_ref(x, edge_index, W1, b1, W2, b2):
        import jax, jax.numpy as jnp
        import numpy as np
        N_NODES = 12500

        def gcn_conv(x, edge_index, W, b, num_nodes):
            src = jnp.concatenate([edge_index[0], jnp.arange(num_nodes, dtype=edge_index.dtype)])
            dst = jnp.concatenate([edge_index[1], jnp.arange(num_nodes, dtype=edge_index.dtype)])
            deg = jax.ops.segment_sum(jnp.ones_like(dst, dtype=x.dtype), dst, num_segments=num_nodes)
            dinv = jnp.where(deg > 0, jax.lax.rsqrt(deg), 0.0)
            norm = dinv[src] * dinv[dst]
            h = x @ W
            msg = h[src] * norm[:, None]
            out = jax.ops.segment_sum(msg, dst, num_segments=num_nodes)
            return out + b
        n = x.shape[0]
        h = jax.nn.relu(gcn_conv(x, edge_index, W1, b1, n))
        out = jax.nn.relu(gcn_conv(h, edge_index, W2, b2, n))
        return out

    def _L3_gnn_ref(x, edge_index, edge_attr, W_node, W_edge, attn_src, attn_dst, ln_gamma, ln_beta):
        import jax, jax.numpy as jnp
        import numpy as np
        N, E = (12500, 200000)
        IN_DIM, OUT_DIM, EDGE_DIM, H = (64, 64, 16, 4)
        HD = OUT_DIM // H
        NEG_SLOPE = 0.2
        EPS_SOFTMAX = 1e-08
        EPS_LN = 1e-05
        n = x.shape[0]
        src, dst = (edge_index[0], edge_index[1])
        h = (x @ W_node).reshape(n, H, HD)
        a_src_node = jnp.einsum('nhd,hd->nh', h, attn_src)
        a_dst_node = jnp.einsum('nhd,hd->nh', h, attn_dst)
        e_score = edge_attr @ W_edge
        attn = a_src_node[src] + a_dst_node[dst] + e_score
        attn = jnp.where(attn >= 0, attn, NEG_SLOPE * attn)
        attn_max = jnp.zeros((n, H), attn.dtype).at[dst].max(attn)
        attn = jnp.exp(attn - attn_max[dst])
        attn_sum = jnp.zeros((n, H), attn.dtype).at[dst].add(attn)
        attn = attn / (attn_sum[dst] + EPS_SOFTMAX)
        msg = h[src] * attn[:, :, None]
        out = jnp.zeros((n, H, HD), h.dtype).at[dst].add(msg).reshape(n, OUT_DIM)
        y = out + h.reshape(n, OUT_DIM)
        mu = jnp.mean(y, axis=-1, keepdims=True)
        var = jnp.mean((y - mu) ** 2, axis=-1, keepdims=True)
        return (y - mu) * jax.lax.rsqrt(var + EPS_LN) * ln_gamma + ln_beta
    edge_index = jnp.stack([src, dst])
    batch0 = jnp.zeros((12500,), jnp.int32)
    x = _layernorm(x + _L0_gnn_ref(x, edge_index, edge_weight), axis=-1)
    x = _layernorm(x + _L1_gnn_ref(x, edge_index, edge_attr_32, L1_gnn_u, batch0, L1_gnn_W1, L1_gnn_b1, L1_gnn_W2, L1_gnn_b2), axis=-1)
    x = _layernorm(x + _L2_gnn_ref(x, edge_index, L2_gnn_W1, L2_gnn_b1, L2_gnn_W2, L2_gnn_b2), axis=-1)
    x = _layernorm(x + _L3_gnn_ref(x, edge_index, edge_attr_16, L3_gnn_W_node, L3_gnn_W_edge, L3_gnn_attn_src, L3_gnn_attn_dst, L3_gnn_ln_gamma, L3_gnn_ln_beta), axis=-1)
    return x

_drawn_inputs = setup_inputs


def setup_inputs(seed=0):
    import zlib

    import numpy as np

    out = dict(_drawn_inputs(seed))
    spreads = {'L1_gnn_b1': (0.0, 0.1),
     'L1_gnn_b2': (0.0, 0.1),
     'L2_gnn_b1': (0.0, 0.1),
     'L2_gnn_b2': (0.0, 0.1),
     'L3_gnn_ln_gamma': (1.0, 0.2),
     'L3_gnn_ln_beta': (0.0, 0.1)}
    factors = {}
    for name, (base, spread) in spreads.items():
        noise = np.random.default_rng([zlib.crc32(name.encode()), seed]).standard_normal(out[name].shape)
        drawn = base * np.exp(spread * noise) if base else spread * noise
        out[name] = jnp.asarray(drawn.astype(out[name].dtype))
    for name, factor in factors.items():
        out[name] = (out[name] * factor).astype(out[name].dtype)
    return out
```

```python
import concourse.bass as bass
from concourse import mybir
from contextlib import ExitStack

P = 128
N_NODES, N_EDGES, D = 12500, 200000, 64
KN = -(-N_NODES // P)
NP = KN * P
J = 16
Q = 4
NB = -(-N_EDGES // (P * 2 * J))
L = NB * 2 * J
EP = P * L
E32, E16, HEADS, HID = 32, 16, 4, 128
HD = D // HEADS
LOW = 128
HIGH = NP // LOW
TW = D + E32 + 1
W01 = D + 2 * E32
W3 = D + HEADS
W3S = D + 2 * HEADS
GT = 7
NG = KN // GT
HUGE = 3.4e38
NOWHERE = float(1 << 22)

f32, bf16, i32 = mybir.dt.float32, mybir.dt.bfloat16, mybir.dt.int32
ALU, ACT, AX = mybir.AluOpType, mybir.ActivationFunctionType, mybir.AxisListType
AT = bass.IndirectOffsetOnAxis


ADDED = {
    "state": 2 * NB, "stored0": 16 * NB, "stored1": 16 * NB, "gathered0": 16 * J * NB, "gathered1": 16 * J * NB,
    "idx0": 16 * NB, "idx1": 16 * NB, "diag": NG, "keys": NG, "pick": NG, "carried": NG, "lk": NG, "grp": NG,
    "turned": NG, "prod": NG, "out_read": NG, "group_t": 2 * NG, "var": 1, "root": 1, "nodes_in": 16 * KN,
    "chunk_end": 1, "end_t": 1, "carry": 1, "carry_t": 1, "table": 1, "table_out": 16, "conv": 1, "relu": 1,
    "onehots": 2 * NB, "onehots_used": 2 * NB, "flag": 1, "flagrow": 1, "chain": 2 * J * NB,
}
PASSES, CONVS = ("src", "c1", "c2", "at"), ("c1", "c2", "at")
ORDER = dict.fromkeys(ADDED, PASSES)
ORDER.update(dict.fromkeys(("gathered0", "gathered1", "idx0", "idx1", "table", "table_out", "conv", "relu", "chain"),
                           CONVS))
ORDER.update(dict.fromkeys(("grp", "turned", "prod", "out_read", "group_t"), ("mlp",) + CONVS))
ORDER.update(dict.fromkeys(("var", "root"), ("ln0", "ln1", "ln2", "ln3a", "ln3")))
ORDER.update(dict.fromkeys(("onehots", "onehots_used"), ("dst", "src")))
ORDER.update(dict.fromkeys(("flag", "flagrow"), ("dst", "src")))


def upto(stage, name):
    return ORDER[name].index(stage) * ADDED[name]


def later(i):
    return not isinstance(i, int) or i > 0


def turns(eng, body, n=NB, peel=1, peel_last=False):
    for i in range(peel):
        body(i)
    with eng.Fori(peel, n - peel_last) as i:
        body(i)
    if peel_last:
        body(n - 1)


class Steps:

    def __init__(self, sem, per, base=0):
        self.sem, self.per, self.base = sem, per, base

    def turn(self, i):
        self.i, self.k = i, 0

    def done(self, ins):
        ins.then_inc(self.sem, 1)
        self.k += 1
        return self.k

    def value(self, k):
        return self.i * self.per + (k + self.base)


def bc(ap, n):
    return ap.rearrange("p (a o) -> p a o", o=1).to_broadcast([ap.shape[0], ap.shape[1], n])


def bf(ap, n):
    return ap.rearrange("p (o a) -> p o a", o=1).to_broadcast([ap.shape[0], n, ap.shape[1]])


def program(nc, a, out):
    with ExitStack() as ctx:
        def sb(name, shape, dt=f32):
            return ctx.enter_context(nc.sbuf_tensor(name, shape, dt))

        def ps(name, shape):
            return ctx.enter_context(nc.psum_tensor(name, shape, f32))

        def sem(name):
            return ctx.enter_context(nc.semaphore(name))

        def dram(name, shape, dt=f32):
            return nc.dram_tensor(name, shape, dt, kind="Internal").ap()

        x_at_start = dram("x_at_start", (EP, D))
        adst_at_start = dram("adst_at_start", (EP, HEADS))
        by_src = dram("by_src", (EP, TW))
        states = {g: dram(f"states_{g}", (EP, w)) for g, w in
                  (("src", W01), ("c1", D), ("c2", D), ("at", W3S))}
        table = {"c1": dram("table_c1", (NP, D)), "c2": dram("table_c2", (NP, D)),
                 "at": dram("table_at", (NP, W3))}
        adst_table = dram("adst_table", (NP, HEADS))
        bound = {(o, w): dram(f"{w}_{o}", (HIGH, LOW)) for o in ("src", "dst") for w in ("start", "end")}

        x = sb("x", [P, KN * D])
        hrows = sb("hrows", [P, KN * W3])
        arena_a = sb("arena_a", [P, KN * W01])
        arena_b = sb("arena_b", [P, KN * W01])
        dst_i = sb("dst_i", [P, L + 1], i32)
        src_f = sb("src_f", [P, L + J])
        digits = {(o, w): sb(f"{w}_{o}", [P, L + J], bf16) for o in ("src", "dst") for w in ("hi", "lo")}
        same_dst = sb("same_dst", [P, L])
        decay = sb("decay", [P, L])
        iota_i = sb("iota_i", [P, P], i32)
        rowno_i = sb("rowno_i", [P, 1], i32)
        iota = sb("iota", [P, P])
        rowno = sb("rowno", [P, 1])
        rowno_l = sb("rowno_l", [P, 1])
        ident = sb("ident", [P, P])
        ident_b = sb("ident_b", [P, P], bf16)
        before = sb("before", [P, P])
        after = sb("after", [P, P])
        ones = sb("ones", [P, P])
        zero_b = sb("zero_b", [P, P], bf16)
        base = sb("base", [HIGH, LOW])
        hist_sb = sb("hist_sb", [HIGH, LOW])
        ends_sb = sb("ends_sb", [HIGH, LOW])
        offs_sb = sb("offs_sb", [HIGH, 1])
        nstart = {o: sb(f"nstart_{o}", [P, KN]) for o in ("src", "dst")}
        nend = {o: sb(f"nend_{o}", [P, KN]) for o in ("src", "dst")}
        has = {o: sb(f"has_{o}", [P, KN]) for o in ("src", "dst")}
        key = {o: sb(f"key_{o}", [P, KN]) for o in ("src", "dst")}
        end_i = {o: sb(f"end_i_{o}", [P, KN], i32) for o in ("src", "dst")}
        start_i = sb("start_i", [P, KN], i32)
        quot_i = sb("quot_i", [P, KN], i32)
        tmpk = sb("tmpk", [P, KN])
        degree = sb("degree", [P, KN])
        dinv = sb("dinv", [P, KN])
        flagrow = {o: sb(f"flagrow_{o}", [P, P]) for o in ("src", "dst")}
        flag = sb("flag", [P, 1])
        diag = sb("diag", [P, P])
        edge_ends = sb("edge_ends", [P, 3])
        chunk_end = sb("chunk_end", [P, W01])
        chunk_in_t = sb("chunk_in_t", [P, P + 1])
        chunk_max_t = sb("chunk_max_t", [P, P + 1])
        chunk_t1 = sb("chunk_t1", [P, P])
        chunk_t2 = sb("chunk_t2", [P, P])
        chunk_in = sb("chunk_in", [P, W01])
        stat1 = sb("stat1", [P, KN])
        stat2 = sb("stat2", [P, KN])
        w1 = sb("w1", [3 * E32, HID])
        w1u = sb("w1u", [HID, 1])
        b1 = sb("b1", [HID, 1])
        u0 = sb("u0", [HID, 1])
        w2 = sb("w2", [HID, D])
        b2 = sb("b2", [P, D])
        wc = {"c1": sb("wc1", [D, D]), "c2": sb("wc2", [D, D]), "at": sb("wnode", [D, D])}
        bcv = {"c1": sb("bc1", [P, D]), "c2": sb("bc2", [P, D])}
        wedge = sb("wedge", [P, E16 * HEADS])
        asrc_w = sb("asrc_w", [P, D])
        adst_w = sb("adst_w", [P, D])
        gamma = sb("gamma", [P, D])
        beta = sb("beta", [P, D])
        first_row = sb("first_row", [P, D])
        first_adst = sb("first_adst", [P, HEADS])
        mask_blk = sb("mask_blk", [P, 2, J])
        cap_blk = sb("cap_blk", [P, 2, J])
        idx_blk = [sb(f"idx_blk{h}", [P, J], i32) for h in range(2)]
        rank_blk = sb("rank_blk", [P, 2, J])
        sel_blk = sb("sel_blk", [P, 2, J])
        digit_blk = {w: [sb(f"digit_{w}{h}", [P, J], bf16) for h in range(2)] for w in ("hi", "lo")}
        src_blk = sb("src_blk", [P, 2, J])
        prev_src = sb("prev_src", [P, 1])

        def carve(tensor, parts, dt=f32):
            at, got = 0, {}
            for name, size in parts:
                got[name] = tensor[:, at:at + size]
                at += size
            assert at <= tensor.shape[1], at
            return got

        cut = carve(arena_b, [("onehot", 2 * J * (LOW + HIGH) // 2), ("rows0", J * TW), ("rows1", J * TW),
                              ("xs0", J * D), ("xs1", J * D), ("xb0", J * D), ("xb1", J * D),
                              ("junk", 2 * P), ("hi_t", 2 * Q * P), ("snap", 2 * P)])
        oh = cut["onehot"].bitcast(bf16)
        oh_hi = [oh[:, h * J * (LOW + HIGH):][:, :J * HIGH].rearrange("p (n t) -> p n t", t=J) for h in range(2)]
        oh_lo = [oh[:, h * J * (LOW + HIGH) + J * HIGH:][:, :J * LOW].rearrange("p (n t) -> p n t", t=J)
                 for h in range(2)]
        rows = [cut[f"rows{h}"].rearrange("p (j f) -> p j f", f=TW) for h in range(2)]
        xs = [cut[f"xs{h}"].rearrange("p (j f) -> p j f", f=D) for h in range(2)]
        xb = [cut[f"xb{h}"].rearrange("p (j f) -> p j f", f=D) for h in range(2)]
        junk = [cut["junk"].bitcast(bf16)[:, q * P:(q + 1) * P] for q in range(4)]
        hi_t = [cut["hi_t"][0:HIGH, q * Q * P:(q + 1) * Q * P] for q in range(2)]
        snap = [cut["snap"][0:HIGH, q * P:(q + 1) * P] for q in range(2)]
        early = carve(arena_a, [("zeros", J * D), ("ih", J * HIGH // 2), ("il", J * LOW // 2)])
        zeros = early["zeros"]
        iota_hi = early["ih"].bitcast(bf16).rearrange("p (n t) -> p n t", t=J)
        iota_lo = early["il"].bitcast(bf16).rearrange("p (n t) -> p n t", t=J)
        late = carve(hrows, [("tb0", J * TW), ("tb1", J * TW)])
        tb = [late[f"tb{h}"].rearrange("p (j f) -> p j f", f=TW) for h in range(2)]
        late = carve(arena_a, [("st0", J * W01), ("st1", J * W01), ("g0", J * W3), ("g1", J * W3),
                               ("a16_0", J * E16), ("a16_1", J * E16), ("prod", J * HEADS * E16),
                               ("sc", J * HEADS), ("mx", (J + 1) * HEADS),
                               ("ex", J * HEADS), ("cf", J * W3), ("tmp", 2 * W3), ("lk", J * HEADS)])
        st = [late[f"st{h}"] for h in range(2)]
        gb = [late[f"g{h}"] for h in range(2)]
        a16 = [late[f"a16_{h}"].rearrange("p (j f) -> p j f", f=E16) for h in range(2)]

        bank = [ps(f"bank{n}", [P, 512]) for n in range(8)]
        hist = bank[0][0:HIGH, 0:LOW]
        p_hi_t = [bank[1][0:HIGH, :], bank[2][0:HIGH, :]]
        p_src = [bank[3], bank[4]]
        p_cnt = [bank[5], bank[6]]
        p_small = bank[7]

        S = {}

        def s(name):
            if name not in S:
                S[name] = sem(name)
            return S[name]

        mrep = chunk_max_t[:, 0:W3S]

        def diagonals(g):
            return hrows[:, 0:GT * P] if g == "src" else arena_b[:, KN * W01 - GT * P:]

        block = ctx.enter_context(nc.Block())

        def rows_of(dram_ap, w):
            return dram_ap.rearrange("(p l) w -> p (l w)", p=P)

        def scattered(i, h):
            return i * (16 * J)

        def blk(i, h):
            return i * 2 + h

        @block.sync
        def _(sp):
            src_v = a["src"].rearrange("(p l) -> p l", p=P)
            dst_v = a["dst"].rearrange("(p l) -> p l", p=P)
            sp.dma_start(arena_b[:, 0:L].bitcast(i32), src_v).then_inc(s("src_loaded"), 16)
            sp.dma_start(dst_i[:, 1:L + 1], dst_v).then_inc(s("dst_loaded"), 16)
            sp.wait_ge(s("dst_col0"), 1)
            sp.dma_start(dst_i[1:P, 0:1], dst_v[0:P - 1, L - 1:L], allow_slow_non_contiguous=True).then_inc(s("dst_loaded"), 16)
            sp.dma_start(decay[:, :], a["w"].rearrange("(p l) -> p l", p=P)).then_inc(s("w_loaded"), 16)
            sp.dma_start(x[:, :], a["x"].rearrange("(p k) d -> p (k d)", p=P)).then_inc(s("x_loaded"), 16)
            sp.wait_ge(s("zeros_set"), 1)
            for r in range(0, L // J):
                if r % 14 == 0:
                    sp.dma_start(rows_of(x_at_start, D)[:, r * J * D:(r + 14) * J * D]
                                 .rearrange("p (n z) -> p n z", n=14),
                                 bf(zeros, 14)).then_inc(s("zeroed"), 16)
            sp.dma_start(rows_of(adst_at_start, HEADS).rearrange("p (n z) -> p n z", n=7),
                         bf(zeros[:, 0:L * HEADS // 7], 7)).then_inc(s("zeroed"), 16)
            def col(v):
                return v.rearrange("(n o) -> n o", o=1)

            def rep(v):
                return v.rearrange("(o n) -> o n", o=1).to_broadcast([P, v.shape[0]])

            wl = s("weights_loaded")
            sp.dma_start(w1[:, :], a["L1_W1"][0:3 * E32, :]).then_inc(wl, 16)
            sp.dma_start(w1u[:, :], a["L1_W1"][3 * E32:3 * E32 + 1, :].rearrange("o n -> n o"),
                         allow_slow_non_contiguous=True).then_inc(wl, 16)
            sp.dma_start(b1[:, :], col(a["L1_b1"])).then_inc(wl, 16)
            sp.dma_start(u0[:, :], a["u"][0:1, :].to_broadcast([HID, 1])).then_inc(wl, 16)
            sp.dma_start(w2[:, :], a["L1_W2"]).then_inc(wl, 16)
            sp.dma_start(b2[:, :], rep(a["L1_b2"])).then_inc(wl, 16)
            sp.dma_start(wc["c1"][:, :], a["L2_W1"]).then_inc(wl, 16)
            sp.dma_start(wc["c2"][:, :], a["L2_W2"]).then_inc(wl, 16)
            sp.dma_start(wc["at"][:, :], a["W_node"]).then_inc(wl, 16)
            sp.dma_start(bcv["c1"][:, :], rep(a["L2_b1"])).then_inc(wl, 16)
            sp.dma_start(bcv["c2"][:, :], rep(a["L2_b2"])).then_inc(wl, 16)
            sp.dma_start(wedge[:, :], rep(a["W_edge"].rearrange("a b -> (a b)"))).then_inc(wl, 16)
            sp.dma_start(asrc_w[:, :], rep(a["attn_src"].rearrange("a b -> (a b)"))).then_inc(wl, 16)
            sp.dma_start(adst_w[:, :], rep(a["attn_dst"].rearrange("a b -> (a b)"))).then_inc(wl, 16)
            sp.dma_start(gamma[:, :], rep(a["gamma"])).then_inc(wl, 16)
            sp.dma_start(beta[:, :], rep(a["beta"])).then_inc(wl, 16)
            for n, o in enumerate(("dst", "src")):
                sp.wait_ge(s("bounds_ready"), n + 1)
                sp.dma_start(bound[o, "start"], base[:, :] if o == "src" else diag[0:HIGH, :])\
                  .then_inc(s("bounds_out"), 16)
                sp.dma_start(bound[o, "end"], ends_sb[:, :]).then_inc(s("bounds_out"), 16)
                sp.wait_ge(s("bounds_out"), 32 * (n + 1))
                for t, w in ((nstart, "start"), (nend, "end")):
                    sp.dma_start(t[o][:, :], bound[o, w].rearrange("h l -> (h l)").rearrange("(p k) -> p k", p=P))\
                      .then_inc(s("bounds_in"), 16)
            sp.wait_ge(s("x_scattered"), 16 * KN)
            a32_v = a["a32"].rearrange("(p l) w -> p l w", p=P)

            def x_block(i, h):
                sp.dma_start(cut[f"xs{h}"], rows_of(x_at_start, D)[:, bass.ds(blk(i, h) * (J * D), J * D)])\
                  .then_inc(s(f"xs_in{h}"), 16)

            def body(i):
                for h in range(2):
                    if h == 0 or not (isinstance(i, int) and i == NB - 1):
                        if later(i) or h:
                            sp.wait_ge(s("rows_ready"), i * 2 + h)
                        x_block(*((i, 1) if h == 0 else (i + 1, 0)))
                    if later(i):
                        sp.wait_ge(s(f"scattered{h}"), scattered(i, h))
                    sp.dma_start(rows[h][:, :, D:D + E32], a32_v[:, bass.ds(blk(i, h) * J, J), :])\
                      .then_inc(s(f"a32_in{h}"), 16)

            x_block(0, 0)
            turns(sp, body, peel_last=True)
            for h in range(2):
                sp.wait_ge(s(f"scattered{h}"), scattered(NB, h))
            by_v = rows_of(by_src, TW)
            sp.dma_start(edge_ends[:, 1:2], by_v[:, TW - 1:TW], allow_slow_non_contiguous=True).then_inc(s("edge_ends_in"), 16)
            sp.dma_start(edge_ends[:, 2:3], by_v[:, L * TW - 1:L * TW], allow_slow_non_contiguous=True).then_inc(s("edge_ends_in"), 16)
            sp.dma_start(edge_ends[1:P, 0:1], by_v[0:P - 1, L * TW - 1:L * TW], allow_slow_non_contiguous=True).then_inc(s("edge_ends_in"), 16)

            def body(i):
                for h in range(2):
                    if later(i):
                        sp.wait_ge(s("state"), upto("src", "state") + i * 2 + h - 1)
                    sp.dma_start(late_tb(h), by_v[:, bass.ds(blk(i, h) * (J * TW), J * TW)])\
                      .then_inc(s(f"tb_in{h}"), 16)
                    store(i, h, "src", W01)

            def late_tb(h):
                return tb[h].rearrange("p j f -> p (j f)")

            def store(i, h, g, w):
                pi, ph = (i, 0) if h else (i - 1, 1)
                if not later(i) and h == 0:
                    return
                write(pi, ph, g, w)

            def write(i, h, g, w):
                sp.wait_ge(s("state"), upto(g, "state") + i * 2 + h + 1)
                sp.dma_start(rows_of(states[g], w)[:, bass.ds(blk(i, h) * (J * w), J * w)],
                             st[h][:, 0:J * w]).then_inc(s(f"stored{h}"), 16)

            turns(sp, body)
            write(NB - 1, 1, "src", W01)
            src_b = a["src"].rearrange("(p l) -> p l", p=P)
            a16_v = a["a16"].rearrange("(p l) w -> p (l w)", p=P)
            for g, w in (("c1", D), ("c2", D), ("at", W3S)):
                sp.wait_ge(s("table"), upto(g, "table") + 1)
                tw = W3 if g == "at" else D
                sp.dma_start(table[g].rearrange("(p k) w -> p (k w)", p=P), hrows[:, 0:KN * tw])\
                  .then_inc(s("table_out"), 16)
                if g == "at":
                    sp.dma_start(adst_table.rearrange("(p k) w -> p (k w)", p=P), arena_b[:, 0:KN * HEADS])\
                      .then_inc(s("table_out"), 16)
                    sp.wait_ge(s("adst_scattered"), 16 * KN)
                    sp.dma_start(arena_b[:, KN * HEADS:KN * HEADS + L * HEADS], rows_of(adst_at_start, HEADS))\
                      .then_inc(s("adst_in"), 16)

                def body(i):
                    for h in range(2):
                        if later(i):
                            sp.wait_ge(s(f"gathered{h}"), upto(g, f"gathered{h}") + i * (16 * J))
                        sp.dma_start(idx_blk[h][:, :], src_b[:, bass.ds(blk(i, h) * J, J)])\
                          .then_inc(s(f"idx{h}"), 16)
                        if g == "at":
                            if later(i):
                                sp.wait_ge(s("state"), upto("at", "state") + i * 2 + h - 1)
                            sp.dma_start(a16[h].rearrange("p j f -> p (j f)"),
                                         a16_v[:, bass.ds(blk(i, h) * (J * E16), J * E16)])\
                              .then_inc(s(f"a16_in{h}"), 16)
                        store(i, h, g, w)

                turns(sp, body)
                write(NB - 1, 1, g, w)
            sp.wait_ge(s("final"), 1)
            sp.dma_start(out.rearrange("(p k) d -> p (k d)", p=P), x[:, :]).then_inc(s("out_done"), 16)
            sp.wait_ge(s("out_done"), 16)

        @block.gpsimd
        def _(pool):
            pool.memset(dst_i[:, 0:1], -1).then_inc(s("dst_col0"), 1)
            pool.memset(zeros, 0.0).then_inc(s("zeros_set"), 1)
            pool.iota(iota_i[:, :], pattern=[[1, P]], base=0, channel_multiplier=0).then_inc(s("iotas"), 1)
            pool.iota(rowno_i[:, :], pattern=[[0, 1]], base=0, channel_multiplier=1).then_inc(s("iotas"), 1)
            pool.wait_ge(s("zeroed"), 16 * (NB * 2 // 14 + 1))
            pool.wait_ge(s("x_loaded"), 16)
            pool.wait_ge(s("node_index"), 1)
            for k in range(KN):
                pool.indirect_dma_start(out=x_at_start, out_offset=AT(ap=start_i[:, k:k + 1], axis=0),
                                        in_=x[:, k * D:(k + 1) * D], in_offset=None,
                                        bounds_check=EP - 1, oob_is_err=False).then_inc(s("x_scattered"), 16)
            pool.indirect_dma_start(out=first_row[:, :], out_offset=None, in_=a["x"],
                                    in_offset=AT(ap=dst_i[:, 1:2], axis=0)).then_inc(s("first_row_in"), 16)

            def body(i):
                for h in range(2):
                    pool.wait_ge(s("rows_ready"), i * 2 + h + 1)
                    pool.wait_ge(s(f"a32_in{h}"), i * 16 + 16)
                    pool.sem_inc(s("pool_begun"), 1)
                    for k in range(J):
                        pool.indirect_dma_start(out=by_src, out_offset=AT(ap=idx_blk[h][:, k:k + 1], axis=0),
                                                in_=rows[h][:, k, :], in_offset=None)\
                            .then_inc(s(f"scattered{h}"), 16)

            turns(pool, body)

            def node_states(g, w, o):
                for h in range(2):
                    pool.wait_ge(s(f"stored{h}"), upto(g, f"stored{h}") + 16 * NB)
                pool.wait_ge(s("chunk_end"), upto(g, "chunk_end") + 1)
                for k in range(KN):
                    pool.indirect_dma_start(out=arena_a[:, k * w:(k + 1) * w], out_offset=None, in_=states[g],
                                            in_offset=AT(ap=end_i[o][:, k:k + 1], axis=0))\
                        .then_inc(s("nodes_in"), 16)

            node_states("src", W01, "src")
            for g, w in (("c1", D), ("c2", D), ("at", W3)):
                pool.wait_ge(s("table_out"), upto(g, "table_out") + 32 if g == "at" else 16)
                if g == "at":
                    for k in range(KN):
                        pool.indirect_dma_start(out=adst_at_start, out_offset=AT(ap=start_i[:, k:k + 1], axis=0),
                                                in_=arena_b[:, k * HEADS:(k + 1) * HEADS], in_offset=None,
                                                bounds_check=EP - 1, oob_is_err=False)\
                            .then_inc(s("adst_scattered"), 16)
                    pool.indirect_dma_start(out=first_adst[:, :], out_offset=None, in_=adst_table,
                                            in_offset=AT(ap=dst_i[:, 1:2], axis=0))\
                        .then_inc(s("first_adst_in"), 16)

                def body(i):
                    for h in range(2):
                        pool.wait_ge(s(f"idx{h}"), upto(g, f"idx{h}") + i * 16 + 16)
                        if later(i):
                            pool.wait_ge(s("state"), upto(g, "state") + i * 2 + h - 1)
                        pool.sem_inc(s("pool_begun"), 1)
                        for k in range(J):
                            pool.indirect_dma_start(out=gb[h][:, k * w:(k + 1) * w], out_offset=None,
                                                    in_=table[g], in_offset=AT(ap=idx_blk[h][:, k:k + 1], axis=0))\
                                .then_inc(s(f"gathered{h}"), 16)

                turns(pool, body)
                node_states(g, W3S if g == "at" else D, "dst")

        def rstd(act, n):
            act.wait_ge(s("var"), upto(n, "var") + 1)
            act.activation(stat2[:, :], stat2[:, :], ACT.Sqrt).then_inc(s("root"), 1)

        work = carve(arena_b, [("t", GT * P), ("r", GT * P), ("g", GT * 3 * E32), ("y", KN * D)])

        def mlp_act(act):
            def body(i):
                act.wait_ge(s("turned"), upto("mlp", "turned") + i + 1)
                act.activation(work["t"][0:3 * E32, 0:512], bank[1][0:3 * E32, :], ACT.Copy).then_inc(s("group_t"), 1)
                act.activation(work["t"][0:3 * E32, 512:GT * P], bank[2][0:3 * E32, 0:GT * P - 512], ACT.Copy)\
                   .then_inc(s("group_t"), 1)
                act.wait_ge(s("mlp_hid"), i + 1)
                act.activation(work["r"][:, 0:512], bank[3][:, :], ACT.Relu, bias=b1[:, 0:1]).then_inc(s("mlp_r"), 1)
                act.activation(work["r"][:, 512:GT * P], bank[4][:, 0:GT * P - 512], ACT.Relu, bias=b1[:, 0:1])\
                   .then_inc(s("mlp_r"), 1)

            act.wait_ge(s("b1_ready"), 1)
            turns(act, body, NG)

        def dense_act(act, g):
            def body(i):
                act.wait_ge(s("turned"), upto(g, "turned") + i + 1)
                act.activation(work["t"][0:D, 0:512], bank[1][0:D, :], ACT.Copy).then_inc(s("group_t"), 1)
                act.activation(work["t"][0:D, 512:GT * P], bank[2][0:D, 0:GT * P - 512], ACT.Copy)\
                   .then_inc(s("group_t"), 1)

            turns(act, body, NG)

        def relu_act(act, g):
            act.wait_ge(s("conv"), upto(g, "conv") + 1)
            act.activation(hrows[:, 0:KN * D], hrows[:, 0:KN * D], ACT.Relu).then_inc(s("relu"), 1)

        def attention_act(act):
            def body(i):
                for h in range(2):
                    act.wait_ge(s("at_args"), i * 2 + h + 1)
                    act.activation(late["ex"], late["ex"], ACT.Exp).then_inc(s("at_exp"), 1)
                    act.activation(late["lk"], late["lk"], ACT.Exp).then_inc(s("at_exp"), 1)

            turns(act, body)
            act.wait_ge(s("at_chunk_args"), 1)
            act.activation(chunk_t1[0:W3S, :], chunk_t1[0:W3S, :], ACT.Exp).then_inc(s("at_chunk_exp"), 1)
            act.activation(chunk_t2[0:W3S, :], chunk_t2[0:W3S, :], ACT.Exp).then_inc(s("at_chunk_exp"), 1)
            act.wait_ge(s("at_node_args"), 1)
            act.activation(node_args(0), node_args(0), ACT.Exp).then_inc(s("at_node_exp"), 1)
            act.activation(node_args(1), node_args(1), ACT.Exp).then_inc(s("at_node_exp"), 1)

        def node_args(n):
            at = KN * W3S + n * KN * HEADS
            return arena_b[:, at:at + KN * HEADS]

        @block.scalar
        def _(act):
            act.wait_ge(s("w_loaded"), 16)
            act.activation(decay[:, :], decay[:, :], ACT.Exp, scale=-1.0).then_inc(s("decay_ready"), 1)

            def turned(g, q):
                act.wait_ge(s("tile_turned"), g + 1)
                act.activation(hi_t[q], p_hi_t[q], ACT.Copy).then_inc(s("hi_t_ready"), 1)

            def body(i):
                for h in range(2):
                    for k in range(J):
                        act.wait_ge(s("hist_added"), i * (2 * J) + h * J + k + 1)
                        act.activation(snap[k % 2], hist, ACT.Copy).then_inc(s("snap_ready"), 1)
                        if k % Q == 2:
                            turned(i * (2 * J // Q) + h * (J // Q) + k // Q + 1, (k // Q + 1) % 2)

            turned(0, 0)
            turns(act, body)

            rstd(act, "ln0")
            mlp_act(act)
            rstd(act, "ln1")
            act.wait_ge(s("degree_ready"), 1)
            act.activation(dinv[:, :], degree[:, :], ACT.Sqrt).then_inc(s("dinv_root"), 1)
            dense_act(act, "c1")
            relu_act(act, "c1")
            dense_act(act, "c2")
            relu_act(act, "c2")
            rstd(act, "ln2")
            dense_act(act, "at")
            attention_act(act)
            rstd(act, "ln3a")
            rstd(act, "ln3")

        @block.tensor
        def _(pe):
            for n, o in enumerate(("dst", "src")):
                if n == 0:
                    pe.wait_ge(s("consts"), 1)
                else:
                    pe.wait_ge(s("hist_read"), 1)
                pe.matmul(hist, zero_b[:, 0:HIGH], zero_b[:, 0:LOW], start=True, stop=False)

                def body(i):
                    for h in range(2):
                        pe.wait_ge(s("onehots"), upto(o, "onehots") + i * 2 + h + 1)
                        for k in range(J):
                            last = pe.matmul(hist, oh_hi[h][:, :, k], oh_lo[h][:, :, k], start=False, stop=False)
                        last.then_inc(s("onehots_used"), 1)

                turns(pe, body)
                pe.matmul(hist, zero_b[:, 0:HIGH], zero_b[:, 0:LOW], start=False, stop=True)\
                  .then_inc(s("hist_ready"), 1)
                pe.wait_ge(s("row_totals"), n + 1)
                pe.matmul(p_small[0:HIGH, 0:1], after[0:HIGH, 0:HIGH], ends_sb[:, LOW - 1:LOW], start=True,
                          stop=True).then_inc(s("row_offsets"), 1)
                if o == "dst":
                    pe.wait_ge(s("flag"), 1)
                    pe.matmul(p_small[:, 128:256], ones[:, :], diag[:, :], start=True, stop=True)\
                      .then_inc(s("flagrow"), 1)
            pe.wait_ge(s("base_ready"), 1)
            pe.matmul(hist, ident[0:HIGH, 0:HIGH], base[:, :], start=True, stop=True).then_inc(s("hist_added"), 1)

            def turn(h, k):
                q, at = k // Q % 2, slice(k % Q * P, (k % Q + 1) * P)
                turned = pe.matmul(p_hi_t[q][:, at], oh_hi[h][:, :, k], ident_b[:, :], start=True, stop=True)
                for n, w in enumerate(("hi", "lo")):
                    spread = pe.matmul(p_src[q][:, at], digit_blk[w][h][:, k:k + 1].to_broadcast([P, P]),
                                       ident_b[:, :], start=(n == 0), stop=(n == 1))
                if k % Q == Q - 1:
                    turned.then_inc(s("tile_turned"), 1)
                    spread.then_inc(s("src_spread"), 1)

            def body(i):
                for h in range(2):
                    for k in range(J):
                        t = i * (2 * J) + h * J + k
                        g = i * (2 * J // Q) + h * (J // Q) + k // Q
                        pe.wait_ge(s("snap_ready"), t + 1)
                        pe.matmul(hist, oh_hi[h][:, :, k], oh_lo[h][:, :, k], start=False, stop=True,
                                  skip_group_check=True).then_inc(s("hist_added"), 1)
                        if k % Q == 0:
                            pe.wait_ge(s("hi_t_ready"), g + 1)
                            if later(i) or h or k >= 2 * Q:
                                pe.wait_ge(s("selected"), (g - 1) * Q)
                        at = slice(k % Q * P, (k % Q + 1) * P)
                        last = pe.matmul(p_cnt[k // Q % 2][:, at], hi_t[k // Q % 2][:, at], snap[k % 2],
                                         start=True, stop=True)
                        if k % Q == Q - 1:
                            last.then_inc(s("counted"), 1)
                        nh, nk = (h, k // Q * Q + Q) if k < J - Q else (1 - h, 0)
                        if k % Q == 0:
                            if nk == 0:
                                pe.wait_ge(s("tile_onehots"), i * 2 + h + 2)
                            if later(i) or h or k:
                                pe.wait_ge(s("ranked"), g)
                            turn(nh, nk)
                            turn(nh, nk + 1)
                        if k % Q == 1:
                            turn(nh, nk + 2)
                            turn(nh, nk + 3)

            pe.wait_ge(s("tile_onehots"), 1)
            for k in range(Q):
                turn(0, k)
            turns(pe, body)

            def flagrow_src():
                pe.wait_ge(s("flag"), upto("src", "flag") + 1)
                pe.matmul(p_small[:, 128:256], ones[:, :], diag[:, :], start=True, stop=True)\
                  .then_inc(s("flagrow"), 1)

            def carries(g, w):
                pe.wait_ge(s("chunk_end"), upto(g, "chunk_end") + 1)
                if g == "src":
                    flagrow_src()
                pe.matmul(p_small[0:w, 0:P], chunk_end[:, 0:w], ident[:, :], start=True, stop=True)\
                  .then_inc(s("end_t"), 1)
                if g == "at":
                    pe.matmul(p_small[0:w, 256:384], mrep, ident[:, :], start=True, stop=True)\
                      .then_inc(s("end_t"), 1)
                pe.wait_ge(s("carry_t"), upto(g, "carry_t") + 1)
                pe.matmul(p_small[:, 384:384 + w], chunk_in_t[0:w, 0:P], ident[0:w, 0:w], start=True, stop=True)\
                  .then_inc(s("carry"), 1)
                if g == "at":
                    pe.matmul(p_small[:, 0:w], chunk_max_t[0:w, 0:P], ident[0:w, 0:w], start=True, stop=True)\
                      .then_inc(s("carry"), 1)

                diag7 = diagonals(g)

                def body(i):
                    pe.wait_ge(s("diag"), upto(g, "diag") + i + 1)
                    pe.matmul(bank[1][:, :], ones[:, :], diag7[:, 0:512], start=True, stop=True)
                    pe.matmul(bank[2][:, 0:GT * P - 512], ones[:, :], diag7[:, 512:GT * P], start=True, stop=True)\
                      .then_inc(s("keys"), 1)
                    pe.wait_ge(s("pick"), upto(g, "pick") + i + 1)
                    for t in range(GT):
                        b = bank[3 + t // 4]
                        last = pe.matmul(b[:, (t % 4) * P:(t % 4) * P + w], diag7[:, t * P:(t + 1) * P],
                                         chunk_in[:, 0:w], start=True, stop=True)
                    last.then_inc(s("carried"), 1)

                turns(pe, body, NG)

            def dense(g, n, w):
                def body(i):
                    pe.wait_ge(s("grp"), upto(g, "grp") + i + 1)
                    for t in range(GT):
                        b = bank[1 + t // 4]
                        last = pe.matmul(b[0:n, (t % 4) * P:(t % 4 + 1) * P], work["g"][:, t * n:(t + 1) * n],
                                         ident[:, :], start=True, stop=True)
                    last.then_inc(s("turned"), 1)
                    pe.wait_ge(s("group_t"), upto(g, "group_t") + i * 2 + 2)
                    if g == "mlp":
                        pe.matmul(bank[3][:, :], w1[:, :], work["t"][0:n, 0:512], start=True, stop=True)
                        pe.matmul(bank[4][:, 0:GT * P - 512], w1[:, :], work["t"][0:n, 512:GT * P], start=True,
                                  stop=True).then_inc(s("mlp_hid"), 1)
                        pe.wait_ge(s("mlp_r"), i * 2 + 2)
                    if later(i):
                        pe.wait_ge(s("out_read"), upto(g, "out_read") + i)
                    for t in range(GT):
                        if g == "mlp":
                            last = pe.matmul(bank[5][:, t * D:(t + 1) * D], work["r"][:, t * P:(t + 1) * P], w[:, :],
                                             start=True, stop=True)
                        else:
                            last = pe.matmul(bank[5][:, t * D:(t + 1) * D], work["t"][0:n, t * P:(t + 1) * P], w[:, :],
                                             start=True, stop=True)
                    last.then_inc(s("prod"), 1)

                turns(pe, body, NG)

            carries("src", W01)
            pe.wait_ge(s("weights_loaded"), 16 * 16)
            dense("mlp", 3 * E32, w2)
            for g, w in (("c1", D), ("c2", D), ("at", W3S)):
                dense(g, D, wc[g])
                carries(g, w)


        @block.vector
        def _(v):
            chain = [0]

            def link(ins):
                chain[0] += 1
                ins.then_inc(s("v_chain"), 1)
                v.wait_ge(s("v_chain"), chain[0])

            def tell(name, n=1):
                v.sem_inc(s(name), n)

            v.wait_ge(s("iotas"), 2)
            link(v.tensor_copy(iota[:, :], iota_i[:, :]))
            link(v.tensor_copy(rowno[:, :], rowno_i[:, :]))
            link(v.tensor_scalar(rowno_l[:, :], rowno[:, :], float(L), None, ALU.mult))
            link(v.tensor_scalar(ident[:, :], iota[:, :], rowno[:, 0:1], None, ALU.is_equal))
            link(v.tensor_copy(ident_b[:, :], ident[:, :]))
            link(v.tensor_scalar(before[:, :], iota[:, :], rowno[:, 0:1], None, ALU.is_lt))
            link(v.tensor_scalar(after[:, :], iota[:, :], rowno[:, 0:1], None, ALU.is_gt))
            link(v.memset(ones[:, :], 1.0))
            link(v.tensor_copy(iota_lo, bc(iota[:, 0:LOW], J)))
            link(v.tensor_scalar(iota_hi, bc(iota[:, 0:HIGH], J), float(LOW), None, ALU.mult))
            link(v.memset(edge_ends[:, 0:1], -1.0))
            link(v.memset(zero_b[:, :], 0.0))
            tell("consts")
            v.wait_ge(s("src_loaded"), 16)
            v.wait_ge(s("dst_loaded"), 32)
            src_i = arena_b[:, 0:L].bitcast(i32)
            t_i = arena_b[:, L:2 * L].bitcast(i32)
            for o, ids in (("dst", dst_i[:, 1:L + 1]), ("src", src_i)):
                link(v.tensor_scalar(t_i, ids, LOW - 1, None, ALU.bitwise_and))
                link(v.tensor_copy(digits[o, "lo"][:, 0:L], t_i))
                link(v.tensor_scalar(t_i, ids, -LOW, None, ALU.bitwise_and))
                link(v.tensor_copy(digits[o, "hi"][:, 0:L], t_i))
                for w in ("hi", "lo"):
                    link(v.memset(digits[o, w][:, L:L + J], 0.0))
            link(v.memset(src_f[:, L:L + J], 0.0))
            link(v.tensor_copy(src_f[:, 0:L], src_i))
            link(v.tensor_tensor(same_dst[:, :], dst_i[:, 1:L + 1], dst_i[:, 0:L], ALU.is_equal))
            def of_nodes(o):
                link(v.tensor_tensor(has[o][:, :], nend[o][:, :], nstart[o][:, :], ALU.is_gt))
                link(v.tensor_scalar(tmpk[:, :], nend[o][:, :], -1.0, 0.0, ALU.add, ALU.max))
                link(v.tensor_copy(end_i[o][:, :], tmpk[:, :]))
                link(v.tensor_scalar(quot_i[:, :], tmpk[:, :], 1.0 / L, None, ALU.mult))
                link(v.tensor_scalar(key[o][:, :], quot_i[:, :], float(L), None, ALU.mult))
                link(v.tensor_tensor(tmpk[:, :], tmpk[:, :], key[o][:, :], ALU.subtract))
                link(v.tensor_scalar(stat1[:, :], tmpk[:, :], 0.0, float(L), ALU.is_lt, ALU.mult))
                link(v.tensor_tensor(key[o][:, :], key[o][:, :], stat1[:, :], ALU.subtract))
                link(v.tensor_scalar(stat1[:, :], tmpk[:, :], float(L), float(L), ALU.is_ge, ALU.mult))
                link(v.tensor_tensor(tmpk[:, :], key[o][:, :], stat1[:, :], ALU.add))
                link(v.tensor_tensor(key[o][:, :], nstart[o][:, :], tmpk[:, :], ALU.is_lt))
                link(v.tensor_scalar(tmpk[:, :], tmpk[:, :], 1.0, None, ALU.add))
                link(v.tensor_tensor(key[o][:, :], key[o][:, :], tmpk[:, :], ALU.mult))
                link(v.tensor_scalar(key[o][:, :], key[o][:, :], -1.0, None, ALU.add))

            def of_dst():
                link(v.tensor_tensor(degree[:, :], nend["dst"][:, :], nstart["dst"][:, :], ALU.subtract))
                link(v.tensor_scalar(degree[:, :], degree[:, :], 1.0, None, ALU.add))
                tell("degree_ready")
                link(v.tensor_scalar(tmpk[:, :], has["dst"][:, :], -NOWHERE, NOWHERE, ALU.mult, ALU.add))
                link(v.tensor_tensor(tmpk[:, :], tmpk[:, :], nstart["dst"][:, :], ALU.add))
                link(v.tensor_copy(start_i[:, :], tmpk[:, :]))
                tell("node_index")
                link(v.tensor_tensor(flag[:, :], dst_i[:, 1:2], dst_i[:, L:L + 1], ALU.is_equal))
                link(v.tensor_tensor(flag[:, :], flag[:, :], same_dst[:, 0:1], ALU.mult))
                v.wait_ge(s("bounds_out"), 32)
                link(v.tensor_scalar(diag[:, :], ident[:, :], flag[:, 0:1], None, ALU.mult))
                tell("flag")
                v.wait_ge(s("flagrow"), upto("dst", "flagrow") + 1)
                link(v.tensor_copy(flagrow["dst"][:, :], p_small[:, 128:256]))

            for n, o in enumerate(("dst", "src")):
                def body(i):
                    for h in range(2):
                        if later(i):
                            v.wait_ge(s("onehots_used"), upto(o, "onehots_used") + i * 2 + h - 1)
                        elif n:
                            v.wait_ge(s("onehots_used"), NB * 2)
                        at = bass.ds(blk(i, h) * J, J)
                        v.tensor_tensor(oh_hi[h], iota_hi, bf(digits[o, "hi"][:, at], HIGH), ALU.is_equal)
                        v.tensor_tensor(oh_lo[h], iota_lo, bf(digits[o, "lo"][:, at], LOW), ALU.is_equal)\
                            .then_inc(s("onehots"), 1)

                turns(v, body)
                v.wait_ge(s("hist_ready"), n + 1)
                if n:
                    v.wait_ge(s("bounds_out"), 32)
                link(v.tensor_copy(hist_sb[:, :], hist))
                tell("hist_read")
                link(v.tensor_tensor_scan(ends_sb[:, :], ones[0:HIGH, 0:LOW], hist_sb[:, :], 0.0, ALU.mult, ALU.add))
                tell("row_totals")
                v.wait_ge(s("row_offsets"), n + 1)
                link(v.tensor_copy(offs_sb[:, :], p_small[0:HIGH, 0:1]))
                link(v.tensor_scalar(ends_sb[:, :], ends_sb[:, :], offs_sb[:, 0:1], None, ALU.add))
                starts = base if o == "src" else diag
                link(v.tensor_tensor(starts[0:HIGH, :], ends_sb[:, :], hist_sb[:, :], ALU.subtract))
                tell("bounds_ready")
                v.wait_ge(s("bounds_in"), 32 * (n + 1))
                of_nodes(o)
                if o == "dst":
                    of_dst()
            tell("base_ready")

            def digits_of(i, h, done):
                at = bass.ds(blk(i, h) * J, J)
                done(v.tensor_copy(digit_blk["hi"][h][:, :], digits["src", "hi"][:, at]))
                done(v.tensor_copy(digit_blk["lo"][h][:, :], digits["src", "lo"][:, at]))
                return done(v.tensor_copy(src_blk[:, h, :], src_f[:, at]))

            def onehots_of(i, h):
                v.tensor_tensor(oh_hi[h], iota_hi, bf(digit_blk["hi"][h][:, :], HIGH), ALU.is_equal)
                v.tensor_tensor(oh_lo[h], iota_lo, bf(digit_blk["lo"][h][:, :], LOW), ALU.is_equal)\
                    .then_inc(s("tile_onehots"), 1)

            v.wait_ge(s("onehots_used"), 2 * NB * 2)
            digits_of(0, 0, link)
            onehots_of(0, 0)
            v.wait_ge(s("decay_ready"), 1)
            v.wait_ge(s("first_row_in"), 16)
            v.wait_ge(s("tile_onehots"), 1)
            c = Steps(s("v_tiles"), 2 * (J + 4))

            def stage_a(i, h, quad, xk):
                for k in range(quad * Q, quad * Q + Q):
                    if k:
                        old = xb[h][:, k - 1, :]
                    elif not later(i) and h == 0:
                        old = first_row[:, :]
                    else:
                        old = xb[1 - h][:, J - 1, :]
                    v.wait_ge(c.sem, c.value(xk))
                    xk = c.done(v.scalar_tensor_tensor(out=xb[h][:, k, :], in0=old, scalar=mask_blk[:, h, k:k + 1],
                                                       in1=xs[h][:, k, :], op0=ALU.mult, op1=ALU.add))
                    if k % Q == 0:
                        v.wait_ge(s("src_spread"), i * (2 * J // Q) + h * (J // Q) + quad + 1)
                    rank = v.scalar_tensor_tensor(out=junk[k % 2], in0=p_src[quad % 2][:, k % Q * P:(k % Q + 1) * P],
                                                  scalar=src_blk[:, h, k:k + 1], in1=before[:, :],
                                                  op0=ALU.is_equal, op1=ALU.mult, accum_out=rank_blk[:, h, k:k + 1])
                rank.then_inc(s("ranked"), 1)
                return xk

            def stage_b(i, h, quad):
                group = i * (2 * J // Q) + h * (J // Q) + quad
                v.wait_ge(s("counted"), group + 1)
                for k in range(quad * Q, quad * Q + Q):
                    place = v.scalar_tensor_tensor(out=junk[2 + k % 2], in0=p_cnt[quad % 2][:, k % Q * P:(k % Q + 1) * P],
                                                   scalar=1.0, in1=oh_lo[h][:, :, k], op0=ALU.mult, op1=ALU.mult,
                                                   accum_out=sel_blk[:, h, k:k + 1])
                    place.then_inc(s("selected"), 1)
                    if k % 2:
                        v.wait_ge(s("selected"), group * Q + k % Q + 1)
                if quad == J // Q - 1:
                    at = bass.ds(blk(i, h) * J, J)
                    if later(i):
                        v.wait_ge(s(f"scattered{h}"), scattered(i, h))
                    v.tensor_tensor(rows[h][:, :, 0:D], xb[h], bc(decay[:, at], D), ALU.mult)
                    v.tensor_copy(rows[h][:, :, TW - 1:TW], bc(src_blk[:, h, :], 1))
                    v.tensor_tensor(idx_blk[h][:, :], rank_blk[:, h, :], sel_blk[:, h, :], ALU.add)\
                        .then_inc(s("rows_ready"), 1)

            def body(i):
                c.turn(i)
                for h in range(2):
                    xk = c.done(v.tensor_copy(mask_blk[:, h, :], same_dst[:, bass.ds(blk(i, h) * J, J)]))
                    v.wait_ge(s(f"xs_in{h}"), i * 16 + 16)
                    for quad in range(J // Q):
                        xk = stage_a(i, h, quad, xk)
                        if quad:
                            stage_b(i, h, quad - 1)
                        elif h:
                            stage_b(i, 0, J // Q - 1)
                        elif later(i):
                            stage_b(i - 1, 1, J // Q - 1)
                        if quad == 1:
                            ni, nh = (i, 1) if h == 0 else (i + 1, 0)
                            if later(i) or h:
                                v.wait_ge(s("hist_added"), (i * 2 + h) * J + 1)
                            v.wait_ge(c.sem, c.value(digits_of(ni, nh, c.done)))
                            onehots_of(ni, nh)
                assert c.k == c.per, (c.k, c.per)

            turns(v, body, peel=2)
            stage_b(NB - 1, 1, J // Q - 1)

            v.wait_ge(s("rows_ready"), NB * 2)
            v.wait_ge(s("edge_ends_in"), 48)
            link(v.memset(chunk_end[:, 0:D + E32], 0.0))
            link(v.memset(chunk_end[:, D + E32:W01], -HUGE))
            link(v.tensor_copy(prev_src[:, :], edge_ends[:, 0:1]))
            c2 = Steps(s("v_src"), 2 * (5 + 2 * J - 1))
            WS = D + E32

            def body(i):
                c2.turn(i)
                for h in range(2):
                    v.wait_ge(s(f"tb_in{h}"), i * 16 + 16)
                    if later(i):
                        v.wait_ge(s(f"stored{h}"), upto("src", f"stored{h}") + i * 16)
                    if later(i) or h:
                        v.wait_ge(s("state"), upto("src", "state") + i * 2 + h)
                    ids = tb[h][:, :, TW - 1]
                    c2.done(v.tensor_tensor(mask_blk[:, h, 0:1], tb[h][:, 0, TW - 1:TW], prev_src[:, :], ALU.is_equal))
                    m = c2.done(v.tensor_tensor(mask_blk[:, h, 1:J], ids[:, 1:J], ids[:, 0:J - 1], ALU.is_equal))
                    v.wait_ge(c2.sem, c2.value(m))
                    c2.done(v.tensor_copy(prev_src[:, :], tb[h][:, J - 1, TW - 1:TW]))
                    m = c2.done(v.tensor_scalar(cap_blk[:, h, :], mask_blk[:, h, :], 2.0, -1.0, ALU.mult, ALU.add))
                    v.wait_ge(c2.sem, c2.value(m))
                    xk = mk = c2.done(v.tensor_scalar(cap_blk[:, h, :], cap_blk[:, h, :], HUGE, None, ALU.mult))
                    for k in range(J):
                        new = st[h][:, k * W01:(k + 1) * W01]
                        if k:
                            old = st[h][:, (k - 1) * W01:k * W01]
                        elif not later(i) and h == 0:
                            old = chunk_end[:, :]
                        else:
                            old = st[1 - h][:, (J - 1) * W01:J * W01]
                        v.wait_ge(c2.sem, c2.value(xk))
                        xk = c2.done(v.scalar_tensor_tensor(out=new[:, 0:WS], in0=old[:, 0:WS],
                                                            scalar=mask_blk[:, h, k:k + 1],
                                                            in1=tb[h][:, k, 0:WS], op0=ALU.mult, op1=ALU.add))
                        v.wait_ge(c2.sem, c2.value(mk))
                        ins = v.scalar_tensor_tensor(out=new[:, WS:W01], in0=old[:, WS:W01],
                                                     scalar=cap_blk[:, h, k:k + 1],
                                                     in1=tb[h][:, k, D:WS], op0=ALU.min, op1=ALU.max)
                        if k < J - 1:
                            mk = c2.done(ins)
                        else:
                            ins.then_inc(s("state"), 1)
                assert c2.k == c2.per, (c2.k, c2.per)

            turns(v, body)

            def chunk_ends(g, w):
                v.wait_ge(s("state"), upto(g, "state") + NB * 2)
                link(v.tensor_copy(chunk_end[:, 0:w], st[1][:, (J - 1) * w:J * w]))

            chunk_ends("src", W01)
            link(v.tensor_tensor(flag[:, :], edge_ends[:, 1:2], edge_ends[:, 2:3], ALU.is_equal))
            link(v.tensor_tensor(edge_ends[:, 0:1], edge_ends[:, 0:1], edge_ends[:, 1:2], ALU.is_equal))
            link(v.tensor_tensor(flag[:, :], flag[:, :], edge_ends[:, 0:1], ALU.mult))
            link(v.tensor_scalar(diag[:, :], ident[:, :], flag[:, 0:1], None, ALU.mult))
            tell("flag")
            tell("chunk_end")
            v.wait_ge(s("flagrow"), upto("src", "flagrow") + 1)
            v.wait_ge(s("end_t"), upto("src", "end_t") + 1)
            link(v.tensor_copy(flagrow["src"][:, :], p_small[:, 128:256]))
            fr = flagrow["src"]
            link(v.memset(chunk_in_t[:, 0:1], 0.0))
            link(v.tensor_tensor_scan(chunk_in_t[0:WS, 1:P + 1], fr[0:WS, :], p_small[0:WS, 0:P], 0.0,
                                      ALU.mult, ALU.add))
            link(v.tensor_scalar(chunk_t1[WS:W01, :], fr[WS:W01, :], 2.0, -1.0, ALU.mult, ALU.add))
            link(v.tensor_scalar(chunk_t1[WS:W01, :], chunk_t1[WS:W01, :], HUGE, None, ALU.mult))
            link(v.tensor_tensor_scan(chunk_in_t[WS:W01, 1:P + 1], chunk_t1[WS:W01, :], p_small[WS:W01, 0:P], 0.0,
                                      ALU.min, ALU.max))
            tell("carry_t")
            v.wait_ge(s("carry"), upto("src", "carry") + 1)
            link(v.tensor_copy(chunk_in[:, :], p_small[:, 384:384 + W01]))

            def lookups(g, o, w):
                diag7 = diagonals(g)
                grp = diag7.rearrange("p (t n) -> p t n", n=P)

                def body(i):
                    if later(i):
                        v.wait_ge(s("carried"), upto(g, "carried") + i)
                    v.tensor_tensor(grp, bf(ident[:, :], GT), bc(key[o][:, bass.ds(i * GT, GT)], P), ALU.mult)\
                        .then_inc(s("diag"), 1)
                    v.wait_ge(s("keys"), upto(g, "keys") + i + 1)
                    v.tensor_scalar(diag7[:, 0:512], bank[1][:, :], rowno_l[:, 0:1], None, ALU.is_equal)
                    v.tensor_scalar(diag7[:, 512:GT * P], bank[2][:, 0:GT * P - 512], rowno_l[:, 0:1], None,
                                    ALU.is_equal).then_inc(s("pick"), 1)
                    v.wait_ge(s("carried"), upto(g, "carried") + i + 1)
                    for b, t0, n in ((bank[3], 0, 4), (bank[4], 4, GT - 4)):
                        ins = v.tensor_copy(
                            arena_b[:, bass.ds(i * (GT * w) + t0 * w, n * w)].rearrange("p (t c) -> p t c", c=w),
                            b[:, 0:n * P].rearrange("p (t c) -> p t c", c=P)[:, :, 0:w])
                    ins.then_inc(s("lk"), 1)

                turns(v, body, NG)
                v.wait_ge(s("lk"), upto(g, "lk") + NG)

            lookups("src", "src", W01)
            v.wait_ge(s("nodes_in"), upto("src", "nodes_in") + 16 * KN)

            def views(w):
                return (arena_a[:, 0:KN * w].rearrange("p (k c) -> p k c", c=w),
                        arena_b[:, 0:KN * w].rearrange("p (k c) -> p k c", c=w))

            def nodes(ap):
                return ap.rearrange("p (k c) -> p k c", k=KN)

            got, car = views(W01)
            hs = has["src"]
            link(v.tensor_tensor(got[:, :, 0:WS], got[:, :, 0:WS], bc(hs[:, :], WS), ALU.mult))
            link(v.tensor_tensor(got[:, :, 0:WS], got[:, :, 0:WS], car[:, :, 0:WS], ALU.add))
            link(v.tensor_scalar(tmpk[:, :], key["src"][:, :], 0.0, None, ALU.is_ge))
            link(v.tensor_scalar(tmpk[:, :], tmpk[:, :], HUGE, -HUGE, ALU.mult, ALU.add))
            link(v.tensor_tensor(car[:, :, WS:W01], car[:, :, WS:W01], bc(tmpk[:, :], E32), ALU.add))
            link(v.tensor_tensor(got[:, :, WS:W01], got[:, :, WS:W01], car[:, :, WS:W01], ALU.max))
            link(v.tensor_tensor(got[:, :, WS:W01], got[:, :, WS:W01], bc(hs[:, :], E32), ALU.mult))

            def layer_norm(n, y, z, scratch):
                y3, z3, s3 = nodes(y), nodes(z), nodes(scratch)
                link(v.tensor_reduce(stat1[:, :], y3, AX.X, ALU.add))
                link(v.tensor_scalar(stat1[:, :], stat1[:, :], 1.0 / D, None, ALU.mult))
                link(v.tensor_tensor(z3, y3, bc(stat1[:, :], D), ALU.subtract))
                link(v.tensor_tensor(s3, z3, z3, ALU.mult))
                link(v.tensor_reduce(stat2[:, :], s3, AX.X, ALU.add))
                link(v.tensor_scalar(stat2[:, :], stat2[:, :], 1.0 / D, 1e-5, ALU.mult, ALU.add))
                tell("var")
                v.wait_ge(s("root"), upto(n, "root") + 1)
                link(v.reciprocal(stat2[:, :], stat2[:, :]))
                link(v.tensor_tensor(z3, z3, bc(stat2[:, :], D), ALU.mult))

            ND = KN * D
            xf = x[:, :]
            link(v.tensor_tensor(nodes(xf), nodes(xf), got[:, :, 0:D], ALU.add))
            layer_norm("ln0", xf, xf, arena_b[:, 0:ND])

            v.wait_ge(s("weights_loaded"), 16 * 16)
            link(v.scalar_tensor_tensor(out=b1[:, :], in0=w1u[:, :], scalar=u0[:, 0:1], in1=b1[:, :],
                                        op0=ALU.mult, op1=ALU.add))
            tell("b1_ready")
            link(v.tensor_tensor(tmpk[:, :], nend["src"][:, :], nstart["src"][:, :], ALU.subtract))
            link(v.tensor_scalar(tmpk[:, :], tmpk[:, :], 1.0, None, ALU.max))
            link(v.reciprocal(tmpk[:, :], tmpk[:, :]))
            hin = work["g"].rearrange("p (t c) -> p t c", c=3 * E32)

            def body(i):
                if later(i):
                    v.wait_ge(s("mlp_out"), i)
                part = arena_a[:, bass.ds(i * (GT * W01), GT * W01)].rearrange("p (t c) -> p t c", c=W01)
                v.tensor_copy(hin[:, :, 0:2 * E32], part[:, :, D:W01])
                v.tensor_tensor(hin[:, :, 2 * E32:], part[:, :, D:D + E32], bc(tmpk[:, bass.ds(i * GT, GT)], E32),
                                ALU.mult).then_inc(s("grp"), 1)
                v.wait_ge(s("prod"), upto("mlp", "prod") + i + 1)
                y = work["y"][:, bass.ds(i * (GT * D), GT * D)]
                v.tensor_tensor(y, bank[5][:, 0:GT * D], x[:, bass.ds(i * (GT * D), GT * D)], ALU.add)\
                    .then_inc(s("out_read"), 1)
                v.wait_ge(s("out_read"), upto("mlp", "out_read") + i + 1)
                y3 = y.rearrange("p (t c) -> p t c", c=D)
                v.tensor_tensor(y3, y3, bf(b2[:, :], GT), ALU.add).then_inc(s("mlp_out"), 1)

            turns(v, body, NG)
            v.wait_ge(s("mlp_out"), NG)
            layer_norm("ln1", work["y"], xf, arena_a[:, 0:ND])

            v.wait_ge(s("dinv_root"), 1)
            link(v.reciprocal(dinv[:, :], dinv[:, :]))

            def dense(g, source, w):
                def body(i):
                    v.tensor_copy(work["g"][:, 0:GT * D], source[:, bass.ds(i * (GT * D), GT * D)])\
                        .then_inc(s("grp"), 1)
                    v.wait_ge(s("prod"), upto(g, "prod") + i + 1)
                    to = hrows[:, bass.ds(i * (GT * w), GT * w)].rearrange("p (t c) -> p t c", c=w)[:, :, 0:D]
                    prod = bank[5][:, 0:GT * D].rearrange("p (t c) -> p t c", c=D)
                    if g == "at":
                        ins = v.tensor_copy(to, prod)
                    else:
                        ins = v.tensor_tensor(to, prod, bc(dinv[:, bass.ds(i * GT, GT)], D), ALU.mult)
                    ins.then_inc(s("out_read"), 1)

                turns(v, body, NG)
                v.wait_ge(s("out_read"), upto(g, "out_read") + NG)

            def conv(g, source):
                dense(g, source, D)
                tell("table")
                link(v.memset(chunk_end[:, :], 0.0))
                cc = Steps(s("chain"), 2 * J, upto(g, "chain"))

                def body(i):
                    cc.turn(i)
                    for h in range(2):
                        if later(i):
                            v.wait_ge(s(f"stored{h}"), upto(g, f"stored{h}") + i * 16)
                        if later(i) or h:
                            v.wait_ge(s("state"), upto(g, "state") + i * 2 + h)
                        xk = cc.done(v.tensor_copy(mask_blk[:, h, :], same_dst[:, bass.ds(blk(i, h) * J, J)]))
                        v.wait_ge(s(f"gathered{h}"), upto(g, f"gathered{h}") + i * (16 * J) + 16 * J)
                        for k in range(J):
                            if k:
                                old = st[h][:, (k - 1) * D:k * D]
                            elif not later(i) and h == 0:
                                old = chunk_end[:, 0:D]
                            else:
                                old = st[1 - h][:, (J - 1) * D:J * D]
                            v.wait_ge(cc.sem, cc.value(xk))
                            ins = v.scalar_tensor_tensor(out=st[h][:, k * D:(k + 1) * D], in0=old,
                                                         scalar=mask_blk[:, h, k:k + 1],
                                                         in1=gb[h][:, k * D:(k + 1) * D], op0=ALU.mult, op1=ALU.add)
                            if k < J - 1:
                                xk = cc.done(ins)
                            else:
                                ins.then_inc(s("state"), 1)
                    assert cc.k == cc.per, (cc.k, cc.per)

                turns(v, body)
                chunk_ends(g, D)
                tell("chunk_end")
                v.wait_ge(s("end_t"), upto(g, "end_t") + 1)
                link(v.tensor_tensor_scan(chunk_in_t[0:D, 1:P + 1], flagrow["dst"][0:D, :], p_small[0:D, 0:P], 0.0,
                                          ALU.mult, ALU.add))
                tell("carry_t")
                v.wait_ge(s("carry"), upto(g, "carry") + 1)
                link(v.tensor_copy(chunk_in[:, 0:D], p_small[:, 384:384 + D]))
                lookups(g, "dst", D)
                v.wait_ge(s("nodes_in"), upto(g, "nodes_in") + 16 * KN)
                got, car = views(D)
                h3 = nodes(hrows[:, 0:ND])
                v.wait_ge(s("table_out"), upto(g, "table_out") + 16)
                link(v.tensor_tensor(got, got, bc(has["dst"][:, :], D), ALU.mult))
                link(v.tensor_tensor(got, got, car, ALU.add))
                link(v.tensor_tensor(h3, got, h3, ALU.add))
                link(v.tensor_tensor(h3, h3, bc(dinv[:, :], D), ALU.mult))
                link(v.tensor_tensor(h3, h3, bf(bcv[g][:, :], KN), ALU.add))
                tell("conv")
                v.wait_ge(s("relu"), upto(g, "relu") + 1)

            conv("c1", x)
            conv("c2", hrows)
            link(v.tensor_tensor(xf, xf, hrows[:, 0:ND], ALU.add))
            layer_norm("ln2", xf, xf, arena_b[:, 0:ND])

            dense("at", x, W3)
            h4 = hrows[:, :].rearrange("p (k c) -> p k c", c=W3)
            pr = arena_a[:, 0:ND]
            for wv, to in ((asrc_w, h4[:, :, D:W3]), (adst_w, arena_b[:, 0:KN * HEADS].rearrange("p (k c) -> p k c", c=HEADS))):
                link(v.tensor_tensor(nodes(pr), h4[:, :, 0:D], bf(wv[:, :], KN), ALU.mult))
                link(v.tensor_reduce(to, pr.rearrange("p (k c d) -> p k c d", c=HEADS, d=HD), AX.X, ALU.add))
            tell("table")
            v.wait_ge(s("adst_in"), 16)
            v.wait_ge(s("first_adst_in"), 16)
            adst = arena_b[:, KN * HEADS:KN * HEADS + L * HEADS]
            adst_h = adst.rearrange("p (l c) -> p c l", c=HEADS)
            for hd in range(HEADS):
                link(v.tensor_tensor_scan(adst_h[:, hd, :], same_dst[:, :], adst_h[:, hd, :],
                                          first_adst[:, hd:hd + 1], ALU.mult, ALU.add))
            mx = late["mx"].rearrange("p (c j) -> p c j", j=J + 1)
            link(v.memset(mx[:, :, J:J + 1], 0.0))
            link(v.memset(chunk_end[:, :], 0.0))

            def hj(name):
                t = late[name]
                return t.rearrange("p (c j) -> p c j", j=J), t.rearrange("p (c j) -> p j c", j=J)

            (ex, ex_j), (lk, lk_j) = hj("ex"), hj("lk")
            sc = late["sc"]
            prod = late["prod"]
            prod4 = prod.rearrange("p (j c f) -> p j c f", c=HEADS, f=E16)
            wv4 = wedge[:, :].rearrange("p (o f c) -> p o c f", o=1, c=HEADS).to_broadcast([P, J, HEADS, E16])
            cf = late["cf"].rearrange("p (j w) -> p j w", w=W3)
            ca = Steps(s("chain"), 2 * (15 + HEADS + 2 * J), upto("at", "chain"))

            def per_head(ap3, n):
                return ap3.rearrange("p j (c o) -> p j c o", o=1).to_broadcast([P, J, HEADS, n])

            def body(i):
                ca.turn(i)

                def then(ins):
                    k = ca.done(ins)
                    v.wait_ge(ca.sem, ca.value(k))

                for h in range(2):
                    if later(i):
                        v.wait_ge(s(f"stored{h}"), upto("at", f"stored{h}") + i * 16)
                    if later(i) or h:
                        v.wait_ge(s("state"), upto("at", "state") + i * 2 + h)
                    m = mask_blk[:, h, :]
                    g3 = gb[h].rearrange("p (j w) -> p j w", w=W3)
                    ca.done(v.tensor_copy(m, same_dst[:, bass.ds(blk(i, h) * J, J)]))
                    ca.done(v.tensor_copy(mx[:, :, 0:1], mx[:, :, J:J + 1]))
                    v.wait_ge(s(f"a16_in{h}"), i * 16 + 16)
                    then(v.tensor_tensor(prod4, a16[h].rearrange("p j (o f) -> p j o f", o=1)
                                         .to_broadcast([P, J, HEADS, E16]), wv4, ALU.mult))
                    then(v.tensor_reduce(sc, prod.rearrange("p (a f) -> p a f", f=E16), AX.X, ALU.add))
                    then(v.tensor_tensor(sc, sc, adst[:, bass.ds(blk(i, h) * (J * HEADS), J * HEADS)], ALU.add))
                    v.wait_ge(s(f"gathered{h}"), upto("at", f"gathered{h}") + i * (16 * J) + 16 * J)
                    sc3 = sc.rearrange("p (j c) -> p j c", c=HEADS)
                    then(v.tensor_tensor(sc3, sc3, g3[:, :, D:W3], ALU.add))
                    then(v.scalar_tensor_tensor(out=lk_j, in0=sc3, scalar=0.2, in1=sc3, op0=ALU.mult, op1=ALU.max))
                    for hd in range(HEADS):
                        k = ca.done(v.tensor_tensor_scan(mx[:, hd, 1:J + 1], m, lk[:, hd, :], mx[:, hd, 0:1],
                                                         ALU.mult, ALU.max))
                    v.wait_ge(ca.sem, ca.value(k))
                    then(v.tensor_tensor(ex, mx[:, :, 0:J], bf(m, HEADS), ALU.mult))
                    then(v.tensor_tensor(ex, ex, mx[:, :, 1:J + 1], ALU.subtract))
                    then(v.tensor_tensor(lk, lk, mx[:, :, 1:J + 1], ALU.subtract))
                    v.sem_inc(s("at_args"), 1)
                    v.wait_ge(s("at_exp"), (i * 2 + h) * 2 + 2)
                    then(v.tensor_tensor(ex, ex, bf(m, HEADS), ALU.mult))
                    ca.done(v.tensor_copy(cf[:, :, 0:D].rearrange("p j (c d) -> p j c d", d=HD), per_head(ex_j, HD)))
                    ca.done(v.tensor_copy(cf[:, :, D:W3], ex_j))
                    hview = g3[:, :, 0:D].rearrange("p j (c d) -> p j c d", d=HD)
                    ca.done(v.tensor_tensor(hview, hview, per_head(lk_j, HD), ALU.mult))
                    ca.done(v.tensor_copy(g3[:, :, D:W3], lk_j))
                    s3 = st[h][:, 0:J * W3S].rearrange("p (j w) -> p j w", w=W3S)
                    then(v.tensor_copy(s3[:, :, W3:W3S], mx[:, :, 1:J + 1].rearrange("p c j -> p j c")))
                    for k in range(J):
                        if k:
                            old = s3[:, k - 1, 0:W3]
                        elif not later(i) and h == 0:
                            old = chunk_end[:, 0:W3]
                        else:
                            old = st[1 - h][:, (J - 1) * W3S:(J - 1) * W3S + W3]
                        tmp = late["tmp"][:, (k % 2) * W3:(k % 2 + 1) * W3]
                        then(v.tensor_tensor(tmp, old, cf[:, k, :], ALU.mult))
                        ins = v.tensor_tensor(s3[:, k, 0:W3], tmp, g3[:, k, :], ALU.add)
                        if k < J - 1:
                            then(ins)
                        else:
                            ins.then_inc(s("state"), 1)
                assert ca.k == ca.per

            turns(v, body)
            chunk_ends("at", W3S)
            link(v.tensor_copy(mrep[:, 0:D].rearrange("p (c d) -> p c d", d=HD), bc(chunk_end[:, W3:W3S], HD)))
            link(v.tensor_copy(mrep[:, D:W3], chunk_end[:, W3:W3S]))
            link(v.tensor_copy(mrep[:, W3:W3S], chunk_end[:, W3:W3S]))
            tell("chunk_end")
            v.wait_ge(s("end_t"), upto("at", "end_t") + 2)
            fr = flagrow["dst"][0:W3S, :]
            pm, psum_t = p_small[0:W3S, 256:384], p_small[0:W3S, 0:P]
            mo = chunk_max_t[0:W3S, :]
            t1, t2 = chunk_t1[0:W3S, :], chunk_t2[0:W3S, :]
            link(v.memset(chunk_max_t[:, 0:1], 0.0))
            link(v.tensor_tensor_scan(mo[:, 1:P + 1], fr, pm, 0.0, ALU.mult, ALU.max))
            link(v.tensor_tensor(t1, fr, mo[:, 0:P], ALU.mult))
            link(v.tensor_tensor(t1, t1, mo[:, 1:P + 1], ALU.subtract))
            link(v.tensor_tensor(t2, pm, mo[:, 1:P + 1], ALU.subtract))
            tell("at_chunk_args")
            v.wait_ge(s("at_chunk_exp"), 2)
            link(v.tensor_tensor(t1, t1, fr, ALU.mult))
            link(v.tensor_tensor(t2, t2, psum_t, ALU.mult))
            link(v.tensor_tensor_scan(chunk_in_t[0:W3S, 1:P + 1], t1, t2, 0.0, ALU.mult, ALU.add))
            tell("carry_t")
            v.wait_ge(s("carry"), upto("at", "carry") + 2)
            link(v.tensor_copy(chunk_in[:, 0:W3], p_small[:, 384:384 + W3]))
            link(v.tensor_copy(chunk_in[:, W3:W3S], p_small[:, W3:W3S]))
            lookups("at", "dst", W3S)
            v.wait_ge(s("nodes_in"), upto("at", "nodes_in") + 16 * KN)
            got, car = views(W3S)
            e_got = node_args(0).rearrange("p (k c) -> p k c", c=HEADS)
            e_car = node_args(1).rearrange("p (k c) -> p k c", c=HEADS)
            link(v.tensor_tensor(got, got, bc(has["dst"][:, :], W3S), ALU.mult))
            link(v.tensor_tensor(e_car, got[:, :, W3:W3S], car[:, :, W3:W3S], ALU.max))
            link(v.tensor_tensor(e_got, got[:, :, W3:W3S], e_car, ALU.subtract))
            link(v.tensor_tensor(e_car, car[:, :, W3:W3S], e_car, ALU.subtract))
            tell("at_node_args")
            v.wait_ge(s("at_node_exp"), 2)

            def heads(ap3):
                return ap3[:, :, 0:D].rearrange("p k (c d) -> p k c d", d=HD)

            def wide(e):
                return e.rearrange("p k (c o) -> p k c o", o=1).to_broadcast([P, KN, HEADS, HD])

            for t3, e in ((got, e_got), (car, e_car)):
                link(v.tensor_tensor(heads(t3), heads(t3), wide(e), ALU.mult))
                link(v.tensor_tensor(t3[:, :, D:W3], t3[:, :, D:W3], e, ALU.mult))
            link(v.tensor_tensor(got[:, :, 0:W3], got[:, :, 0:W3], car[:, :, 0:W3], ALU.add))
            link(v.tensor_scalar(e_got, got[:, :, D:W3], 1e-8, None, ALU.add))
            link(v.reciprocal(e_got, e_got))
            link(v.tensor_tensor(heads(got), heads(got), wide(e_got), ALU.mult))
            y = arena_b[:, 0:ND]
            link(v.tensor_tensor(nodes(y), got[:, :, 0:D], h4[:, :, 0:D], ALU.add))
            layer_norm("ln3a", y, y, arena_a[:, 0:ND])
            link(v.tensor_tensor(nodes(y), nodes(y), bf(gamma[:, :], KN), ALU.mult))
            link(v.tensor_tensor(nodes(y), nodes(y), bf(beta[:, :], KN), ALU.add))
            link(v.tensor_tensor(xf, xf, y, ALU.add))
            layer_norm("ln3", xf, xf, arena_a[:, 0:ND])
            tell("final")


_NAMES = {
    "x": "x", "src": "src", "dst": "dst", "a16": "edge_attr_16", "a32": "edge_attr_32", "w": "edge_weight",
    "u": "L1_gnn_u", "L1_W1": "L1_gnn_W1", "L1_b1": "L1_gnn_b1", "L1_W2": "L1_gnn_W2", "L1_b2": "L1_gnn_b2",
    "L2_W1": "L2_gnn_W1", "L2_b1": "L2_gnn_b1", "L2_W2": "L2_gnn_W2", "L2_b2": "L2_gnn_b2",
    "W_node": "L3_gnn_W_node", "W_edge": "L3_gnn_W_edge", "attn_src": "L3_gnn_attn_src",
    "attn_dst": "L3_gnn_attn_dst", "gamma": "L3_gnn_ln_gamma", "beta": "L3_gnn_ln_beta",
}


def kernel(**inputs):
    import numpy as np
    import concourse.bacc as bacc
    from concourse.bass_utils import run_bass_kernel_spmd

    nc = bacc.Bacc("TRN2", target_bir_lowering=False, num_devices=1)
    arrays, aps = {}, {}
    for short, name in _NAMES.items():
        v = np.asarray(inputs[name])
        rows_padded = {"x": NP, "src": EP, "dst": EP, "a16": EP, "a32": EP, "w": EP}.get(short)
        if rows_padded:
            full = np.full((rows_padded,) + v.shape[1:], N_NODES if short in ("src", "dst") else 0, v.dtype)
            full[:v.shape[0]] = v
            v = full
        v = np.ascontiguousarray(v)
        arrays[f"in_{short}"] = v
        aps[short] = nc.dram_tensor(f"in_{short}", v.shape, mybir.dt.from_np(v.dtype), kind="ExternalInput").ap()
    out = nc.dram_tensor("out_x", (NP, D), f32, kind="ExternalOutput").ap()
    program(nc, aps, out)
    r = run_bass_kernel_spmd(nc, [arrays], core_ids=[0])
    return r.results[0]["out_x"][:N_NODES]
```

```python
import concourse.bass as bass
from concourse import mybir
from contextlib import ExitStack

P = 128
N_NODES, N_EDGES, D = 12500, 200000, 64
KN = -(-N_NODES // P)
NP = KN * P
J = 16
Q = 4
NB = -(-N_EDGES // (P * 2 * J))
L = NB * 2 * J
EP = P * L
E32, E16, HEADS, HID = 32, 16, 4, 128
HD = D // HEADS
LOW = 128
HIGH = NP // LOW
TW = D + E32 + 1
W01 = D + 2 * E32
W3 = D + HEADS
W3S = D + 2 * HEADS
GT = 7
NG = KN // GT
HUGE = 3.4e38
NOWHERE = float(1 << 22)

f32, bf16, i32 = mybir.dt.float32, mybir.dt.bfloat16, mybir.dt.int32
ALU, ACT, AX = mybir.AluOpType, mybir.ActivationFunctionType, mybir.AxisListType
AT = bass.IndirectOffsetOnAxis


ADDED = {
    "state": 2 * NB, "stored0": 16 * NB, "stored1": 16 * NB, "gathered0": 16 * J * NB, "gathered1": 16 * J * NB,
    "idx0": 16 * NB, "idx1": 16 * NB, "fix_in": 16, "fixed": 1, "fix_out": 16, "grp": NG,
    "turned": NG, "prod": NG, "out_read": NG, "group_t": 2 * NG, "var": 1, "root": 1, "nodes_in": 16 * KN,
    "chunk_end": 1, "end_t": 1, "carry": 1, "carry_t": 1, "table": 1, "table_out": 16, "conv": 1, "relu": 1,
    "onehots": 2 * NB, "onehots_used": 2 * NB, "flag": 1, "flagrow": 1, "chain": 2 * J * NB,
}
PASSES, CONVS = ("src", "c1", "c2", "at"), ("c1", "c2", "at")
ORDER = dict.fromkeys(ADDED, PASSES)
ORDER.update(dict.fromkeys(("gathered0", "gathered1", "idx0", "idx1", "table", "table_out", "conv", "relu", "chain"),
                           CONVS))
ORDER.update(dict.fromkeys(("grp", "turned", "prod", "out_read", "group_t"), ("mlp",) + CONVS))
ORDER.update(dict.fromkeys(("var", "root"), ("ln0", "ln1", "ln2", "ln3a", "ln3")))
ORDER.update(dict.fromkeys(("onehots", "onehots_used"), ("dst", "src")))
ORDER.update(dict.fromkeys(("flag", "flagrow"), ("dst", "src")))


def upto(stage, name):
    return ORDER[name].index(stage) * ADDED[name]


def later(i):
    return not isinstance(i, int) or i > 0


def turns(eng, body, n=NB, peel=1, peel_last=False):
    for i in range(peel):
        body(i)
    with eng.Fori(peel, n - peel_last) as i:
        body(i)
    if peel_last:
        body(n - 1)


class Steps:

    def __init__(self, sem, per, base=0):
        self.sem, self.per, self.base = sem, per, base

    def turn(self, i):
        self.i, self.k = i, 0

    def done(self, ins):
        ins.then_inc(self.sem, 1)
        self.k += 1
        return self.k

    def value(self, k):
        return self.i * self.per + (k + self.base)


def bc(ap, n):
    return ap.rearrange("p (a o) -> p a o", o=1).to_broadcast([ap.shape[0], ap.shape[1], n])


def bf(ap, n):
    return ap.rearrange("p (o a) -> p o a", o=1).to_broadcast([ap.shape[0], n, ap.shape[1]])


def program(nc, a, out):
    with ExitStack() as ctx:
        def sb(name, shape, dt=f32):
            return ctx.enter_context(nc.sbuf_tensor(name, shape, dt))

        def ps(name, shape):
            return ctx.enter_context(nc.psum_tensor(name, shape, f32))

        def sem(name):
            return ctx.enter_context(nc.semaphore(name))

        def dram(name, shape, dt=f32):
            return nc.dram_tensor(name, shape, dt, kind="Internal").ap()

        x_at_start = dram("x_at_start", (EP, D))
        adst_at_start = dram("adst_at_start", (EP, HEADS))
        by_src = dram("by_src", (EP, TW))
        states = {g: dram(f"states_{g}", (EP, w)) for g, w in
                  (("src", W01), ("c1", D), ("c2", D), ("at", W3S))}
        table = {"c1": dram("table_c1", (NP, D)), "c2": dram("table_c2", (NP, D)),
                 "at": dram("table_at", (NP, W3))}
        adst_table = dram("adst_table", (NP, HEADS))
        bound = {(o, w): dram(f"{w}_{o}", (HIGH, LOW)) for o in ("src", "dst") for w in ("start", "end")}

        x = sb("x", [P, KN * D])
        hrows = sb("hrows", [P, KN * W3])
        arena_a = sb("arena_a", [P, KN * W01])
        arena_b = sb("arena_b", [P, KN * W01])
        dst_i = sb("dst_i", [P, L + 1], i32)
        src_f = sb("src_f", [P, L + J])
        digits = {(o, w): sb(f"{w}_{o}", [P, L + J], bf16) for o in ("src", "dst") for w in ("hi", "lo")}
        same_dst = sb("same_dst", [P, L])
        decay = sb("decay", [P, L])
        iota_i = sb("iota_i", [P, P], i32)
        rowno_i = sb("rowno_i", [P, 1], i32)
        iota = sb("iota", [P, P])
        rowno = sb("rowno", [P, 1])
        rowno_l = sb("rowno_l", [P, 1])
        ident = sb("ident", [P, P])
        ident_b = sb("ident_b", [P, P], bf16)
        before = sb("before", [P, P])
        after = sb("after", [P, P])
        ones = sb("ones", [P, P])
        zero_b = sb("zero_b", [P, P], bf16)
        base = sb("base", [HIGH, LOW])
        hist_sb = sb("hist_sb", [HIGH, LOW])
        ends_sb = sb("ends_sb", [HIGH, LOW])
        offs_sb = sb("offs_sb", [HIGH, 1])
        nstart = {o: sb(f"nstart_{o}", [P, KN]) for o in ("src", "dst")}
        nend = {o: sb(f"nend_{o}", [P, KN]) for o in ("src", "dst")}
        has = {o: sb(f"has_{o}", [P, KN]) for o in ("src", "dst")}
        end_i = {o: sb(f"end_i_{o}", [P, KN], i32) for o in ("src", "dst")}
        start_i = sb("start_i", [P, KN], i32)
        tmpk = sb("tmpk", [P, KN])
        degree = sb("degree", [P, KN])
        dinv = sb("dinv", [P, KN])
        flagrow = {o: sb(f"flagrow_{o}", [P, P]) for o in ("src", "dst")}
        flag = sb("flag", [P, 1])
        diag = sb("diag", [P, P])
        edge_ends = sb("edge_ends", [P, 3])
        chunk_end = sb("chunk_end", [P, W01])
        chunk_in_t = sb("chunk_in_t", [P, P + 1])
        chunk_max_t = sb("chunk_max_t", [P, P + 1])
        chunk_t1 = sb("chunk_t1", [P, P])
        chunk_t2 = sb("chunk_t2", [P, P])
        chunk_in = sb("chunk_in", [P, W01])
        first_src = sb("first_src", [P, 1], i32)
        first_end = {o: sb(f"first_end_{o}", [P, 1]) for o in ("src", "dst")}
        fix_from = {o: sb(f"fix_from_{o}", [P, 1], i32) for o in ("src", "dst")}
        fix_to = {o: sb(f"fix_to_{o}", [P, 1], i32) for o in ("src", "dst")}
        fix_tmp = sb("fix_tmp", [P, 2])
        fix_rows = sb("fix_rows", [P, W01])
        fix_exp = sb("fix_exp", [P, 2 * HEADS])
        stat1 = sb("stat1", [P, KN])
        stat2 = sb("stat2", [P, KN])
        w1 = sb("w1", [3 * E32, HID])
        w1u = sb("w1u", [HID, 1])
        b1 = sb("b1", [HID, 1])
        u0 = sb("u0", [HID, 1])
        w2 = sb("w2", [HID, D])
        b2 = sb("b2", [P, D])
        wc = {"c1": sb("wc1", [D, D]), "c2": sb("wc2", [D, D]), "at": sb("wnode", [D, D])}
        bcv = {"c1": sb("bc1", [P, D]), "c2": sb("bc2", [P, D])}
        wedge = sb("wedge", [P, E16 * HEADS])
        asrc_w = sb("asrc_w", [P, D])
        adst_w = sb("adst_w", [P, D])
        gamma = sb("gamma", [P, D])
        beta = sb("beta", [P, D])
        first_row = sb("first_row", [P, D])
        first_adst = sb("first_adst", [P, HEADS])
        mask_blk = sb("mask_blk", [P, 2, J])
        cap_blk = sb("cap_blk", [P, 2, J])
        idx_blk = [sb(f"idx_blk{h}", [P, J], i32) for h in range(2)]
        rank_blk = sb("rank_blk", [P, 2, J])
        sel_blk = sb("sel_blk", [P, 2, J])
        digit_blk = {w: [sb(f"digit_{w}{h}", [P, J], bf16) for h in range(2)] for w in ("hi", "lo")}
        src_blk = sb("src_blk", [P, 2, J])
        prev_src = sb("prev_src", [P, 1])

        def carve(tensor, parts, dt=f32):
            at, got = 0, {}
            for name, size in parts:
                got[name] = tensor[:, at:at + size]
                at += size
            assert at <= tensor.shape[1], at
            return got

        cut = carve(arena_b, [("onehot", 2 * J * (LOW + HIGH) // 2), ("rows0", J * TW), ("rows1", J * TW),
                              ("xs0", J * D), ("xs1", J * D), ("xb0", J * D), ("xb1", J * D),
                              ("junk", 2 * P), ("hi_t", 2 * Q * P), ("snap", 2 * P)])
        oh = cut["onehot"].bitcast(bf16)
        oh_hi = [oh[:, h * J * (LOW + HIGH):][:, :J * HIGH].rearrange("p (n t) -> p n t", t=J) for h in range(2)]
        oh_lo = [oh[:, h * J * (LOW + HIGH) + J * HIGH:][:, :J * LOW].rearrange("p (n t) -> p n t", t=J)
                 for h in range(2)]
        rows = [cut[f"rows{h}"].rearrange("p (j f) -> p j f", f=TW) for h in range(2)]
        xs = [cut[f"xs{h}"].rearrange("p (j f) -> p j f", f=D) for h in range(2)]
        xb = [cut[f"xb{h}"].rearrange("p (j f) -> p j f", f=D) for h in range(2)]
        junk = [cut["junk"].bitcast(bf16)[:, q * P:(q + 1) * P] for q in range(4)]
        hi_t = [cut["hi_t"][0:HIGH, q * Q * P:(q + 1) * Q * P] for q in range(2)]
        snap = [cut["snap"][0:HIGH, q * P:(q + 1) * P] for q in range(2)]
        early = carve(arena_a, [("zeros", J * D), ("ih", J * HIGH // 2), ("il", J * LOW // 2)])
        zeros = early["zeros"]
        iota_hi = early["ih"].bitcast(bf16).rearrange("p (n t) -> p n t", t=J)
        iota_lo = early["il"].bitcast(bf16).rearrange("p (n t) -> p n t", t=J)
        late = carve(hrows, [("tb0", J * TW), ("tb1", J * TW)])
        tb = [late[f"tb{h}"].rearrange("p (j f) -> p j f", f=TW) for h in range(2)]
        late = carve(arena_a, [("st0", J * W01), ("st1", J * W01), ("g0", J * W3), ("g1", J * W3),
                               ("a16_0", J * E16), ("a16_1", J * E16), ("prod", J * HEADS * E16),
                               ("sc", J * HEADS), ("mx", (J + 1) * HEADS),
                               ("ex", J * HEADS), ("cf", J * W3), ("tmp", 2 * W3), ("lk", J * HEADS)])
        st = [late[f"st{h}"] for h in range(2)]
        gb = [late[f"g{h}"] for h in range(2)]
        a16 = [late[f"a16_{h}"].rearrange("p (j f) -> p j f", f=E16) for h in range(2)]

        bank = [ps(f"bank{n}", [P, 512]) for n in range(8)]
        hist = bank[0][0:HIGH, 0:LOW]
        p_hi_t = [bank[1][0:HIGH, :], bank[2][0:HIGH, :]]
        p_src = [bank[3], bank[4]]
        p_cnt = [bank[5], bank[6]]
        p_small = bank[7]

        S = {}

        def s(name):
            if name not in S:
                S[name] = sem(name)
            return S[name]

        mrep = chunk_max_t[:, 0:W3S]

        block = ctx.enter_context(nc.Block())

        def rows_of(dram_ap, w):
            return dram_ap.rearrange("(p l) w -> p (l w)", p=P)

        def scattered(i, h):
            return i * (16 * J)

        def blk(i, h):
            return i * 2 + h

        @block.sync
        def _(sp):
            src_v = a["src"].rearrange("(p l) -> p l", p=P)
            dst_v = a["dst"].rearrange("(p l) -> p l", p=P)
            sp.dma_start(arena_b[:, 0:L].bitcast(i32), src_v).then_inc(s("src_loaded"), 16)
            sp.dma_start(dst_i[:, 1:L + 1], dst_v).then_inc(s("dst_loaded"), 16)
            sp.wait_ge(s("dst_col0"), 1)
            sp.dma_start(dst_i[1:P, 0:1], dst_v[0:P - 1, L - 1:L], allow_slow_non_contiguous=True).then_inc(s("dst_loaded"), 16)
            sp.dma_start(decay[:, :], a["w"].rearrange("(p l) -> p l", p=P)).then_inc(s("w_loaded"), 16)
            sp.dma_start(x[:, :], a["x"].rearrange("(p k) d -> p (k d)", p=P)).then_inc(s("x_loaded"), 16)
            sp.wait_ge(s("zeros_set"), 1)
            for r in range(0, L // J):
                if r % 14 == 0:
                    sp.dma_start(rows_of(x_at_start, D)[:, r * J * D:(r + 14) * J * D]
                                 .rearrange("p (n z) -> p n z", n=14),
                                 bf(zeros, 14)).then_inc(s("zeroed"), 16)
            sp.dma_start(rows_of(adst_at_start, HEADS).rearrange("p (n z) -> p n z", n=7),
                         bf(zeros[:, 0:L * HEADS // 7], 7)).then_inc(s("zeroed"), 16)
            def col(v):
                return v.rearrange("(n o) -> n o", o=1)

            def rep(v):
                return v.rearrange("(o n) -> o n", o=1).to_broadcast([P, v.shape[0]])

            wl = s("weights_loaded")
            sp.dma_start(w1[:, :], a["L1_W1"][0:3 * E32, :]).then_inc(wl, 16)
            sp.dma_start(w1u[:, :], a["L1_W1"][3 * E32:3 * E32 + 1, :].rearrange("o n -> n o"),
                         allow_slow_non_contiguous=True).then_inc(wl, 16)
            sp.dma_start(b1[:, :], col(a["L1_b1"])).then_inc(wl, 16)
            sp.dma_start(u0[:, :], a["u"][0:1, :].to_broadcast([HID, 1])).then_inc(wl, 16)
            sp.dma_start(w2[:, :], a["L1_W2"]).then_inc(wl, 16)
            sp.dma_start(b2[:, :], rep(a["L1_b2"])).then_inc(wl, 16)
            sp.dma_start(wc["c1"][:, :], a["L2_W1"]).then_inc(wl, 16)
            sp.dma_start(wc["c2"][:, :], a["L2_W2"]).then_inc(wl, 16)
            sp.dma_start(wc["at"][:, :], a["W_node"]).then_inc(wl, 16)
            sp.dma_start(bcv["c1"][:, :], rep(a["L2_b1"])).then_inc(wl, 16)
            sp.dma_start(bcv["c2"][:, :], rep(a["L2_b2"])).then_inc(wl, 16)
            sp.dma_start(wedge[:, :], rep(a["W_edge"].rearrange("a b -> (a b)"))).then_inc(wl, 16)
            sp.dma_start(asrc_w[:, :], rep(a["attn_src"].rearrange("a b -> (a b)"))).then_inc(wl, 16)
            sp.dma_start(adst_w[:, :], rep(a["attn_dst"].rearrange("a b -> (a b)"))).then_inc(wl, 16)
            sp.dma_start(gamma[:, :], rep(a["gamma"])).then_inc(wl, 16)
            sp.dma_start(beta[:, :], rep(a["beta"])).then_inc(wl, 16)
            for n, o in enumerate(("dst", "src")):
                sp.wait_ge(s("bounds_ready"), n + 1)
                sp.dma_start(bound[o, "start"], base[:, :] if o == "src" else diag[0:HIGH, :])\
                  .then_inc(s("bounds_out"), 16)
                sp.dma_start(bound[o, "end"], ends_sb[:, :]).then_inc(s("bounds_out"), 16)
                sp.wait_ge(s("bounds_out"), 32 * (n + 1))
                for t, w in ((nstart, "start"), (nend, "end")):
                    sp.dma_start(t[o][:, :], bound[o, w].rearrange("h l -> (h l)").rearrange("(p k) -> p k", p=P))\
                      .then_inc(s("bounds_in"), 16)
            sp.wait_ge(s("x_scattered"), 16 * KN)
            a32_v = a["a32"].rearrange("(p l) w -> p l w", p=P)

            def x_block(i, h):
                sp.dma_start(cut[f"xs{h}"], rows_of(x_at_start, D)[:, bass.ds(blk(i, h) * (J * D), J * D)])\
                  .then_inc(s(f"xs_in{h}"), 16)

            def body(i):
                for h in range(2):
                    if h == 0 or not (isinstance(i, int) and i == NB - 1):
                        if later(i) or h:
                            sp.wait_ge(s("rows_ready"), i * 2 + h)
                        x_block(*((i, 1) if h == 0 else (i + 1, 0)))
                    if later(i):
                        sp.wait_ge(s(f"scattered{h}"), scattered(i, h))
                    sp.dma_start(rows[h][:, :, D:D + E32], a32_v[:, bass.ds(blk(i, h) * J, J), :])\
                      .then_inc(s(f"a32_in{h}"), 16)

            x_block(0, 0)
            turns(sp, body, peel_last=True)
            for h in range(2):
                sp.wait_ge(s(f"scattered{h}"), scattered(NB, h))
            by_v = rows_of(by_src, TW)
            sp.dma_start(edge_ends[:, 1:2], by_v[:, TW - 1:TW], allow_slow_non_contiguous=True).then_inc(s("edge_ends_in"), 16)
            sp.dma_start(edge_ends[:, 2:3], by_v[:, L * TW - 1:L * TW], allow_slow_non_contiguous=True).then_inc(s("edge_ends_in"), 16)
            sp.dma_start(edge_ends[1:P, 0:1], by_v[0:P - 1, L * TW - 1:L * TW], allow_slow_non_contiguous=True).then_inc(s("edge_ends_in"), 16)

            def body(i):
                for h in range(2):
                    if later(i):
                        sp.wait_ge(s("state"), upto("src", "state") + i * 2 + h - 1)
                    sp.dma_start(late_tb(h), by_v[:, bass.ds(blk(i, h) * (J * TW), J * TW)])\
                      .then_inc(s(f"tb_in{h}"), 16)
                    store(i, h, "src", W01)

            def late_tb(h):
                return tb[h].rearrange("p j f -> p (j f)")

            def store(i, h, g, w):
                pi, ph = (i, 0) if h else (i - 1, 1)
                if not later(i) and h == 0:
                    return
                write(pi, ph, g, w)

            def write(i, h, g, w):
                sp.wait_ge(s("state"), upto(g, "state") + i * 2 + h + 1)
                sp.dma_start(rows_of(states[g], w)[:, bass.ds(blk(i, h) * (J * w), J * w)],
                             st[h][:, 0:J * w]).then_inc(s(f"stored{h}"), 16)

            turns(sp, body)
            write(NB - 1, 1, "src", W01)
            src_b = a["src"].rearrange("(p l) -> p l", p=P)
            a16_v = a["a16"].rearrange("(p l) w -> p (l w)", p=P)
            for g, w in (("c1", D), ("c2", D), ("at", W3S)):
                sp.wait_ge(s("table"), upto(g, "table") + 1)
                tw = W3 if g == "at" else D
                sp.dma_start(table[g].rearrange("(p k) w -> p (k w)", p=P), hrows[:, 0:KN * tw])\
                  .then_inc(s("table_out"), 16)
                if g == "at":
                    sp.dma_start(adst_table.rearrange("(p k) w -> p (k w)", p=P), arena_b[:, 0:KN * HEADS])\
                      .then_inc(s("table_out"), 16)
                    sp.wait_ge(s("adst_scattered"), 16 * KN)
                    sp.dma_start(arena_b[:, KN * HEADS:KN * HEADS + L * HEADS], rows_of(adst_at_start, HEADS))\
                      .then_inc(s("adst_in"), 16)

                def body(i):
                    for h in range(2):
                        if later(i):
                            sp.wait_ge(s(f"gathered{h}"), upto(g, f"gathered{h}") + i * (16 * J))
                        sp.dma_start(idx_blk[h][:, :], src_b[:, bass.ds(blk(i, h) * J, J)])\
                          .then_inc(s(f"idx{h}"), 16)
                        if g == "at":
                            if later(i):
                                sp.wait_ge(s("state"), upto("at", "state") + i * 2 + h - 1)
                            sp.dma_start(a16[h].rearrange("p j f -> p (j f)"),
                                         a16_v[:, bass.ds(blk(i, h) * (J * E16), J * E16)])\
                              .then_inc(s(f"a16_in{h}"), 16)
                        store(i, h, g, w)

                turns(sp, body)
                write(NB - 1, 1, g, w)
            sp.wait_ge(s("final"), 1)
            sp.dma_start(out.rearrange("(p k) d -> p (k d)", p=P), x[:, :]).then_inc(s("out_done"), 16)
            sp.wait_ge(s("out_done"), 16)

        @block.gpsimd
        def _(pool):
            pool.memset(dst_i[:, 0:1], -1).then_inc(s("dst_col0"), 1)
            pool.memset(zeros, 0.0).then_inc(s("zeros_set"), 1)
            pool.iota(iota_i[:, :], pattern=[[1, P]], base=0, channel_multiplier=0).then_inc(s("iotas"), 1)
            pool.iota(rowno_i[:, :], pattern=[[0, 1]], base=0, channel_multiplier=1).then_inc(s("iotas"), 1)
            pool.wait_ge(s("zeroed"), 16 * (NB * 2 // 14 + 1))
            pool.wait_ge(s("x_loaded"), 16)
            pool.wait_ge(s("node_index"), 1)
            for k in range(KN):
                pool.indirect_dma_start(out=x_at_start, out_offset=AT(ap=start_i[:, k:k + 1], axis=0),
                                        in_=x[:, k * D:(k + 1) * D], in_offset=None,
                                        bounds_check=EP - 1, oob_is_err=False).then_inc(s("x_scattered"), 16)
            pool.indirect_dma_start(out=first_row[:, :], out_offset=None, in_=a["x"],
                                    in_offset=AT(ap=dst_i[:, 1:2], axis=0)).then_inc(s("first_row_in"), 16)

            def first_ends(o, ids):
                pool.indirect_dma_start(out=first_end[o][:, :], out_offset=None,
                                        in_=bound[o, "end"].rearrange("h (l o) -> (h l) o", o=1),
                                        in_offset=AT(ap=ids, axis=0)).then_inc(s(f"first_end_{o}"), 16)

            first_ends("dst", dst_i[:, 1:2])

            def body(i):
                for h in range(2):
                    pool.wait_ge(s("rows_ready"), i * 2 + h + 1)
                    pool.wait_ge(s(f"a32_in{h}"), i * 16 + 16)
                    pool.sem_inc(s("pool_begun"), 1)
                    for k in range(J):
                        pool.indirect_dma_start(out=by_src, out_offset=AT(ap=idx_blk[h][:, k:k + 1], axis=0),
                                                in_=rows[h][:, k, :], in_offset=None)\
                            .then_inc(s(f"scattered{h}"), 16)

            turns(pool, body)

            def node_states(g, w, o):
                for h in range(2):
                    pool.wait_ge(s(f"stored{h}"), upto(g, f"stored{h}") + 16 * NB)
                pool.indirect_dma_start(out=fix_rows[:, 0:w], out_offset=None, in_=states[g],
                                        in_offset=AT(ap=fix_from[o][:, 0:1], axis=0)).then_inc(s("fix_in"), 16)
                pool.wait_ge(s("chunk_end"), upto(g, "chunk_end") + 1)
                pool.wait_ge(s("fixed"), upto(g, "fixed") + 1)
                pool.indirect_dma_start(out=states[g], out_offset=AT(ap=fix_to[o][:, 0:1], axis=0),
                                        in_=fix_rows[:, 0:w], in_offset=None,
                                        bounds_check=EP - 1, oob_is_err=False).then_inc(s("fix_out"), 16)
                pool.wait_ge(s("fix_out"), upto(g, "fix_out") + 16)
                for k in range(KN):
                    pool.indirect_dma_start(out=arena_a[:, k * w:(k + 1) * w], out_offset=None, in_=states[g],
                                            in_offset=AT(ap=end_i[o][:, k:k + 1], axis=0))\
                        .then_inc(s("nodes_in"), 16)

            pool.wait_ge(s("fix_index"), 1)
            pool.wait_ge(s("first_src"), 1)
            first_ends("src", first_src[:, 0:1])
            pool.wait_ge(s("fix_index"), 2)
            node_states("src", W01, "src")
            for g, w in (("c1", D), ("c2", D), ("at", W3)):
                pool.wait_ge(s("table_out"), upto(g, "table_out") + 32 if g == "at" else 16)
                if g == "at":
                    for k in range(KN):
                        pool.indirect_dma_start(out=adst_at_start, out_offset=AT(ap=start_i[:, k:k + 1], axis=0),
                                                in_=arena_b[:, k * HEADS:(k + 1) * HEADS], in_offset=None,
                                                bounds_check=EP - 1, oob_is_err=False)\
                            .then_inc(s("adst_scattered"), 16)
                    pool.indirect_dma_start(out=first_adst[:, :], out_offset=None, in_=adst_table,
                                            in_offset=AT(ap=dst_i[:, 1:2], axis=0))\
                        .then_inc(s("first_adst_in"), 16)

                def body(i):
                    for h in range(2):
                        pool.wait_ge(s(f"idx{h}"), upto(g, f"idx{h}") + i * 16 + 16)
                        if later(i):
                            pool.wait_ge(s("state"), upto(g, "state") + i * 2 + h - 1)
                        pool.sem_inc(s("pool_begun"), 1)
                        for k in range(J):
                            pool.indirect_dma_start(out=gb[h][:, k * w:(k + 1) * w], out_offset=None,
                                                    in_=table[g], in_offset=AT(ap=idx_blk[h][:, k:k + 1], axis=0))\
                                .then_inc(s(f"gathered{h}"), 16)

                turns(pool, body)
                node_states(g, W3S if g == "at" else D, "dst")

        def rstd(act, n):
            act.wait_ge(s("var"), upto(n, "var") + 1)
            act.activation(stat2[:, :], stat2[:, :], ACT.Sqrt).then_inc(s("root"), 1)

        work = carve(arena_b, [("t0", GT * P), ("t1", GT * P), ("r", GT * P), ("g0", GT * 3 * E32),
                               ("g1", GT * 3 * E32), ("y", KN * D)])

        def turned_act(act, g, n, i, h):
            act.wait_ge(s("turned"), upto(g, "turned") + i * 2 + h + 1)
            act.activation(work[f"t{h}"][0:n, 0:512], bank[1][0:n, :], ACT.Copy).then_inc(s("group_t"), 1)
            act.activation(work[f"t{h}"][0:n, 512:GT * P], bank[2][0:n, 0:GT * P - 512], ACT.Copy)\
               .then_inc(s("group_t"), 1)

        def mlp_act(act):
            def body(i):
                for h in range(2):
                    turned_act(act, "mlp", 3 * E32, i, h)
                    act.wait_ge(s("mlp_hid"), i * 2 + h + 1)
                    act.activation(work["r"][:, 0:512], bank[3][:, :], ACT.Relu, bias=b1[:, 0:1])\
                       .then_inc(s("mlp_r"), 1)
                    act.activation(work["r"][:, 512:GT * P], bank[4][:, 0:GT * P - 512], ACT.Relu, bias=b1[:, 0:1])\
                       .then_inc(s("mlp_r"), 1)

            act.wait_ge(s("b1_ready"), 1)
            turns(act, body, NG // 2)

        def dense_act(act, g):
            def body(i):
                for h in range(2):
                    turned_act(act, g, D, i, h)

            turns(act, body, NG // 2)

        def relu_act(act, g):
            act.wait_ge(s("conv"), upto(g, "conv") + 1)
            act.activation(hrows[:, 0:KN * D], hrows[:, 0:KN * D], ACT.Relu).then_inc(s("relu"), 1)

        def attention_act(act):
            def body(i):
                for h in range(2):
                    act.wait_ge(s("at_args"), i * 2 + h + 1)
                    act.activation(late["ex"], late["ex"], ACT.Exp).then_inc(s("at_exp"), 1)
                    act.activation(late["lk"], late["lk"], ACT.Exp).then_inc(s("at_exp"), 1)

            turns(act, body)
            act.wait_ge(s("at_chunk_args"), 1)
            act.activation(chunk_t1[0:W3S, :], chunk_t1[0:W3S, :], ACT.Exp).then_inc(s("at_chunk_exp"), 1)
            act.activation(chunk_t2[0:W3S, :], chunk_t2[0:W3S, :], ACT.Exp).then_inc(s("at_chunk_exp"), 1)
            act.wait_ge(s("at_fix_args"), 1)
            act.activation(fix_exp[:, :], fix_exp[:, :], ACT.Exp).then_inc(s("at_fix_exp"), 1)

        @block.scalar
        def _(act):
            act.wait_ge(s("w_loaded"), 16)
            act.activation(decay[:, :], decay[:, :], ACT.Exp, scale=-1.0).then_inc(s("decay_ready"), 1)

            def turned(g, q):
                act.wait_ge(s("tile_turned"), g + 1)
                act.activation(hi_t[q], p_hi_t[q], ACT.Copy).then_inc(s("hi_t_ready"), 1)

            def body(i):
                for h in range(2):
                    for k in range(J):
                        act.wait_ge(s("hist_added"), i * (2 * J) + h * J + k + 1)
                        act.activation(snap[k % 2], hist, ACT.Copy).then_inc(s("snap_ready"), 1)
                        if k % Q == 2:
                            turned(i * (2 * J // Q) + h * (J // Q) + k // Q + 1, (k // Q + 1) % 2)

            turned(0, 0)
            turns(act, body)

            rstd(act, "ln0")
            mlp_act(act)
            rstd(act, "ln1")
            act.wait_ge(s("degree_ready"), 1)
            act.activation(dinv[:, :], degree[:, :], ACT.Sqrt).then_inc(s("dinv_root"), 1)
            dense_act(act, "c1")
            relu_act(act, "c1")
            dense_act(act, "c2")
            relu_act(act, "c2")
            rstd(act, "ln2")
            dense_act(act, "at")
            attention_act(act)
            rstd(act, "ln3a")
            rstd(act, "ln3")

        @block.tensor
        def _(pe):
            for n, o in enumerate(("dst", "src")):
                if n == 0:
                    pe.wait_ge(s("consts"), 1)
                else:
                    pe.wait_ge(s("hist_read"), 1)
                pe.matmul(hist, zero_b[:, 0:HIGH], zero_b[:, 0:LOW], start=True, stop=False)

                def body(i):
                    for h in range(2):
                        pe.wait_ge(s("onehots"), upto(o, "onehots") + i * 2 + h + 1)
                        for k in range(J):
                            last = pe.matmul(hist, oh_hi[h][:, :, k], oh_lo[h][:, :, k], start=False, stop=False)
                        last.then_inc(s("onehots_used"), 1)

                turns(pe, body)
                pe.matmul(hist, zero_b[:, 0:HIGH], zero_b[:, 0:LOW], start=False, stop=True)\
                  .then_inc(s("hist_ready"), 1)
                pe.wait_ge(s("row_totals"), n + 1)
                pe.matmul(p_small[0:HIGH, 0:1], after[0:HIGH, 0:HIGH], ends_sb[:, LOW - 1:LOW], start=True,
                          stop=True).then_inc(s("row_offsets"), 1)
                if o == "dst":
                    pe.wait_ge(s("flag"), 1)
                    pe.matmul(p_small[:, 128:256], ones[:, :], diag[:, :], start=True, stop=True)\
                      .then_inc(s("flagrow"), 1)
            pe.wait_ge(s("base_ready"), 1)
            pe.matmul(hist, ident[0:HIGH, 0:HIGH], base[:, :], start=True, stop=True).then_inc(s("hist_added"), 1)

            def turn(h, k):
                q, at = k // Q % 2, slice(k % Q * P, (k % Q + 1) * P)
                turned = pe.matmul(p_hi_t[q][:, at], oh_hi[h][:, :, k], ident_b[:, :], start=True, stop=True)
                for n, w in enumerate(("hi", "lo")):
                    spread = pe.matmul(p_src[q][:, at], digit_blk[w][h][:, k:k + 1].to_broadcast([P, P]),
                                       ident_b[:, :], start=(n == 0), stop=(n == 1))
                if k % Q == Q - 1:
                    turned.then_inc(s("tile_turned"), 1)
                    spread.then_inc(s("src_spread"), 1)

            def body(i):
                for h in range(2):
                    for k in range(J):
                        t = i * (2 * J) + h * J + k
                        g = i * (2 * J // Q) + h * (J // Q) + k // Q
                        pe.wait_ge(s("snap_ready"), t + 1)
                        pe.matmul(hist, oh_hi[h][:, :, k], oh_lo[h][:, :, k], start=False, stop=True,
                                  skip_group_check=True).then_inc(s("hist_added"), 1)
                        if k % Q == 0:
                            pe.wait_ge(s("hi_t_ready"), g + 1)
                            if later(i) or h or k >= 2 * Q:
                                pe.wait_ge(s("selected"), (g - 1) * Q)
                        at = slice(k % Q * P, (k % Q + 1) * P)
                        last = pe.matmul(p_cnt[k // Q % 2][:, at], hi_t[k // Q % 2][:, at], snap[k % 2],
                                         start=True, stop=True)
                        if k % Q == Q - 1:
                            last.then_inc(s("counted"), 1)
                        nh, nk = (h, k // Q * Q + Q) if k < J - Q else (1 - h, 0)
                        if k % Q == 0:
                            if nk == 0:
                                pe.wait_ge(s("tile_onehots"), i * 2 + h + 2)
                            if later(i) or h or k:
                                pe.wait_ge(s("ranked"), g)
                            turn(nh, nk)
                            turn(nh, nk + 1)
                        if k % Q == 1:
                            turn(nh, nk + 2)
                            turn(nh, nk + 3)

            pe.wait_ge(s("tile_onehots"), 1)
            for k in range(Q):
                turn(0, k)
            turns(pe, body)

            def flagrow_src():
                pe.wait_ge(s("flag"), upto("src", "flag") + 1)
                pe.matmul(p_small[:, 128:256], ones[:, :], diag[:, :], start=True, stop=True)\
                  .then_inc(s("flagrow"), 1)

            def carries(g, w):
                pe.wait_ge(s("chunk_end"), upto(g, "chunk_end") + 1)
                if g == "src":
                    flagrow_src()
                pe.matmul(p_small[0:w, 0:P], chunk_end[:, 0:w], ident[:, :], start=True, stop=True)\
                  .then_inc(s("end_t"), 1)
                if g == "at":
                    pe.matmul(p_small[0:w, 256:384], mrep, ident[:, :], start=True, stop=True)\
                      .then_inc(s("end_t"), 1)
                pe.wait_ge(s("carry_t"), upto(g, "carry_t") + 1)
                pe.matmul(p_small[:, 384:384 + w], chunk_in_t[0:w, 0:P], ident[0:w, 0:w], start=True, stop=True)\
                  .then_inc(s("carry"), 1)
                if g == "at":
                    pe.matmul(p_small[:, 0:w], chunk_max_t[0:w, 0:P], ident[0:w, 0:w], start=True, stop=True)\
                      .then_inc(s("carry"), 1)

            def dense(g, n, w):
                def turn_group(i, h):
                    pe.wait_ge(s("grp"), upto(g, "grp") + i * 2 + h + 1)
                    for t in range(GT):
                        b = bank[1 + t // 4]
                        last = pe.matmul(b[0:n, (t % 4) * P:(t % 4 + 1) * P], work[f"g{h}"][:, t * n:(t + 1) * n],
                                         ident[:, :], start=True, stop=True)
                    last.then_inc(s("turned"), 1)

                def body(i):
                    for h in range(2):
                        pe.wait_ge(s("group_t"), upto(g, "group_t") + i * 4 + h * 2 + 2)
                        turned = work[f"t{h}"]
                        if g == "mlp":
                            pe.matmul(bank[3][:, :], w1[:, :], turned[0:n, 0:512], start=True, stop=True)
                            pe.matmul(bank[4][:, 0:GT * P - 512], w1[:, :], turned[0:n, 512:GT * P], start=True,
                                      stop=True).then_inc(s("mlp_hid"), 1)
                        if h == 0:
                            turn_group(i, 1)
                        elif not (isinstance(i, int) and i == NG // 2 - 1):
                            turn_group(i + 1, 0)
                        if g == "mlp":
                            pe.wait_ge(s("mlp_r"), i * 4 + h * 2 + 2)
                        if later(i):
                            pe.wait_ge(s("out_read"), upto(g, "out_read") + i * 2 + h - 1)
                        rows_t = work["r"] if g == "mlp" else turned[0:n, :]
                        for t in range(GT):
                            last = pe.matmul(bank[5 + h][:, t * D:(t + 1) * D], rows_t[:, t * P:(t + 1) * P], w[:, :],
                                             start=True, stop=True)
                        last.then_inc(s("prod"), 1)

                turn_group(0, 0)
                turns(pe, body, NG // 2, peel_last=True)

            carries("src", W01)
            pe.wait_ge(s("weights_loaded"), 16 * 16)
            dense("mlp", 3 * E32, w2)
            for g, w in (("c1", D), ("c2", D), ("at", W3S)):
                dense(g, D, wc[g])
                carries(g, w)


        @block.vector
        def _(v):
            chain = [0]

            def link(ins):
                chain[0] += 1
                ins.then_inc(s("v_chain"), 1)
                v.wait_ge(s("v_chain"), chain[0])

            def tell(name, n=1):
                v.sem_inc(s(name), n)

            v.wait_ge(s("iotas"), 2)
            link(v.tensor_copy(iota[:, :], iota_i[:, :]))
            link(v.tensor_copy(rowno[:, :], rowno_i[:, :]))
            link(v.tensor_scalar(rowno_l[:, :], rowno[:, :], float(L), None, ALU.mult))
            link(v.tensor_scalar(ident[:, :], iota[:, :], rowno[:, 0:1], None, ALU.is_equal))
            link(v.tensor_copy(ident_b[:, :], ident[:, :]))
            link(v.tensor_scalar(before[:, :], iota[:, :], rowno[:, 0:1], None, ALU.is_lt))
            link(v.tensor_scalar(after[:, :], iota[:, :], rowno[:, 0:1], None, ALU.is_gt))
            link(v.memset(ones[:, :], 1.0))
            link(v.tensor_copy(iota_lo, bc(iota[:, 0:LOW], J)))
            link(v.tensor_scalar(iota_hi, bc(iota[:, 0:HIGH], J), float(LOW), None, ALU.mult))
            link(v.memset(edge_ends[:, 0:1], -1.0))
            link(v.memset(zero_b[:, :], 0.0))
            tell("consts")
            v.wait_ge(s("src_loaded"), 16)
            v.wait_ge(s("dst_loaded"), 32)
            src_i = arena_b[:, 0:L].bitcast(i32)
            t_i = arena_b[:, L:2 * L].bitcast(i32)
            for o, ids in (("dst", dst_i[:, 1:L + 1]), ("src", src_i)):
                link(v.tensor_scalar(t_i, ids, LOW - 1, None, ALU.bitwise_and))
                link(v.tensor_copy(digits[o, "lo"][:, 0:L], t_i))
                link(v.tensor_scalar(t_i, ids, -LOW, None, ALU.bitwise_and))
                link(v.tensor_copy(digits[o, "hi"][:, 0:L], t_i))
                for w in ("hi", "lo"):
                    link(v.memset(digits[o, w][:, L:L + J], 0.0))
            link(v.memset(src_f[:, L:L + J], 0.0))
            link(v.tensor_copy(src_f[:, 0:L], src_i))
            link(v.tensor_tensor(same_dst[:, :], dst_i[:, 1:L + 1], dst_i[:, 0:L], ALU.is_equal))
            def of_nodes(o):
                link(v.tensor_tensor(has[o][:, :], nend[o][:, :], nstart[o][:, :], ALU.is_gt))
                link(v.tensor_scalar(tmpk[:, :], nend[o][:, :], -1.0, 0.0, ALU.add, ALU.max))
                link(v.tensor_copy(end_i[o][:, :], tmpk[:, :]))

            def fix_index(o, continues):
                v.wait_ge(s(f"first_end_{o}"), 16)
                end, inside = fix_tmp[:, 0:1], fix_tmp[:, 1:2]
                link(v.tensor_scalar(end, first_end[o][:, :], -1.0, None, ALU.add))
                link(v.tensor_copy(fix_from[o][:, :], end))
                link(v.tensor_tensor(inside, end, rowno_l[:, :], ALU.subtract))
                link(v.tensor_scalar(inside, inside, float(L), None, ALU.is_lt))
                link(v.tensor_tensor(inside, inside, continues, ALU.mult))
                link(v.tensor_scalar(inside, inside, -NOWHERE, NOWHERE, ALU.mult, ALU.add))
                link(v.tensor_tensor(inside, inside, end, ALU.add))
                link(v.tensor_copy(fix_to[o][:, :], inside))
                tell("fix_index")

            def of_dst():
                link(v.tensor_tensor(degree[:, :], nend["dst"][:, :], nstart["dst"][:, :], ALU.subtract))
                link(v.tensor_scalar(degree[:, :], degree[:, :], 1.0, None, ALU.add))
                tell("degree_ready")
                link(v.tensor_scalar(tmpk[:, :], has["dst"][:, :], -NOWHERE, NOWHERE, ALU.mult, ALU.add))
                link(v.tensor_tensor(tmpk[:, :], tmpk[:, :], nstart["dst"][:, :], ALU.add))
                link(v.tensor_copy(start_i[:, :], tmpk[:, :]))
                tell("node_index")
                link(v.tensor_tensor(flag[:, :], dst_i[:, 1:2], dst_i[:, L:L + 1], ALU.is_equal))
                link(v.tensor_tensor(flag[:, :], flag[:, :], same_dst[:, 0:1], ALU.mult))
                v.wait_ge(s("bounds_out"), 32)
                link(v.tensor_scalar(diag[:, :], ident[:, :], flag[:, 0:1], None, ALU.mult))
                tell("flag")
                v.wait_ge(s("flagrow"), upto("dst", "flagrow") + 1)
                link(v.tensor_copy(flagrow["dst"][:, :], p_small[:, 128:256]))

            for n, o in enumerate(("dst", "src")):
                def body(i):
                    for h in range(2):
                        if later(i):
                            v.wait_ge(s("onehots_used"), upto(o, "onehots_used") + i * 2 + h - 1)
                        elif n:
                            v.wait_ge(s("onehots_used"), NB * 2)
                        at = bass.ds(blk(i, h) * J, J)
                        v.tensor_tensor(oh_hi[h], iota_hi, bf(digits[o, "hi"][:, at], HIGH), ALU.is_equal)
                        v.tensor_tensor(oh_lo[h], iota_lo, bf(digits[o, "lo"][:, at], LOW), ALU.is_equal)\
                            .then_inc(s("onehots"), 1)

                turns(v, body)
                v.wait_ge(s("hist_ready"), n + 1)
                if n:
                    v.wait_ge(s("bounds_out"), 32)
                link(v.tensor_copy(hist_sb[:, :], hist))
                tell("hist_read")
                link(v.tensor_tensor_scan(ends_sb[:, :], ones[0:HIGH, 0:LOW], hist_sb[:, :], 0.0, ALU.mult, ALU.add))
                tell("row_totals")
                v.wait_ge(s("row_offsets"), n + 1)
                link(v.tensor_copy(offs_sb[:, :], p_small[0:HIGH, 0:1]))
                link(v.tensor_scalar(ends_sb[:, :], ends_sb[:, :], offs_sb[:, 0:1], None, ALU.add))
                starts = base if o == "src" else diag
                link(v.tensor_tensor(starts[0:HIGH, :], ends_sb[:, :], hist_sb[:, :], ALU.subtract))
                tell("bounds_ready")
                v.wait_ge(s("bounds_in"), 32 * (n + 1))
                of_nodes(o)
                if o == "dst":
                    of_dst()
            tell("base_ready")

            def digits_of(i, h, done):
                at = bass.ds(blk(i, h) * J, J)
                done(v.tensor_copy(digit_blk["hi"][h][:, :], digits["src", "hi"][:, at]))
                done(v.tensor_copy(digit_blk["lo"][h][:, :], digits["src", "lo"][:, at]))
                return done(v.tensor_copy(src_blk[:, h, :], src_f[:, at]))

            def onehots_of(i, h):
                v.tensor_tensor(oh_hi[h], iota_hi, bf(digit_blk["hi"][h][:, :], HIGH), ALU.is_equal)
                v.tensor_tensor(oh_lo[h], iota_lo, bf(digit_blk["lo"][h][:, :], LOW), ALU.is_equal)\
                    .then_inc(s("tile_onehots"), 1)

            v.wait_ge(s("onehots_used"), 2 * NB * 2)
            digits_of(0, 0, link)
            onehots_of(0, 0)
            v.wait_ge(s("decay_ready"), 1)
            v.wait_ge(s("first_row_in"), 16)
            v.wait_ge(s("tile_onehots"), 1)
            c = Steps(s("v_tiles"), 2 * (J + 4))

            def stage_a(i, h, quad, xk):
                for k in range(quad * Q, quad * Q + Q):
                    if k:
                        old = xb[h][:, k - 1, :]
                    elif not later(i) and h == 0:
                        old = first_row[:, :]
                    else:
                        old = xb[1 - h][:, J - 1, :]
                    v.wait_ge(c.sem, c.value(xk))
                    xk = c.done(v.scalar_tensor_tensor(out=xb[h][:, k, :], in0=old, scalar=mask_blk[:, h, k:k + 1],
                                                       in1=xs[h][:, k, :], op0=ALU.mult, op1=ALU.add))
                    if k % Q == 0:
                        v.wait_ge(s("src_spread"), i * (2 * J // Q) + h * (J // Q) + quad + 1)
                    rank = v.scalar_tensor_tensor(out=junk[k % 2], in0=p_src[quad % 2][:, k % Q * P:(k % Q + 1) * P],
                                                  scalar=src_blk[:, h, k:k + 1], in1=before[:, :],
                                                  op0=ALU.is_equal, op1=ALU.mult, accum_out=rank_blk[:, h, k:k + 1])
                rank.then_inc(s("ranked"), 1)
                return xk

            def stage_b(i, h, quad):
                group = i * (2 * J // Q) + h * (J // Q) + quad
                v.wait_ge(s("counted"), group + 1)
                for k in range(quad * Q, quad * Q + Q):
                    place = v.scalar_tensor_tensor(out=junk[2 + k % 2], in0=p_cnt[quad % 2][:, k % Q * P:(k % Q + 1) * P],
                                                   scalar=1.0, in1=oh_lo[h][:, :, k], op0=ALU.mult, op1=ALU.mult,
                                                   accum_out=sel_blk[:, h, k:k + 1])
                    place.then_inc(s("selected"), 1)
                    if k % 2:
                        v.wait_ge(s("selected"), group * Q + k % Q + 1)
                if quad == J // Q - 1:
                    at = bass.ds(blk(i, h) * J, J)
                    if later(i):
                        v.wait_ge(s(f"scattered{h}"), scattered(i, h))
                    v.tensor_tensor(rows[h][:, :, 0:D], xb[h], bc(decay[:, at], D), ALU.mult)
                    v.tensor_copy(rows[h][:, :, TW - 1:TW], bc(src_blk[:, h, :], 1))
                    v.tensor_tensor(idx_blk[h][:, :], rank_blk[:, h, :], sel_blk[:, h, :], ALU.add)\
                        .then_inc(s("rows_ready"), 1)

            def body(i):
                c.turn(i)
                for h in range(2):
                    xk = c.done(v.tensor_copy(mask_blk[:, h, :], same_dst[:, bass.ds(blk(i, h) * J, J)]))
                    v.wait_ge(s(f"xs_in{h}"), i * 16 + 16)
                    for quad in range(J // Q):
                        xk = stage_a(i, h, quad, xk)
                        if quad:
                            stage_b(i, h, quad - 1)
                        elif h:
                            stage_b(i, 0, J // Q - 1)
                        elif later(i):
                            stage_b(i - 1, 1, J // Q - 1)
                        if quad == 1:
                            ni, nh = (i, 1) if h == 0 else (i + 1, 0)
                            if later(i) or h:
                                v.wait_ge(s("hist_added"), (i * 2 + h) * J + 1)
                            v.wait_ge(c.sem, c.value(digits_of(ni, nh, c.done)))
                            onehots_of(ni, nh)
                assert c.k == c.per, (c.k, c.per)

            turns(v, body, peel=2)
            stage_b(NB - 1, 1, J // Q - 1)

            v.wait_ge(s("rows_ready"), NB * 2)
            fix_index("dst", same_dst[:, 0:1])
            v.wait_ge(s("edge_ends_in"), 48)
            link(v.tensor_copy(first_src[:, :], edge_ends[:, 1:2]))
            tell("first_src")
            link(v.memset(chunk_end[:, 0:D + E32], 0.0))
            link(v.memset(chunk_end[:, D + E32:W01], -HUGE))
            link(v.tensor_copy(prev_src[:, :], edge_ends[:, 0:1]))
            c2 = Steps(s("v_src"), 2 * (5 + 2 * J - 1))
            WS = D + E32

            def body(i):
                c2.turn(i)
                for h in range(2):
                    v.wait_ge(s(f"tb_in{h}"), i * 16 + 16)
                    if later(i):
                        v.wait_ge(s(f"stored{h}"), upto("src", f"stored{h}") + i * 16)
                    if later(i) or h:
                        v.wait_ge(s("state"), upto("src", "state") + i * 2 + h)
                    ids = tb[h][:, :, TW - 1]
                    c2.done(v.tensor_tensor(mask_blk[:, h, 0:1], tb[h][:, 0, TW - 1:TW], prev_src[:, :], ALU.is_equal))
                    m = c2.done(v.tensor_tensor(mask_blk[:, h, 1:J], ids[:, 1:J], ids[:, 0:J - 1], ALU.is_equal))
                    v.wait_ge(c2.sem, c2.value(m))
                    c2.done(v.tensor_copy(prev_src[:, :], tb[h][:, J - 1, TW - 1:TW]))
                    m = c2.done(v.tensor_scalar(cap_blk[:, h, :], mask_blk[:, h, :], 2.0, -1.0, ALU.mult, ALU.add))
                    v.wait_ge(c2.sem, c2.value(m))
                    xk = mk = c2.done(v.tensor_scalar(cap_blk[:, h, :], cap_blk[:, h, :], HUGE, None, ALU.mult))
                    for k in range(J):
                        new = st[h][:, k * W01:(k + 1) * W01]
                        if k:
                            old = st[h][:, (k - 1) * W01:k * W01]
                        elif not later(i) and h == 0:
                            old = chunk_end[:, :]
                        else:
                            old = st[1 - h][:, (J - 1) * W01:J * W01]
                        v.wait_ge(c2.sem, c2.value(xk))
                        xk = c2.done(v.scalar_tensor_tensor(out=new[:, 0:WS], in0=old[:, 0:WS],
                                                            scalar=mask_blk[:, h, k:k + 1],
                                                            in1=tb[h][:, k, 0:WS], op0=ALU.mult, op1=ALU.add))
                        v.wait_ge(c2.sem, c2.value(mk))
                        ins = v.scalar_tensor_tensor(out=new[:, WS:W01], in0=old[:, WS:W01],
                                                     scalar=cap_blk[:, h, k:k + 1],
                                                     in1=tb[h][:, k, D:WS], op0=ALU.min, op1=ALU.max)
                        if k < J - 1:
                            mk = c2.done(ins)
                        else:
                            ins.then_inc(s("state"), 1)
                assert c2.k == c2.per, (c2.k, c2.per)

            turns(v, body)

            def chunk_ends(g, w):
                v.wait_ge(s("state"), upto(g, "state") + NB * 2)
                link(v.tensor_copy(chunk_end[:, 0:w], st[1][:, (J - 1) * w:J * w]))

            chunk_ends("src", W01)
            link(v.tensor_tensor(flag[:, :], edge_ends[:, 1:2], edge_ends[:, 2:3], ALU.is_equal))
            link(v.tensor_tensor(edge_ends[:, 0:1], edge_ends[:, 0:1], edge_ends[:, 1:2], ALU.is_equal))
            link(v.tensor_tensor(flag[:, :], flag[:, :], edge_ends[:, 0:1], ALU.mult))
            fix_index("src", edge_ends[:, 0:1])
            link(v.tensor_scalar(diag[:, :], ident[:, :], flag[:, 0:1], None, ALU.mult))
            tell("flag")
            tell("chunk_end")
            v.wait_ge(s("flagrow"), upto("src", "flagrow") + 1)
            v.wait_ge(s("end_t"), upto("src", "end_t") + 1)
            link(v.tensor_copy(flagrow["src"][:, :], p_small[:, 128:256]))
            fr = flagrow["src"]
            link(v.memset(chunk_in_t[:, 0:1], 0.0))
            link(v.tensor_tensor_scan(chunk_in_t[0:WS, 1:P + 1], fr[0:WS, :], p_small[0:WS, 0:P], 0.0,
                                      ALU.mult, ALU.add))
            link(v.tensor_scalar(chunk_t1[WS:W01, :], fr[WS:W01, :], 2.0, -1.0, ALU.mult, ALU.add))
            link(v.tensor_scalar(chunk_t1[WS:W01, :], chunk_t1[WS:W01, :], HUGE, None, ALU.mult))
            link(v.tensor_tensor_scan(chunk_in_t[WS:W01, 1:P + 1], chunk_t1[WS:W01, :], p_small[WS:W01, 0:P], 0.0,
                                      ALU.min, ALU.max))
            tell("carry_t")
            v.wait_ge(s("carry"), upto("src", "carry") + 1)
            link(v.tensor_copy(chunk_in[:, :], p_small[:, 384:384 + W01]))

            v.wait_ge(s("fix_in"), 16)
            link(v.tensor_tensor(fix_rows[:, 0:WS], fix_rows[:, 0:WS], chunk_in[:, 0:WS], ALU.add))
            link(v.tensor_tensor(fix_rows[:, WS:W01], fix_rows[:, WS:W01], chunk_in[:, WS:W01], ALU.max))
            tell("fixed")
            v.wait_ge(s("nodes_in"), upto("src", "nodes_in") + 16 * KN)

            def gathered(w):
                return arena_a[:, 0:KN * w].rearrange("p (k c) -> p k c", c=w)

            def nodes(ap):
                return ap.rearrange("p (k c) -> p k c", k=KN)

            got = gathered(W01)
            link(v.tensor_tensor(got, got, bc(has["src"][:, :], W01), ALU.mult))

            def layer_norm(n, y, z, scratch):
                y3, z3, s3 = nodes(y), nodes(z), nodes(scratch)
                link(v.tensor_reduce(stat1[:, :], y3, AX.X, ALU.add))
                link(v.tensor_scalar(stat1[:, :], stat1[:, :], 1.0 / D, None, ALU.mult))
                link(v.tensor_tensor(z3, y3, bc(stat1[:, :], D), ALU.subtract))
                link(v.tensor_tensor(s3, z3, z3, ALU.mult))
                link(v.tensor_reduce(stat2[:, :], s3, AX.X, ALU.add))
                link(v.tensor_scalar(stat2[:, :], stat2[:, :], 1.0 / D, 1e-5, ALU.mult, ALU.add))
                tell("var")
                v.wait_ge(s("root"), upto(n, "root") + 1)
                link(v.reciprocal(stat2[:, :], stat2[:, :]))
                link(v.tensor_tensor(z3, z3, bc(stat2[:, :], D), ALU.mult))

            ND = KN * D
            xf = x[:, :]
            link(v.tensor_tensor(nodes(xf), nodes(xf), got[:, :, 0:D], ALU.add))
            layer_norm("ln0", xf, xf, arena_b[:, 0:ND])

            v.wait_ge(s("weights_loaded"), 16 * 16)
            link(v.scalar_tensor_tensor(out=b1[:, :], in0=w1u[:, :], scalar=u0[:, 0:1], in1=b1[:, :],
                                        op0=ALU.mult, op1=ALU.add))
            tell("b1_ready")
            link(v.tensor_tensor(tmpk[:, :], nend["src"][:, :], nstart["src"][:, :], ALU.subtract))
            link(v.tensor_scalar(tmpk[:, :], tmpk[:, :], 1.0, None, ALU.max))
            link(v.reciprocal(tmpk[:, :], tmpk[:, :]))

            def groups(g, fill, take):
                def body(i):
                    for h in range(2):
                        if h == 0:
                            fill(i * 2 + 1, 1)
                        elif not (isinstance(i, int) and i == NG // 2 - 1):
                            fill(i * 2 + 2, 0)
                        v.wait_ge(s("prod"), upto(g, "prod") + i * 2 + h + 1)
                        take(i * 2 + h, bank[5 + h][:, 0:GT * D])

                fill(0, 0)
                turns(v, body, NG // 2, peel_last=True)
                v.wait_ge(s("out_read"), upto(g, "out_read") + NG)

            def fill(n, h):
                part = arena_a[:, bass.ds(n * (GT * W01), GT * W01)].rearrange("p (t c) -> p t c", c=W01)
                hin = work[f"g{h}"].rearrange("p (t c) -> p t c", c=3 * E32)
                v.tensor_copy(hin[:, :, 0:2 * E32], part[:, :, D:W01])
                v.tensor_tensor(hin[:, :, 2 * E32:], part[:, :, D:D + E32], bc(tmpk[:, bass.ds(n * GT, GT)], E32),
                                ALU.mult).then_inc(s("grp"), 1)

            def take(n, prod):
                at = bass.ds(n * (GT * D), GT * D)
                v.tensor_tensor(work["y"][:, at], prod, x[:, at], ALU.add).then_inc(s("out_read"), 1)

            groups("mlp", fill, take)
            link(v.tensor_tensor(nodes(work["y"]), nodes(work["y"]), bf(b2[:, :], KN), ALU.add))
            layer_norm("ln1", work["y"], xf, arena_a[:, 0:ND])

            v.wait_ge(s("dinv_root"), 1)
            link(v.reciprocal(dinv[:, :], dinv[:, :]))

            def dense(g, source, w):
                def fill(n, h):
                    v.tensor_copy(work[f"g{h}"][:, 0:GT * D], source[:, bass.ds(n * (GT * D), GT * D)])\
                        .then_inc(s("grp"), 1)

                def take(n, prod):
                    to = hrows[:, bass.ds(n * (GT * w), GT * w)].rearrange("p (t c) -> p t c", c=w)[:, :, 0:D]
                    prod = prod.rearrange("p (t c) -> p t c", c=D)
                    if g == "at":
                        ins = v.tensor_copy(to, prod)
                    else:
                        ins = v.tensor_tensor(to, prod, bc(dinv[:, bass.ds(n * GT, GT)], D), ALU.mult)
                    ins.then_inc(s("out_read"), 1)

                groups(g, fill, take)

            def conv(g, source):
                dense(g, source, D)
                tell("table")
                link(v.memset(chunk_end[:, :], 0.0))
                cc = Steps(s("chain"), 2 * J, upto(g, "chain"))

                def body(i):
                    cc.turn(i)
                    for h in range(2):
                        if later(i):
                            v.wait_ge(s(f"stored{h}"), upto(g, f"stored{h}") + i * 16)
                        if later(i) or h:
                            v.wait_ge(s("state"), upto(g, "state") + i * 2 + h)
                        xk = cc.done(v.tensor_copy(mask_blk[:, h, :], same_dst[:, bass.ds(blk(i, h) * J, J)]))
                        v.wait_ge(s(f"gathered{h}"), upto(g, f"gathered{h}") + i * (16 * J) + 16 * J)
                        for k in range(J):
                            if k:
                                old = st[h][:, (k - 1) * D:k * D]
                            elif not later(i) and h == 0:
                                old = chunk_end[:, 0:D]
                            else:
                                old = st[1 - h][:, (J - 1) * D:J * D]
                            v.wait_ge(cc.sem, cc.value(xk))
                            ins = v.scalar_tensor_tensor(out=st[h][:, k * D:(k + 1) * D], in0=old,
                                                         scalar=mask_blk[:, h, k:k + 1],
                                                         in1=gb[h][:, k * D:(k + 1) * D], op0=ALU.mult, op1=ALU.add)
                            if k < J - 1:
                                xk = cc.done(ins)
                            else:
                                ins.then_inc(s("state"), 1)
                    assert cc.k == cc.per, (cc.k, cc.per)

                turns(v, body)
                chunk_ends(g, D)
                tell("chunk_end")
                v.wait_ge(s("end_t"), upto(g, "end_t") + 1)
                link(v.tensor_tensor_scan(chunk_in_t[0:D, 1:P + 1], flagrow["dst"][0:D, :], p_small[0:D, 0:P], 0.0,
                                          ALU.mult, ALU.add))
                tell("carry_t")
                v.wait_ge(s("carry"), upto(g, "carry") + 1)
                link(v.tensor_copy(chunk_in[:, 0:D], p_small[:, 384:384 + D]))
                v.wait_ge(s("fix_in"), upto(g, "fix_in") + 16)
                link(v.tensor_tensor(fix_rows[:, 0:D], fix_rows[:, 0:D], chunk_in[:, 0:D], ALU.add))
                tell("fixed")
                v.wait_ge(s("nodes_in"), upto(g, "nodes_in") + 16 * KN)
                got = gathered(D)
                h3 = nodes(hrows[:, 0:ND])
                v.wait_ge(s("table_out"), upto(g, "table_out") + 16)
                link(v.tensor_tensor(got, got, bc(has["dst"][:, :], D), ALU.mult))
                link(v.tensor_tensor(h3, got, h3, ALU.add))
                link(v.tensor_tensor(h3, h3, bc(dinv[:, :], D), ALU.mult))
                link(v.tensor_tensor(h3, h3, bf(bcv[g][:, :], KN), ALU.add))
                tell("conv")
                v.wait_ge(s("relu"), upto(g, "relu") + 1)

            conv("c1", x)
            conv("c2", hrows)
            link(v.tensor_tensor(xf, xf, hrows[:, 0:ND], ALU.add))
            layer_norm("ln2", xf, xf, arena_b[:, 0:ND])

            dense("at", x, W3)
            h4 = hrows[:, :].rearrange("p (k c) -> p k c", c=W3)
            pr = arena_a[:, 0:ND]
            for wv, to in ((asrc_w, h4[:, :, D:W3]), (adst_w, arena_b[:, 0:KN * HEADS].rearrange("p (k c) -> p k c", c=HEADS))):
                link(v.tensor_tensor(nodes(pr), h4[:, :, 0:D], bf(wv[:, :], KN), ALU.mult))
                link(v.tensor_reduce(to, pr.rearrange("p (k c d) -> p k c d", c=HEADS, d=HD), AX.X, ALU.add))
            tell("table")
            v.wait_ge(s("adst_in"), 16)
            v.wait_ge(s("first_adst_in"), 16)
            adst = arena_b[:, KN * HEADS:KN * HEADS + L * HEADS]
            adst_h = adst.rearrange("p (l c) -> p c l", c=HEADS)
            for hd in range(HEADS):
                link(v.tensor_tensor_scan(adst_h[:, hd, :], same_dst[:, :], adst_h[:, hd, :],
                                          first_adst[:, hd:hd + 1], ALU.mult, ALU.add))
            mx = late["mx"].rearrange("p (c j) -> p c j", j=J + 1)
            link(v.memset(mx[:, :, J:J + 1], 0.0))
            link(v.memset(chunk_end[:, :], 0.0))

            def hj(name):
                t = late[name]
                return t.rearrange("p (c j) -> p c j", j=J), t.rearrange("p (c j) -> p j c", j=J)

            (ex, ex_j), (lk, lk_j) = hj("ex"), hj("lk")
            sc = late["sc"]
            prod = late["prod"]
            prod4 = prod.rearrange("p (j c f) -> p j c f", c=HEADS, f=E16)
            wv4 = wedge[:, :].rearrange("p (o f c) -> p o c f", o=1, c=HEADS).to_broadcast([P, J, HEADS, E16])
            cf = late["cf"].rearrange("p (j w) -> p j w", w=W3)
            ca = Steps(s("chain"), 2 * (15 + HEADS + 2 * J), upto("at", "chain"))

            def per_head(ap3, n):
                return ap3.rearrange("p j (c o) -> p j c o", o=1).to_broadcast([P, J, HEADS, n])

            def body(i):
                ca.turn(i)

                def then(ins):
                    k = ca.done(ins)
                    v.wait_ge(ca.sem, ca.value(k))

                for h in range(2):
                    if later(i):
                        v.wait_ge(s(f"stored{h}"), upto("at", f"stored{h}") + i * 16)
                    if later(i) or h:
                        v.wait_ge(s("state"), upto("at", "state") + i * 2 + h)
                    m = mask_blk[:, h, :]
                    g3 = gb[h].rearrange("p (j w) -> p j w", w=W3)
                    ca.done(v.tensor_copy(m, same_dst[:, bass.ds(blk(i, h) * J, J)]))
                    ca.done(v.tensor_copy(mx[:, :, 0:1], mx[:, :, J:J + 1]))
                    v.wait_ge(s(f"a16_in{h}"), i * 16 + 16)
                    then(v.tensor_tensor(prod4, a16[h].rearrange("p j (o f) -> p j o f", o=1)
                                         .to_broadcast([P, J, HEADS, E16]), wv4, ALU.mult))
                    then(v.tensor_reduce(sc, prod.rearrange("p (a f) -> p a f", f=E16), AX.X, ALU.add))
                    then(v.tensor_tensor(sc, sc, adst[:, bass.ds(blk(i, h) * (J * HEADS), J * HEADS)], ALU.add))
                    v.wait_ge(s(f"gathered{h}"), upto("at", f"gathered{h}") + i * (16 * J) + 16 * J)
                    sc3 = sc.rearrange("p (j c) -> p j c", c=HEADS)
                    then(v.tensor_tensor(sc3, sc3, g3[:, :, D:W3], ALU.add))
                    then(v.scalar_tensor_tensor(out=lk_j, in0=sc3, scalar=0.2, in1=sc3, op0=ALU.mult, op1=ALU.max))
                    for hd in range(HEADS):
                        k = ca.done(v.tensor_tensor_scan(mx[:, hd, 1:J + 1], m, lk[:, hd, :], mx[:, hd, 0:1],
                                                         ALU.mult, ALU.max))
                    v.wait_ge(ca.sem, ca.value(k))
                    then(v.tensor_tensor(ex, mx[:, :, 0:J], bf(m, HEADS), ALU.mult))
                    then(v.tensor_tensor(ex, ex, mx[:, :, 1:J + 1], ALU.subtract))
                    then(v.tensor_tensor(lk, lk, mx[:, :, 1:J + 1], ALU.subtract))
                    v.sem_inc(s("at_args"), 1)
                    v.wait_ge(s("at_exp"), (i * 2 + h) * 2 + 2)
                    then(v.tensor_tensor(ex, ex, bf(m, HEADS), ALU.mult))
                    ca.done(v.tensor_copy(cf[:, :, 0:D].rearrange("p j (c d) -> p j c d", d=HD), per_head(ex_j, HD)))
                    ca.done(v.tensor_copy(cf[:, :, D:W3], ex_j))
                    hview = g3[:, :, 0:D].rearrange("p j (c d) -> p j c d", d=HD)
                    ca.done(v.tensor_tensor(hview, hview, per_head(lk_j, HD), ALU.mult))
                    ca.done(v.tensor_copy(g3[:, :, D:W3], lk_j))
                    s3 = st[h][:, 0:J * W3S].rearrange("p (j w) -> p j w", w=W3S)
                    then(v.tensor_copy(s3[:, :, W3:W3S], mx[:, :, 1:J + 1].rearrange("p c j -> p j c")))
                    for k in range(J):
                        if k:
                            old = s3[:, k - 1, 0:W3]
                        elif not later(i) and h == 0:
                            old = chunk_end[:, 0:W3]
                        else:
                            old = st[1 - h][:, (J - 1) * W3S:(J - 1) * W3S + W3]
                        tmp = late["tmp"][:, (k % 2) * W3:(k % 2 + 1) * W3]
                        then(v.tensor_tensor(tmp, old, cf[:, k, :], ALU.mult))
                        ins = v.tensor_tensor(s3[:, k, 0:W3], tmp, g3[:, k, :], ALU.add)
                        if k < J - 1:
                            then(ins)
                        else:
                            ins.then_inc(s("state"), 1)
                assert ca.k == ca.per

            turns(v, body)
            chunk_ends("at", W3S)
            link(v.tensor_copy(mrep[:, 0:D].rearrange("p (c d) -> p c d", d=HD), bc(chunk_end[:, W3:W3S], HD)))
            link(v.tensor_copy(mrep[:, D:W3], chunk_end[:, W3:W3S]))
            link(v.tensor_copy(mrep[:, W3:W3S], chunk_end[:, W3:W3S]))
            tell("chunk_end")
            v.wait_ge(s("end_t"), upto("at", "end_t") + 2)
            fr = flagrow["dst"][0:W3S, :]
            pm, psum_t = p_small[0:W3S, 256:384], p_small[0:W3S, 0:P]
            mo = chunk_max_t[0:W3S, :]
            t1, t2 = chunk_t1[0:W3S, :], chunk_t2[0:W3S, :]
            link(v.memset(chunk_max_t[:, 0:1], 0.0))
            link(v.tensor_tensor_scan(mo[:, 1:P + 1], fr, pm, 0.0, ALU.mult, ALU.max))
            link(v.tensor_tensor(t1, fr, mo[:, 0:P], ALU.mult))
            link(v.tensor_tensor(t1, t1, mo[:, 1:P + 1], ALU.subtract))
            link(v.tensor_tensor(t2, pm, mo[:, 1:P + 1], ALU.subtract))
            tell("at_chunk_args")
            v.wait_ge(s("at_chunk_exp"), 2)
            link(v.tensor_tensor(t1, t1, fr, ALU.mult))
            link(v.tensor_tensor(t2, t2, psum_t, ALU.mult))
            link(v.tensor_tensor_scan(chunk_in_t[0:W3S, 1:P + 1], t1, t2, 0.0, ALU.mult, ALU.add))
            tell("carry_t")
            v.wait_ge(s("carry"), upto("at", "carry") + 2)
            link(v.tensor_copy(chunk_in[:, 0:W3], p_small[:, 384:384 + W3]))
            link(v.tensor_copy(chunk_in[:, W3:W3S], p_small[:, W3:W3S]))
            v.wait_ge(s("fix_in"), upto("at", "fix_in") + 16)
            e_state, e_carry = fix_exp[:, 0:HEADS], fix_exp[:, HEADS:2 * HEADS]
            link(v.tensor_tensor(chunk_end[:, 0:HEADS], fix_rows[:, W3:W3S], chunk_in[:, W3:W3S], ALU.max))
            link(v.tensor_tensor(e_state, fix_rows[:, W3:W3S], chunk_end[:, 0:HEADS], ALU.subtract))
            link(v.tensor_tensor(e_carry, chunk_in[:, W3:W3S], chunk_end[:, 0:HEADS], ALU.subtract))
            tell("at_fix_args")
            v.wait_ge(s("at_fix_exp"), 1)
            for t, e in ((fix_rows, e_state), (chunk_in, e_carry)):
                by_head = t[:, 0:D].rearrange("p (c d) -> p c d", d=HD)
                link(v.tensor_tensor(by_head, by_head, bc(e, HD), ALU.mult))
                link(v.tensor_tensor(t[:, D:W3], t[:, D:W3], e, ALU.mult))
            link(v.tensor_tensor(fix_rows[:, 0:W3], fix_rows[:, 0:W3], chunk_in[:, 0:W3], ALU.add))
            tell("fixed")
            v.wait_ge(s("nodes_in"), upto("at", "nodes_in") + 16 * KN)
            got = gathered(W3S)
            link(v.tensor_tensor(got, got, bc(has["dst"][:, :], W3S), ALU.mult))
            e_got = arena_b[:, ND:ND + KN * HEADS].rearrange("p (k c) -> p k c", c=HEADS)

            def heads(ap3):
                return ap3[:, :, 0:D].rearrange("p k (c d) -> p k c d", d=HD)

            def wide(e):
                return e.rearrange("p k (c o) -> p k c o", o=1).to_broadcast([P, KN, HEADS, HD])

            link(v.tensor_scalar(e_got, got[:, :, D:W3], 1e-8, None, ALU.add))
            link(v.reciprocal(e_got, e_got))
            link(v.tensor_tensor(heads(got), heads(got), wide(e_got), ALU.mult))
            y = arena_b[:, 0:ND]
            link(v.tensor_tensor(nodes(y), got[:, :, 0:D], h4[:, :, 0:D], ALU.add))
            layer_norm("ln3a", y, y, arena_a[:, 0:ND])
            link(v.tensor_tensor(nodes(y), nodes(y), bf(gamma[:, :], KN), ALU.mult))
            link(v.tensor_tensor(nodes(y), nodes(y), bf(beta[:, :], KN), ALU.add))
            link(v.tensor_tensor(xf, xf, y, ALU.add))
            layer_norm("ln3", xf, xf, arena_a[:, 0:ND])
            tell("final")


_NAMES = {
    "x": "x", "src": "src", "dst": "dst", "a16": "edge_attr_16", "a32": "edge_attr_32", "w": "edge_weight",
    "u": "L1_gnn_u", "L1_W1": "L1_gnn_W1", "L1_b1": "L1_gnn_b1", "L1_W2": "L1_gnn_W2", "L1_b2": "L1_gnn_b2",
    "L2_W1": "L2_gnn_W1", "L2_b1": "L2_gnn_b1", "L2_W2": "L2_gnn_W2", "L2_b2": "L2_gnn_b2",
    "W_node": "L3_gnn_W_node", "W_edge": "L3_gnn_W_edge", "attn_src": "L3_gnn_attn_src",
    "attn_dst": "L3_gnn_attn_dst", "gamma": "L3_gnn_ln_gamma", "beta": "L3_gnn_ln_beta",
}


def kernel(**inputs):
    import numpy as np
    import concourse.bacc as bacc
    from concourse.bass_utils import run_bass_kernel_spmd

    nc = bacc.Bacc("TRN2", target_bir_lowering=False, num_devices=1)
    arrays, aps = {}, {}
    for short, name in _NAMES.items():
        v = np.asarray(inputs[name])
        rows_padded = {"x": NP, "src": EP, "dst": EP, "a16": EP, "a32": EP, "w": EP}.get(short)
        if rows_padded:
            full = np.full((rows_padded,) + v.shape[1:], N_NODES if short in ("src", "dst") else 0, v.dtype)
            full[:v.shape[0]] = v
            v = full
        v = np.ascontiguousarray(v)
        arrays[f"in_{short}"] = v
        aps[short] = nc.dram_tensor(f"in_{short}", v.shape, mybir.dt.from_np(v.dtype), kind="ExternalInput").ap()
    out = nc.dram_tensor("out_x", (NP, D), f32, kind="ExternalOutput").ap()
    program(nc, aps, out)
    r = run_bass_kernel_spmd(nc, [arrays], core_ids=[0])
    return r.results[0]["out_x"][:N_NODES]
```

```python
import concourse.bass as bass
from concourse import mybir
from contextlib import ExitStack

P = 128
N_NODES, N_EDGES, D = 12500, 200000, 64
KN = -(-N_NODES // P)
NP = KN * P
J = 16
Q = 4
NB = -(-N_EDGES // (P * 2 * J))
L = NB * 2 * J
R = 4
EP = P * L
E32, E16, HEADS, HID = 32, 16, 4, 128
HD = D // HEADS
LOW = 128
HIGH = NP // LOW
TW = D + E32 + 1
W01 = D + 2 * E32
W3 = D + HEADS
W3S = D + 2 * HEADS
GT = 7
NG = KN // GT
PARTS = ((0, 4), (4, 4), (8, NG - 8))
PK = max(n for _, n in PARTS) * GT
HUGE = 3.4e38
NOWHERE = float(1 << 22)

f32, bf16, i32 = mybir.dt.float32, mybir.dt.bfloat16, mybir.dt.int32
ALU, ACT, AX = mybir.AluOpType, mybir.ActivationFunctionType, mybir.AxisListType
AT = bass.IndirectOffsetOnAxis


ADDED = {
    "state": 2 * NB, "stored0": 16 * NB, "stored1": 16 * NB, "gathered0": 16 * J * NB, "gathered1": 16 * J * NB,
    "idx0": 16 * NB, "idx1": 16 * NB, "fix_in": 16, "fixed": 1, "fix_out": 16,
    "chunk_end": 1, "end_t": 1, "carry": 1, "carry_t": 1, "table": len(PARTS),
    "table_out": 16 * len(PARTS),
    "onehots": 2 * NB, "onehots_used": 2 * NB, "flag": 1, "flagrow": 1, "chain": 2 * J * NB,
}
PASSES, CONVS = ("src", "c1", "c2", "at"), ("c1", "c2", "at")
ORDER = dict.fromkeys(ADDED, PASSES)
ORDER.update(dict.fromkeys(("gathered0", "gathered1", "idx0", "idx1", "table", "table_out", "chain"),
                           CONVS))
ORDER.update(dict.fromkeys(("onehots", "onehots_used"), ("dst", "src")))
ORDER.update(dict.fromkeys(("flag", "flagrow"), ("dst", "src")))


def upto(stage, name):
    return ORDER[name].index(stage) * ADDED[name]


DENSE = [(g, p) for p in range(len(PARTS)) for g in ("mlp", "c1")] + [(g, p) for g in ("c2", "at")
                                                                    for p in range(len(PARTS))]


def groups_before(stage, part):
    return sum(PARTS[p][1] for _, p in DENSE[:DENSE.index((stage, part))]) - PARTS[part][0]


def columns(part):
    g0, n = PARTS[part]
    return g0 * GT, (g0 + n) * GT


def part_turns(eng, body, part):
    first, end = PARTS[part][0] // 2, (PARTS[part][0] + PARTS[part][1]) // 2
    body(first, False)
    if end - first > 2:
        with eng.Fori(first + 1, end - 1) as i:
            body(i, False)
    body(end - 1, True)


def later(i):
    return not isinstance(i, int) or i > 0


def turns(eng, body, n=NB, peel=1, peel_last=False):
    for i in range(peel):
        body(i)
    with eng.Fori(peel, n - peel_last) as i:
        body(i)
    if peel_last:
        body(n - 1)


class Steps:

    def __init__(self, sem, per, base=0):
        self.sem, self.per, self.base = sem, per, base

    def turn(self, i):
        self.i, self.k = i, 0

    def done(self, ins):
        ins.then_inc(self.sem, 1)
        self.k += 1
        return self.k

    def value(self, k):
        return self.i * self.per + (k + self.base)


def bc(ap, n):
    return ap.rearrange("p (a o) -> p a o", o=1).to_broadcast([ap.shape[0], ap.shape[1], n])


def bf(ap, n):
    return ap.rearrange("p (o a) -> p o a", o=1).to_broadcast([ap.shape[0], n, ap.shape[1]])


def program(nc, a, out):
    with ExitStack() as ctx:
        def sb(name, shape, dt=f32):
            return ctx.enter_context(nc.sbuf_tensor(name, shape, dt))

        def ps(name, shape):
            return ctx.enter_context(nc.psum_tensor(name, shape, f32))

        def sem(name):
            return ctx.enter_context(nc.semaphore(name))

        def dram(name, shape, dt=f32):
            return nc.dram_tensor(name, shape, dt, kind="Internal").ap()

        x_at_start = dram("x_at_start", (EP, D))
        adst_at_start = dram("adst_at_start", (EP, HEADS))
        by_src = dram("by_src", (EP, TW))
        states = {g: dram(f"states_{g}", (EP, w)) for g, w in
                  (("src", W01), ("c1", D), ("c2", D), ("at", W3S))}
        table = {"c1": dram("table_c1", (NP, D)), "c2": dram("table_c2", (NP, D)),
                 "at": dram("table_at", (NP, W3))}
        adst_table = dram("adst_table", (NP, HEADS))
        bound = {(o, w): dram(f"{w}_{o}", (HIGH, LOW)) for o in ("src", "dst") for w in ("start", "end")}

        x = sb("x", [P, KN * D])
        hrows = sb("hrows", [P, KN * W3])
        arena_a = sb("arena_a", [P, KN * W01])
        arena_b = sb("arena_b", [P, KN * W01])
        dst_i = sb("dst_i", [P, L + 1], i32)
        src_f = sb("src_f", [P, L + J])
        digits = {(o, w): sb(f"{w}_{o}", [P, L + J], bf16) for o in ("src", "dst") for w in ("hi", "lo")}
        same_dst = sb("same_dst", [P, L])
        decay = sb("decay", [P, L])
        iota_i = sb("iota_i", [P, P], i32)
        rowno_i = sb("rowno_i", [P, 1], i32)
        iota = sb("iota", [P, P])
        rowno = sb("rowno", [P, 1])
        rowno_l = sb("rowno_l", [P, 1])
        ident = sb("ident", [P, P])
        ident_b = sb("ident_b", [P, P], bf16)
        conv_rows = hrows[:, KN * HEADS:KN * HEADS + KN * D]
        before = sb("before", [P, P])
        after = sb("after", [P, P])
        ones = sb("ones", [P, P])
        zero_b = sb("zero_b", [P, P], bf16)
        base = sb("base", [HIGH, LOW])
        hist_sb = sb("hist_sb", [HIGH, LOW])
        ends_sb = sb("ends_sb", [HIGH, LOW])
        offs_sb = sb("offs_sb", [HIGH, 1])
        nstart = {o: sb(f"nstart_{o}", [P, KN]) for o in ("src", "dst")}
        nend = {o: sb(f"nend_{o}", [P, KN]) for o in ("src", "dst")}
        has = {o: sb(f"has_{o}", [P, KN]) for o in ("src", "dst")}
        end_i = {o: sb(f"end_i_{o}", [P, KN], i32) for o in ("src", "dst")}
        start_i = sb("start_i", [P, KN], i32)
        tmpk = sb("tmpk", [P, KN])
        degree = sb("degree", [P, KN])
        dinv = sb("dinv", [P, KN])
        flagrow = {o: sb(f"flagrow_{o}", [P, P]) for o in ("src", "dst")}
        flag = sb("flag", [P, 1])
        diag = sb("diag", [P, P])
        edge_ends = sb("edge_ends", [P, 3])
        chunk_end = sb("chunk_end", [P, W01])
        chunk_in_t = sb("chunk_in_t", [P, P + 1])
        chunk_max_t = sb("chunk_max_t", [P, P + 1])
        chunk_t1 = sb("chunk_t1", [P, P])
        chunk_t2 = sb("chunk_t2", [P, P])
        chunk_in = sb("chunk_in", [P, W01])
        first_src = sb("first_src", [P, 1], i32)
        first_end = {o: sb(f"first_end_{o}", [P, 1]) for o in ("src", "dst")}
        fix_from = {o: sb(f"fix_from_{o}", [P, 1], i32) for o in ("src", "dst")}
        fix_to = {o: sb(f"fix_to_{o}", [P, 1], i32) for o in ("src", "dst")}
        fix_tmp = sb("fix_tmp", [P, 2])
        fix_rows = sb("fix_rows", [P, W01])
        fix_exp = sb("fix_exp", [P, 2 * HEADS])
        stat1 = sb("stat1", [P, KN])
        stat2 = sb("stat2", [P, KN])
        w1 = sb("w1", [3 * E32, HID])
        w1u = sb("w1u", [HID, 1])
        b1 = sb("b1", [HID, 1])
        u0 = sb("u0", [HID, 1])
        w2 = sb("w2", [HID, D])
        b2 = sb("b2", [P, D])
        wc = {"c1": sb("wc1", [D, D]), "c2": sb("wc2", [D, D]), "at": sb("wnode", [D, D])}
        bcv = {"c1": sb("bc1", [P, D]), "c2": sb("bc2", [P, D])}
        wedge = sb("wedge", [P, E16 * HEADS])
        asrc_w = sb("asrc_w", [P, D])
        adst_w = sb("adst_w", [P, D])
        gamma = sb("gamma", [P, D])
        beta = sb("beta", [P, D])
        first_row = sb("first_row", [P, D])
        first_adst = sb("first_adst", [P, HEADS])
        mask_blk = sb("mask_blk", [P, 2, J])
        cap_blk = sb("cap_blk", [P, 2, J])
        idx_blk = [sb(f"idx_blk{h}", [P, J], i32) for h in range(2)]
        rank_blk = sb("rank_blk", [P, 2, J])
        sel_blk = sb("sel_blk", [P, 2, J])
        digit_blk = {w: [sb(f"digit_{w}{h}", [P, J], bf16) for h in range(2)] for w in ("hi", "lo")}
        src_blk = sb("src_blk", [P, 2, J])

        def carve(tensor, parts, dt=f32):
            at, got = 0, {}
            for name, size in parts:
                got[name] = tensor[:, at:at + size]
                at += size
            assert at <= tensor.shape[1], at
            return got

        cut = carve(arena_b, [("onehot", 2 * J * (LOW + HIGH) // 2), ("rows0", J * TW), ("rows1", J * TW),
                              ("xs0", J * D), ("xs1", J * D), ("xb0", J * D), ("xb1", J * D),
                              ("junk", 2 * P), ("hi_t", 2 * Q * P), ("snap", 2 * P)])
        oh = cut["onehot"].bitcast(bf16)
        oh_hi = [oh[:, h * J * (LOW + HIGH):][:, :J * HIGH].rearrange("p (n t) -> p n t", t=J) for h in range(2)]
        oh_lo = [oh[:, h * J * (LOW + HIGH) + J * HIGH:][:, :J * LOW].rearrange("p (n t) -> p n t", t=J)
                 for h in range(2)]
        rows = [cut[f"rows{h}"].rearrange("p (j f) -> p j f", f=TW) for h in range(2)]
        xs = [cut[f"xs{h}"].rearrange("p (j f) -> p j f", f=D) for h in range(2)]
        xb = [cut[f"xb{h}"].rearrange("p (j f) -> p j f", f=D) for h in range(2)]
        junk = [cut["junk"].bitcast(bf16)[:, q * P:(q + 1) * P] for q in range(4)]
        hi_t = [cut["hi_t"][0:HIGH, q * Q * P:(q + 1) * Q * P] for q in range(2)]
        snap = [cut["snap"][0:HIGH, q * P:(q + 1) * P] for q in range(2)]
        early = carve(arena_a, [("zeros", J * D), ("ih", J * HIGH // 2), ("il", J * LOW // 2)])
        zeros = early["zeros"]
        iota_hi = early["ih"].bitcast(bf16).rearrange("p (n t) -> p n t", t=J)
        iota_lo = early["il"].bitcast(bf16).rearrange("p (n t) -> p n t", t=J)
        late = carve(hrows, [(f"tb{h}", J * TW) for h in range(R)])
        tb = [late[f"tb{h}"].rearrange("p (j f) -> p j f", f=TW) for h in range(R)]
        late = carve(arena_a, [("st0", J * W01), ("st1", J * W01), ("g0", J * W3), ("g1", J * W3),
                               ("a16_0", J * E16), ("a16_1", J * E16), ("prod", J * HEADS * E16),
                               ("sc", J * HEADS), ("mx", (J + 1) * HEADS),
                               ("ex", J * HEADS), ("cf", J * W3), ("tmp", 2 * W3), ("lk", J * HEADS)])
        st = [late[f"st{h}"] for h in range(2)]
        gb = [late[f"g{h}"] for h in range(2)]
        a16 = [late[f"a16_{h}"].rearrange("p (j f) -> p j f", f=E16) for h in range(2)]

        bank = [ps(f"bank{n}", [P, 512]) for n in range(8)]
        hist = bank[0][0:HIGH, 0:LOW]
        p_hi_t = [bank[1][0:HIGH, :], bank[2][0:HIGH, :]]
        p_src = [bank[3], bank[4]]
        p_cnt = [bank[5], bank[6]]
        p_small = bank[7]

        S = {}

        def s(name):
            if name not in S:
                S[name] = sem(name)
            return S[name]

        mrep = chunk_max_t[:, 0:W3S]

        work = carve(arena_b, [("t0", GT * P), ("t1", GT * P), ("r", GT * P), ("g0", GT * 3 * E32),
                               ("g1", GT * 3 * E32), ("y", PK * D), ("s", PK * D), ("adst", KN * HEADS),
                               ("e", PK * HEADS)])

        block = ctx.enter_context(nc.Block())

        def rows_of(dram_ap, w):
            return dram_ap.rearrange("(p l) w -> p (l w)", p=P)

        def scattered(i, h):
            return i * (16 * J)

        def blk(i, h):
            return i * 2 + h

        @block.sync
        def _(sp):
            src_v = a["src"].rearrange("(p l) -> p l", p=P)
            dst_v = a["dst"].rearrange("(p l) -> p l", p=P)
            sp.dma_start(arena_b[:, 0:L].bitcast(i32), src_v).then_inc(s("src_loaded"), 16)
            sp.dma_start(dst_i[:, 1:L + 1], dst_v).then_inc(s("dst_loaded"), 16)
            sp.wait_ge(s("dst_col0"), 1)
            sp.dma_start(dst_i[1:P, 0:1], dst_v[0:P - 1, L - 1:L], allow_slow_non_contiguous=True).then_inc(s("dst_loaded"), 16)
            sp.dma_start(decay[:, :], a["w"].rearrange("(p l) -> p l", p=P)).then_inc(s("w_loaded"), 16)
            sp.dma_start(x[:, :], a["x"].rearrange("(p k) d -> p (k d)", p=P)).then_inc(s("x_loaded"), 16)
            sp.wait_ge(s("zeros_set"), 1)
            for r in range(0, L // J):
                if r % 14 == 0:
                    sp.dma_start(rows_of(x_at_start, D)[:, r * J * D:(r + 14) * J * D]
                                 .rearrange("p (n z) -> p n z", n=14),
                                 bf(zeros, 14)).then_inc(s("zeroed"), 16)
            sp.dma_start(rows_of(adst_at_start, HEADS).rearrange("p (n z) -> p n z", n=7),
                         bf(zeros[:, 0:L * HEADS // 7], 7)).then_inc(s("zeroed"), 16)
            def col(v):
                return v.rearrange("(n o) -> n o", o=1)

            def rep(v):
                return v.rearrange("(o n) -> o n", o=1).to_broadcast([P, v.shape[0]])

            wl = s("weights_loaded")
            sp.dma_start(w1[:, :], a["L1_W1"][0:3 * E32, :]).then_inc(wl, 16)
            sp.dma_start(w1u[:, :], a["L1_W1"][3 * E32:3 * E32 + 1, :].rearrange("o n -> n o"),
                         allow_slow_non_contiguous=True).then_inc(wl, 16)
            sp.dma_start(b1[:, :], col(a["L1_b1"])).then_inc(wl, 16)
            sp.dma_start(u0[:, :], a["u"][0:1, :].to_broadcast([HID, 1])).then_inc(wl, 16)
            sp.dma_start(w2[:, :], a["L1_W2"]).then_inc(wl, 16)
            sp.dma_start(b2[:, :], rep(a["L1_b2"])).then_inc(wl, 16)
            sp.dma_start(wc["c1"][:, :], a["L2_W1"]).then_inc(wl, 16)
            sp.dma_start(wc["c2"][:, :], a["L2_W2"]).then_inc(wl, 16)
            sp.dma_start(wc["at"][:, :], a["W_node"]).then_inc(wl, 16)
            sp.dma_start(bcv["c1"][:, :], rep(a["L2_b1"])).then_inc(wl, 16)
            sp.dma_start(bcv["c2"][:, :], rep(a["L2_b2"])).then_inc(wl, 16)
            sp.dma_start(wedge[:, :], rep(a["W_edge"].rearrange("a b -> (a b)"))).then_inc(wl, 16)
            sp.dma_start(asrc_w[:, :], rep(a["attn_src"].rearrange("a b -> (a b)"))).then_inc(wl, 16)
            sp.dma_start(adst_w[:, :], rep(a["attn_dst"].rearrange("a b -> (a b)"))).then_inc(wl, 16)
            sp.dma_start(gamma[:, :], rep(a["gamma"])).then_inc(wl, 16)
            sp.dma_start(beta[:, :], rep(a["beta"])).then_inc(wl, 16)
            for n, o in enumerate(("dst", "src")):
                sp.wait_ge(s("bounds_ready"), n + 1)
                sp.dma_start(bound[o, "start"], base[:, :] if o == "src" else diag[0:HIGH, :])\
                  .then_inc(s("bounds_out"), 16)
                sp.dma_start(bound[o, "end"], ends_sb[:, :]).then_inc(s("bounds_out"), 16)
                sp.wait_ge(s("bounds_out"), 32 * (n + 1))
                for t, w in ((nstart, "start"), (nend, "end")):
                    sp.dma_start(t[o][:, :], bound[o, w].rearrange("h l -> (h l)").rearrange("(p k) -> p k", p=P))\
                      .then_inc(s("bounds_in"), 16)
            sp.wait_ge(s("x_scattered"), 16 * KN)
            a32_v = a["a32"].rearrange("(p l) w -> p l w", p=P)

            def x_block(i, h):
                sp.dma_start(cut[f"xs{h}"], rows_of(x_at_start, D)[:, bass.ds(blk(i, h) * (J * D), J * D)])\
                  .then_inc(s(f"xs_in{h}"), 16)

            def body(i):
                for h in range(2):
                    if h == 0 or not (isinstance(i, int) and i == NB - 1):
                        if later(i) or h:
                            sp.wait_ge(s("rows_ready"), i * 2 + h)
                        x_block(*((i, 1) if h == 0 else (i + 1, 0)))
                    if later(i):
                        sp.wait_ge(s(f"scattered{h}"), scattered(i, h))
                    sp.dma_start(rows[h][:, :, D:D + E32], a32_v[:, bass.ds(blk(i, h) * J, J), :])\
                      .then_inc(s(f"a32_in{h}"), 16)

            x_block(0, 0)
            turns(sp, body, peel_last=True)
            for h in range(2):
                sp.wait_ge(s(f"scattered{h}"), scattered(NB, h))
            by_v = rows_of(by_src, TW)
            sp.dma_start(edge_ends[:, 1:2], by_v[:, TW - 1:TW], allow_slow_non_contiguous=True).then_inc(s("edge_ends_in"), 16)
            sp.dma_start(edge_ends[:, 2:3], by_v[:, L * TW - 1:L * TW], allow_slow_non_contiguous=True).then_inc(s("edge_ends_in"), 16)
            sp.dma_start(edge_ends[1:P, 0:1], by_v[0:P - 1, L * TW - 1:L * TW], allow_slow_non_contiguous=True).then_inc(s("edge_ends_in"), 16)

            def load(i, h):
                sp.dma_start(tb[h].rearrange("p j f -> p (j f)"),
                             by_v[:, bass.ds((i * R + h) * (J * TW), J * TW)]).then_inc(s(f"tb_in{h}"), 16)

            def body(i, blocks=R, more=True):
                for h in range(blocks):
                    if more:
                        if later(i) or h >= 2:
                            sp.wait_ge(s("state"), i * R + h - 1)
                        load(*((i, h + 2) if h < 2 else (i + 1, h - 2)))
                    if later(i) or h:
                        write_src(i * R + h - 1, (h - 1) % 2)

            def write_src(b, h):
                sp.wait_ge(s("state"), b + 1)
                sp.dma_start(rows_of(states["src"], W01)[:, bass.ds(b * (J * W01), J * W01)],
                             st[h][:, 0:J * W01]).then_inc(s(f"stored{h}"), 16)

            load(0, 0)
            load(0, 1)
            turns(sp, body, NB * 2 // R)
            body(NB * 2 // R, 2, more=False)
            write_src(NB * 2 - 1, 1)

            def store(i, h, g, w):
                pi, ph = (i, 0) if h else (i - 1, 1)
                if not later(i) and h == 0:
                    return
                write(pi, ph, g, w)

            def write(i, h, g, w):
                sp.wait_ge(s("state"), upto(g, "state") + i * 2 + h + 1)
                sp.dma_start(rows_of(states[g], w)[:, bass.ds(blk(i, h) * (J * w), J * w)],
                             st[h][:, 0:J * w]).then_inc(s(f"stored{h}"), 16)

            src_b = a["src"].rearrange("(p l) -> p l", p=P)
            a16_v = a["a16"].rearrange("(p l) w -> p (l w)", p=P)
            for g, w in (("c1", D), ("c2", D), ("at", W3S)):
                tw = W3 if g == "at" else D
                for p in range(len(PARTS)):
                    c0, c1 = columns(p)
                    sp.wait_ge(s("table"), upto(g, "table") + p + 1)
                    held = hrows if g == "at" else conv_rows
                    sp.dma_start(table[g].rearrange("(p k) w -> p k w", p=P)[:, c0:c1, :],
                                 held[:, c0 * tw:c1 * tw].rearrange("p (k w) -> p k w", w=tw))\
                      .then_inc(s("table_out"), 16)
                if g == "at":
                    sp.dma_start(adst_table.rearrange("(p k) w -> p (k w)", p=P), work["adst"])\
                      .then_inc(s("adst_table_out"), 16)
                    sp.wait_ge(s("adst_scattered"), 16 * KN)
                    sp.dma_start(arena_b[:, 0:L * HEADS], rows_of(adst_at_start, HEADS))\
                      .then_inc(s("adst_in"), 16)

                def body(i):
                    for h in range(2):
                        if later(i):
                            sp.wait_ge(s(f"gathered{h}"), upto(g, f"gathered{h}") + i * (16 * J))
                        sp.dma_start(idx_blk[h][:, :], src_b[:, bass.ds(blk(i, h) * J, J)])\
                          .then_inc(s(f"idx{h}"), 16)
                        if g == "at":
                            if later(i):
                                sp.wait_ge(s("state"), upto("at", "state") + i * 2 + h - 1)
                            sp.dma_start(a16[h].rearrange("p j f -> p (j f)"),
                                         a16_v[:, bass.ds(blk(i, h) * (J * E16), J * E16)])\
                              .then_inc(s(f"a16_in{h}"), 16)
                        store(i, h, g, w)

                turns(sp, body)
                write(NB - 1, 1, g, w)
            for p in range(len(PARTS)):
                c0, c1 = columns(p)
                sp.wait_ge(s("final"), p + 1)
                sp.dma_start(out.rearrange("(p k) d -> p k d", p=P)[:, c0:c1, :],
                             x[:, c0 * D:c1 * D].rearrange("p (k d) -> p k d", d=D)).then_inc(s("out_done"), 16)
            sp.wait_ge(s("out_done"), 16 * len(PARTS))

        @block.gpsimd
        def _(pool):
            pool.memset(dst_i[:, 0:1], -1).then_inc(s("dst_col0"), 1)
            pool.memset(zeros, 0.0).then_inc(s("zeros_set"), 1)
            pool.iota(iota_i[:, :], pattern=[[1, P]], base=0, channel_multiplier=0).then_inc(s("iotas"), 1)
            pool.iota(rowno_i[:, :], pattern=[[0, 1]], base=0, channel_multiplier=1).then_inc(s("iotas"), 1)
            pool.wait_ge(s("zeroed"), 16 * (NB * 2 // 14 + 1))
            pool.wait_ge(s("x_loaded"), 16)
            pool.wait_ge(s("node_index"), 1)
            for k in range(KN):
                pool.indirect_dma_start(out=x_at_start, out_offset=AT(ap=start_i[:, k:k + 1], axis=0),
                                        in_=x[:, k * D:(k + 1) * D], in_offset=None,
                                        bounds_check=EP - 1, oob_is_err=False).then_inc(s("x_scattered"), 16)
            pool.indirect_dma_start(out=first_row[:, :], out_offset=None, in_=a["x"],
                                    in_offset=AT(ap=dst_i[:, 1:2], axis=0)).then_inc(s("first_row_in"), 16)

            def first_ends(o, ids):
                pool.indirect_dma_start(out=first_end[o][:, :], out_offset=None,
                                        in_=bound[o, "end"].rearrange("h (l o) -> (h l) o", o=1),
                                        in_offset=AT(ap=ids, axis=0)).then_inc(s(f"first_end_{o}"), 16)

            first_ends("dst", dst_i[:, 1:2])

            def body(i):
                for h in range(2):
                    pool.wait_ge(s("rows_ready"), i * 2 + h + 1)
                    pool.wait_ge(s(f"a32_in{h}"), i * 16 + 16)
                    pool.sem_inc(s("pool_begun"), 1)
                    for k in range(J):
                        pool.indirect_dma_start(out=by_src, out_offset=AT(ap=idx_blk[h][:, k:k + 1], axis=0),
                                                in_=rows[h][:, k, :], in_offset=None)\
                            .then_inc(s(f"scattered{h}"), 16)

            turns(pool, body)

            def node_states(g, w, o):
                for h in range(2):
                    pool.wait_ge(s(f"stored{h}"), upto(g, f"stored{h}") + 16 * NB)
                pool.indirect_dma_start(out=fix_rows[:, 0:w], out_offset=None, in_=states[g],
                                        in_offset=AT(ap=fix_from[o][:, 0:1], axis=0)).then_inc(s("fix_in"), 16)
                pool.wait_ge(s("chunk_end"), upto(g, "chunk_end") + 1)
                pool.wait_ge(s("fixed"), upto(g, "fixed") + 1)
                pool.indirect_dma_start(out=states[g], out_offset=AT(ap=fix_to[o][:, 0:1], axis=0),
                                        in_=fix_rows[:, 0:w], in_offset=None,
                                        bounds_check=EP - 1, oob_is_err=False).then_inc(s("fix_out"), 16)
                pool.wait_ge(s("fix_out"), upto(g, "fix_out") + 16)
                for p in range(len(PARTS)):
                    for k in range(*columns(p)):
                        pool.indirect_dma_start(out=arena_a[:, k * w:(k + 1) * w], out_offset=None, in_=states[g],
                                                in_offset=AT(ap=end_i[o][:, k:k + 1], axis=0))\
                            .then_inc(s(f"nodes_in{p}"), 16)

            pool.wait_ge(s("fix_index"), 1)
            pool.wait_ge(s("first_src"), 1)
            first_ends("src", first_src[:, 0:1])
            pool.wait_ge(s("fix_index"), 2)
            node_states("src", W01, "src")
            for g, w in (("c1", D), ("c2", D), ("at", W3)):
                if g == "at":
                    for p in range(len(PARTS)):
                        pool.wait_ge(s("table"), upto("at", "table") + p + 1)
                        for k in range(*columns(p)):
                            pool.indirect_dma_start(out=adst_at_start, out_offset=AT(ap=start_i[:, k:k + 1], axis=0),
                                                    in_=work["adst"][:, k * HEADS:(k + 1) * HEADS], in_offset=None,
                                                    bounds_check=EP - 1, oob_is_err=False)\
                                .then_inc(s("adst_scattered"), 16)
                    pool.wait_ge(s("adst_table_out"), 16)
                    pool.indirect_dma_start(out=first_adst[:, :], out_offset=None, in_=adst_table,
                                            in_offset=AT(ap=dst_i[:, 1:2], axis=0))\
                        .then_inc(s("first_adst_in"), 16)

                pool.wait_ge(s("table_out"), upto(g, "table_out") + 16 * len(PARTS))

                def body(i):
                    for h in range(2):
                        pool.wait_ge(s(f"idx{h}"), upto(g, f"idx{h}") + i * 16 + 16)
                        if later(i):
                            pool.wait_ge(s("state"), upto(g, "state") + i * 2 + h - 1)
                        pool.sem_inc(s("pool_begun"), 1)
                        for k in range(J):
                            pool.indirect_dma_start(out=gb[h][:, k * w:(k + 1) * w], out_offset=None,
                                                    in_=table[g], in_offset=AT(ap=idx_blk[h][:, k:k + 1], axis=0))\
                                .then_inc(s(f"gathered{h}"), 16)

                turns(pool, body)
                node_states(g, W3S if g == "at" else D, "dst")

        roots = [0]

        def rstd(act, p):
            c0, c1 = columns(p)
            roots[0] += 1
            act.wait_ge(s("var"), roots[0])
            act.activation(stat2[:, c0:c1], stat2[:, c0:c1], ACT.Sqrt).then_inc(s("root"), 1)

        def turned_act(act, g, p, n, i, h):
            act.wait_ge(s("turned"), i * 2 + (groups_before(g, p) + h + 1))
            act.activation(work[f"t{h}"][0:n, 0:512], bank[1][0:n, :], ACT.Copy).then_inc(s("group_t"), 1)
            act.activation(work[f"t{h}"][0:n, 512:GT * P], bank[2][0:n, 0:GT * P - 512], ACT.Copy)\
               .then_inc(s("group_t"), 1)

        def mlp_act(act, p):
            def body(i, last):
                for h in range(2):
                    turned_act(act, "mlp", p, 3 * E32, i, h)
                    act.wait_ge(s("mlp_hid"), i * 2 + h + 1)
                    act.activation(work["r"][:, 0:512], bank[3][:, :], ACT.Relu, bias=b1[:, 0:1])\
                       .then_inc(s("mlp_r"), 1)
                    act.activation(work["r"][:, 512:GT * P], bank[4][:, 0:GT * P - 512], ACT.Relu, bias=b1[:, 0:1])\
                       .then_inc(s("mlp_r"), 1)

            act.wait_ge(s("b1_ready"), 1)
            part_turns(act, body, p)

        def dense_act(act, g, p):
            def body(i, last):
                for h in range(2):
                    turned_act(act, g, p, D, i, h)

            part_turns(act, body, p)

        def attention_act(act):
            def body(i):
                for h in range(2):
                    act.wait_ge(s("at_args"), i * 2 + h + 1)
                    act.activation(late["ex"], late["ex"], ACT.Exp).then_inc(s("at_exp"), 1)
                    act.activation(late["lk"], late["lk"], ACT.Exp).then_inc(s("at_exp"), 1)

            turns(act, body)
            act.wait_ge(s("at_chunk_args"), 1)
            act.activation(chunk_t1[0:W3S, :], chunk_t1[0:W3S, :], ACT.Exp).then_inc(s("at_chunk_exp"), 1)
            act.activation(chunk_t2[0:W3S, :], chunk_t2[0:W3S, :], ACT.Exp).then_inc(s("at_chunk_exp"), 1)
            act.wait_ge(s("at_fix_args"), 1)
            act.activation(fix_exp[:, :], fix_exp[:, :], ACT.Exp).then_inc(s("at_fix_exp"), 1)

        @block.scalar
        def _(act):
            act.wait_ge(s("w_loaded"), 16)
            act.activation(decay[:, :], decay[:, :], ACT.Exp, scale=-1.0).then_inc(s("decay_ready"), 1)

            def turned(g, q):
                act.wait_ge(s("tile_turned"), g + 1)
                act.activation(hi_t[q], p_hi_t[q], ACT.Copy).then_inc(s("hi_t_ready"), 1)

            def body(i):
                for h in range(2):
                    for k in range(J):
                        act.wait_ge(s("hist_added"), i * (2 * J) + h * J + k + 1)
                        act.activation(snap[k % 2], hist, ACT.Copy).then_inc(s("snap_ready"), 1)
                        if k % Q == 2:
                            turned(i * (2 * J // Q) + h * (J // Q) + k // Q + 1, (k // Q + 1) % 2)

            turned(0, 0)
            turns(act, body)

            act.wait_ge(s("degree_ready"), 1)
            act.activation(dinv[:, :], degree[:, :], ACT.Sqrt).then_inc(s("dinv_root"), 1)
            for p in range(len(PARTS)):
                rstd(act, p)
                mlp_act(act, p)
                rstd(act, p)
                dense_act(act, "c1", p)
            for p in range(len(PARTS)):
                dense_act(act, "c2", p)
            for p in range(len(PARTS)):
                rstd(act, p)
                dense_act(act, "at", p)
            attention_act(act)
            for p in range(len(PARTS)):
                rstd(act, p)
                rstd(act, p)

        @block.tensor
        def _(pe):
            for n, o in enumerate(("dst", "src")):
                if n == 0:
                    pe.wait_ge(s("consts"), 1)
                else:
                    pe.wait_ge(s("hist_read"), 1)
                pe.matmul(hist, zero_b[:, 0:HIGH], zero_b[:, 0:LOW], start=True, stop=False)

                def body(i):
                    for h in range(2):
                        pe.wait_ge(s("onehots"), upto(o, "onehots") + i * 2 + h + 1)
                        for k in range(J):
                            last = pe.matmul(hist, oh_hi[h][:, :, k], oh_lo[h][:, :, k], start=False, stop=False)
                        last.then_inc(s("onehots_used"), 1)

                turns(pe, body)
                pe.matmul(hist, zero_b[:, 0:HIGH], zero_b[:, 0:LOW], start=False, stop=True)\
                  .then_inc(s("hist_ready"), 1)
                pe.wait_ge(s("row_totals"), n + 1)
                pe.matmul(p_small[0:HIGH, 0:1], after[0:HIGH, 0:HIGH], ends_sb[:, LOW - 1:LOW], start=True,
                          stop=True).then_inc(s("row_offsets"), 1)
                if o == "dst":
                    pe.wait_ge(s("flag"), 1)
                    pe.matmul(p_small[:, 128:256], ones[:, :], diag[:, :], start=True, stop=True)\
                      .then_inc(s("flagrow"), 1)
            pe.wait_ge(s("base_ready"), 1)
            pe.matmul(hist, ident[0:HIGH, 0:HIGH], base[:, :], start=True, stop=True).then_inc(s("hist_added"), 1)

            def turn(h, k):
                q, at = k // Q % 2, slice(k % Q * P, (k % Q + 1) * P)
                turned = pe.matmul(p_hi_t[q][:, at], oh_hi[h][:, :, k], ident_b[:, :], start=True, stop=True)
                for n, w in enumerate(("hi", "lo")):
                    spread = pe.matmul(p_src[q][:, at], digit_blk[w][h][:, k:k + 1].to_broadcast([P, P]),
                                       ident_b[:, :], start=(n == 0), stop=(n == 1))
                if k % Q == Q - 1:
                    turned.then_inc(s("tile_turned"), 1)
                    spread.then_inc(s("src_spread"), 1)

            def body(i):
                for h in range(2):
                    for k in range(J):
                        t = i * (2 * J) + h * J + k
                        g = i * (2 * J // Q) + h * (J // Q) + k // Q
                        pe.wait_ge(s("snap_ready"), t + 1)
                        pe.matmul(hist, oh_hi[h][:, :, k], oh_lo[h][:, :, k], start=False, stop=True,
                                  skip_group_check=True).then_inc(s("hist_added"), 1)
                        if k % Q == 0:
                            pe.wait_ge(s("hi_t_ready"), g + 1)
                            if later(i) or h or k >= 2 * Q:
                                pe.wait_ge(s("selected"), (g - 1) * Q)
                        at = slice(k % Q * P, (k % Q + 1) * P)
                        last = pe.matmul(p_cnt[k // Q % 2][:, at], hi_t[k // Q % 2][:, at], snap[k % 2],
                                         start=True, stop=True)
                        if k % Q == Q - 1:
                            last.then_inc(s("counted"), 1)
                        nh, nk = (h, k // Q * Q + Q) if k < J - Q else (1 - h, 0)
                        if k % Q == 0:
                            if nk == 0:
                                pe.wait_ge(s("tile_onehots"), i * 2 + h + 2)
                            if later(i) or h or k:
                                pe.wait_ge(s("ranked"), g)
                            turn(nh, nk)
                            turn(nh, nk + 1)
                        if k % Q == 1:
                            turn(nh, nk + 2)
                            turn(nh, nk + 3)

            pe.wait_ge(s("tile_onehots"), 1)
            for k in range(Q):
                turn(0, k)
            turns(pe, body)

            def flagrow_src():
                pe.wait_ge(s("flag"), upto("src", "flag") + 1)
                pe.matmul(p_small[:, 128:256], ones[:, :], diag[:, :], start=True, stop=True)\
                  .then_inc(s("flagrow"), 1)

            def carries(g, w):
                pe.wait_ge(s("chunk_end"), upto(g, "chunk_end") + 1)
                if g == "src":
                    flagrow_src()
                pe.matmul(p_small[0:w, 0:P], chunk_end[:, 0:w], ident[:, :], start=True, stop=True)\
                  .then_inc(s("end_t"), 1)
                if g == "at":
                    pe.matmul(p_small[0:w, 256:384], mrep, ident[:, :], start=True, stop=True)\
                      .then_inc(s("end_t"), 1)
                pe.wait_ge(s("carry_t"), upto(g, "carry_t") + 1)
                pe.matmul(p_small[:, 384:384 + w], chunk_in_t[0:w, 0:P], ident[0:w, 0:w], start=True, stop=True)\
                  .then_inc(s("carry"), 1)
                if g == "at":
                    pe.matmul(p_small[:, 0:w], chunk_max_t[0:w, 0:P], ident[0:w, 0:w], start=True, stop=True)\
                      .then_inc(s("carry"), 1)

            def dense(g, p, n, w):
                before_g = groups_before(g, p)

                def turn_group(i, h):
                    pe.wait_ge(s("grp"), i * 2 + (before_g + h + 1))
                    for t in range(GT):
                        b = bank[1 + t // 4]
                        last = pe.matmul(b[0:n, (t % 4) * P:(t % 4 + 1) * P], work[f"g{h}"][:, t * n:(t + 1) * n],
                                         ident[:, :], start=True, stop=True)
                    last.then_inc(s("turned"), 1)

                def body(i, last_turn):
                    for h in range(2):
                        pe.wait_ge(s("group_t"), i * 4 + (before_g * 2 + h * 2 + 2))
                        turned = work[f"t{h}"]
                        if g == "mlp":
                            pe.matmul(bank[3][:, :], w1[:, :], turned[0:n, 0:512], start=True, stop=True)
                            pe.matmul(bank[4][:, 0:GT * P - 512], w1[:, :], turned[0:n, 512:GT * P], start=True,
                                      stop=True).then_inc(s("mlp_hid"), 1)
                        if h == 0:
                            turn_group(i, 1)
                        elif not last_turn:
                            turn_group(i + 1, 0)
                        if g == "mlp":
                            pe.wait_ge(s("mlp_r"), i * 4 + h * 2 + 2)
                        if later(i):
                            pe.wait_ge(s("out_read"), i * 2 + (before_g + h - 1))
                        rows_t = work["r"] if g == "mlp" else turned[0:n, :]
                        for t in range(GT):
                            last = pe.matmul(bank[5 + h][:, t * D:(t + 1) * D], rows_t[:, t * P:(t + 1) * P], w[:, :],
                                             start=True, stop=True)
                        last.then_inc(s("prod"), 1)

                turn_group(PARTS[p][0] // 2, 0)
                part_turns(pe, body, p)

            carries("src", W01)
            pe.wait_ge(s("weights_loaded"), 16 * 16)
            for p in range(len(PARTS)):
                dense("mlp", p, 3 * E32, w2)
                dense("c1", p, D, wc["c1"])
            carries("c1", D)
            for p in range(len(PARTS)):
                dense("c2", p, D, wc["c2"])
            carries("c2", D)
            for p in range(len(PARTS)):
                dense("at", p, D, wc["at"])
            carries("at", W3S)

        @block.vector
        def _(v):
            chain = [0]

            def link(ins):
                chain[0] += 1
                ins.then_inc(s("v_chain"), 1)
                v.wait_ge(s("v_chain"), chain[0])

            def tell(name, n=1):
                v.sem_inc(s(name), n)

            v.wait_ge(s("iotas"), 2)
            link(v.tensor_copy(iota[:, :], iota_i[:, :]))
            link(v.tensor_copy(rowno[:, :], rowno_i[:, :]))
            link(v.tensor_scalar(rowno_l[:, :], rowno[:, :], float(L), None, ALU.mult))
            link(v.tensor_scalar(ident[:, :], iota[:, :], rowno[:, 0:1], None, ALU.is_equal))
            link(v.tensor_copy(ident_b[:, :], ident[:, :]))
            link(v.tensor_scalar(before[:, :], iota[:, :], rowno[:, 0:1], None, ALU.is_lt))
            link(v.tensor_scalar(after[:, :], iota[:, :], rowno[:, 0:1], None, ALU.is_gt))
            link(v.memset(ones[:, :], 1.0))
            link(v.tensor_copy(iota_lo, bc(iota[:, 0:LOW], J)))
            link(v.tensor_scalar(iota_hi, bc(iota[:, 0:HIGH], J), float(LOW), None, ALU.mult))
            link(v.memset(edge_ends[:, 0:1], -1.0))
            link(v.memset(zero_b[:, :], 0.0))
            tell("consts")
            v.wait_ge(s("src_loaded"), 16)
            v.wait_ge(s("dst_loaded"), 32)
            src_i = arena_b[:, 0:L].bitcast(i32)
            t_i = arena_b[:, L:2 * L].bitcast(i32)
            for o, ids in (("dst", dst_i[:, 1:L + 1]), ("src", src_i)):
                link(v.tensor_scalar(t_i, ids, LOW - 1, None, ALU.bitwise_and))
                link(v.tensor_copy(digits[o, "lo"][:, 0:L], t_i))
                link(v.tensor_scalar(t_i, ids, -LOW, None, ALU.bitwise_and))
                link(v.tensor_copy(digits[o, "hi"][:, 0:L], t_i))
                for w in ("hi", "lo"):
                    link(v.memset(digits[o, w][:, L:L + J], 0.0))
            link(v.memset(src_f[:, L:L + J], 0.0))
            link(v.tensor_copy(src_f[:, 0:L], src_i))
            link(v.tensor_tensor(same_dst[:, :], dst_i[:, 1:L + 1], dst_i[:, 0:L], ALU.is_equal))
            def of_nodes(o):
                link(v.tensor_tensor(has[o][:, :], nend[o][:, :], nstart[o][:, :], ALU.is_gt))
                link(v.tensor_scalar(tmpk[:, :], nend[o][:, :], -1.0, 0.0, ALU.add, ALU.max))
                link(v.tensor_copy(end_i[o][:, :], tmpk[:, :]))

            def fix_index(o, continues):
                v.wait_ge(s(f"first_end_{o}"), 16)
                end, inside = fix_tmp[:, 0:1], fix_tmp[:, 1:2]
                link(v.tensor_scalar(end, first_end[o][:, :], -1.0, None, ALU.add))
                link(v.tensor_copy(fix_from[o][:, :], end))
                link(v.tensor_tensor(inside, end, rowno_l[:, :], ALU.subtract))
                link(v.tensor_scalar(inside, inside, float(L), None, ALU.is_lt))
                link(v.tensor_tensor(inside, inside, continues, ALU.mult))
                link(v.tensor_scalar(inside, inside, -NOWHERE, NOWHERE, ALU.mult, ALU.add))
                link(v.tensor_tensor(inside, inside, end, ALU.add))
                link(v.tensor_copy(fix_to[o][:, :], inside))
                tell("fix_index")

            def of_dst():
                link(v.tensor_tensor(degree[:, :], nend["dst"][:, :], nstart["dst"][:, :], ALU.subtract))
                link(v.tensor_scalar(degree[:, :], degree[:, :], 1.0, None, ALU.add))
                tell("degree_ready")
                link(v.tensor_scalar(tmpk[:, :], has["dst"][:, :], -NOWHERE, NOWHERE, ALU.mult, ALU.add))
                link(v.tensor_tensor(tmpk[:, :], tmpk[:, :], nstart["dst"][:, :], ALU.add))
                link(v.tensor_copy(start_i[:, :], tmpk[:, :]))
                tell("node_index")
                link(v.tensor_tensor(flag[:, :], dst_i[:, 1:2], dst_i[:, L:L + 1], ALU.is_equal))
                link(v.tensor_tensor(flag[:, :], flag[:, :], same_dst[:, 0:1], ALU.mult))
                v.wait_ge(s("bounds_out"), 32)
                link(v.tensor_scalar(diag[:, :], ident[:, :], flag[:, 0:1], None, ALU.mult))
                tell("flag")
                v.wait_ge(s("flagrow"), upto("dst", "flagrow") + 1)
                link(v.tensor_copy(flagrow["dst"][:, :], p_small[:, 128:256]))

            for n, o in enumerate(("dst", "src")):
                def body(i):
                    for h in range(2):
                        if later(i):
                            v.wait_ge(s("onehots_used"), upto(o, "onehots_used") + i * 2 + h - 1)
                        elif n:
                            v.wait_ge(s("onehots_used"), NB * 2)
                        at = bass.ds(blk(i, h) * J, J)
                        v.tensor_tensor(oh_hi[h], iota_hi, bf(digits[o, "hi"][:, at], HIGH), ALU.is_equal)
                        v.tensor_tensor(oh_lo[h], iota_lo, bf(digits[o, "lo"][:, at], LOW), ALU.is_equal)\
                            .then_inc(s("onehots"), 1)

                turns(v, body)
                v.wait_ge(s("hist_ready"), n + 1)
                if n:
                    v.wait_ge(s("bounds_out"), 32)
                link(v.tensor_copy(hist_sb[:, :], hist))
                tell("hist_read")
                link(v.tensor_tensor_scan(ends_sb[:, :], ones[0:HIGH, 0:LOW], hist_sb[:, :], 0.0, ALU.mult, ALU.add))
                tell("row_totals")
                v.wait_ge(s("row_offsets"), n + 1)
                link(v.tensor_copy(offs_sb[:, :], p_small[0:HIGH, 0:1]))
                link(v.tensor_scalar(ends_sb[:, :], ends_sb[:, :], offs_sb[:, 0:1], None, ALU.add))
                starts = base if o == "src" else diag
                link(v.tensor_tensor(starts[0:HIGH, :], ends_sb[:, :], hist_sb[:, :], ALU.subtract))
                tell("bounds_ready")
                v.wait_ge(s("bounds_in"), 32 * (n + 1))
                of_nodes(o)
                if o == "dst":
                    of_dst()
            tell("base_ready")

            def digits_of(i, h, done):
                at = bass.ds(blk(i, h) * J, J)
                done(v.tensor_copy(digit_blk["hi"][h][:, :], digits["src", "hi"][:, at]))
                done(v.tensor_copy(digit_blk["lo"][h][:, :], digits["src", "lo"][:, at]))
                return done(v.tensor_copy(src_blk[:, h, :], src_f[:, at]))

            def onehots_of(i, h):
                v.tensor_tensor(oh_hi[h], iota_hi, bf(digit_blk["hi"][h][:, :], HIGH), ALU.is_equal)
                v.tensor_tensor(oh_lo[h], iota_lo, bf(digit_blk["lo"][h][:, :], LOW), ALU.is_equal)\
                    .then_inc(s("tile_onehots"), 1)

            v.wait_ge(s("onehots_used"), 2 * NB * 2)
            digits_of(0, 0, link)
            onehots_of(0, 0)
            v.wait_ge(s("decay_ready"), 1)
            v.wait_ge(s("first_row_in"), 16)
            v.wait_ge(s("tile_onehots"), 1)
            c = Steps(s("v_tiles"), 2 * (J + 4))

            def stage_a(i, h, quad, xk):
                for k in range(quad * Q, quad * Q + Q):
                    if k:
                        old = xb[h][:, k - 1, :]
                    elif not later(i) and h == 0:
                        old = first_row[:, :]
                    else:
                        old = xb[1 - h][:, J - 1, :]
                    v.wait_ge(c.sem, c.value(xk))
                    xk = c.done(v.scalar_tensor_tensor(out=xb[h][:, k, :], in0=old, scalar=mask_blk[:, h, k:k + 1],
                                                       in1=xs[h][:, k, :], op0=ALU.mult, op1=ALU.add))
                    if k % Q == 0:
                        v.wait_ge(s("src_spread"), i * (2 * J // Q) + h * (J // Q) + quad + 1)
                    rank = v.scalar_tensor_tensor(out=junk[k % 2], in0=p_src[quad % 2][:, k % Q * P:(k % Q + 1) * P],
                                                  scalar=src_blk[:, h, k:k + 1], in1=before[:, :],
                                                  op0=ALU.is_equal, op1=ALU.mult, accum_out=rank_blk[:, h, k:k + 1])
                rank.then_inc(s("ranked"), 1)
                return xk

            def stage_b(i, h, quad):
                group = i * (2 * J // Q) + h * (J // Q) + quad
                v.wait_ge(s("counted"), group + 1)
                for k in range(quad * Q, quad * Q + Q):
                    place = v.scalar_tensor_tensor(out=junk[2 + k % 2], in0=p_cnt[quad % 2][:, k % Q * P:(k % Q + 1) * P],
                                                   scalar=1.0, in1=oh_lo[h][:, :, k], op0=ALU.mult, op1=ALU.mult,
                                                   accum_out=sel_blk[:, h, k:k + 1])
                    place.then_inc(s("selected"), 1)
                    if k % 2:
                        v.wait_ge(s("selected"), group * Q + k % Q + 1)
                if quad == J // Q - 1:
                    at = bass.ds(blk(i, h) * J, J)
                    if later(i):
                        v.wait_ge(s(f"scattered{h}"), scattered(i, h))
                    v.tensor_tensor(rows[h][:, :, 0:D], xb[h], bc(decay[:, at], D), ALU.mult)
                    v.tensor_copy(rows[h][:, :, TW - 1:TW], bc(src_blk[:, h, :], 1))
                    v.tensor_tensor(idx_blk[h][:, :], rank_blk[:, h, :], sel_blk[:, h, :], ALU.add)\
                        .then_inc(s("rows_ready"), 1)

            def body(i):
                c.turn(i)
                for h in range(2):
                    xk = c.done(v.tensor_copy(mask_blk[:, h, :], same_dst[:, bass.ds(blk(i, h) * J, J)]))
                    v.wait_ge(s(f"xs_in{h}"), i * 16 + 16)
                    for quad in range(J // Q):
                        xk = stage_a(i, h, quad, xk)
                        if quad:
                            stage_b(i, h, quad - 1)
                        elif h:
                            stage_b(i, 0, J // Q - 1)
                        elif later(i):
                            stage_b(i - 1, 1, J // Q - 1)
                        if quad == 1:
                            ni, nh = (i, 1) if h == 0 else (i + 1, 0)
                            if later(i) or h:
                                v.wait_ge(s("hist_added"), (i * 2 + h) * J + 1)
                            v.wait_ge(c.sem, c.value(digits_of(ni, nh, c.done)))
                            onehots_of(ni, nh)
                assert c.k == c.per, (c.k, c.per)

            turns(v, body, peel=2)
            stage_b(NB - 1, 1, J // Q - 1)

            v.wait_ge(s("rows_ready"), NB * 2)
            fix_index("dst", same_dst[:, 0:1])
            v.wait_ge(s("edge_ends_in"), 48)
            link(v.tensor_copy(first_src[:, :], edge_ends[:, 1:2]))
            tell("first_src")
            link(v.memset(chunk_end[:, 0:D + E32], 0.0))
            link(v.memset(chunk_end[:, D + E32:W01], -HUGE))
            c2 = Steps(s("v_src"), R * (4 + 2 * J - 1))
            WS = D + E32

            def same_src(h, before_block):
                ids, q = tb[h][:, :, TW - 1], h % 2
                return (v.tensor_tensor(mask_blk[:, q, 0:1], ids[:, 0:1], before_block, ALU.is_equal),
                        v.tensor_tensor(mask_blk[:, q, 1:J], ids[:, 1:J], ids[:, 0:J - 1], ALU.is_equal))

            def caps(h, step):
                if step == 0:
                    return v.tensor_scalar(cap_blk[:, h, :], mask_blk[:, h, :], 2.0, -1.0, ALU.mult, ALU.add)
                return v.tensor_scalar(cap_blk[:, h, :], cap_blk[:, h, :], HUGE, None, ALU.mult)

            v.wait_ge(s("tb_in0"), 16)
            for ins in same_src(0, edge_ends[:, 0:1]):
                link(ins)
            link(caps(0, 0))
            link(caps(0, 1))

            def body(i, blocks=R):
                c2.turn(i)
                for h in range(blocks):
                    q = h % 2
                    more = blocks == R or h < blocks - 1
                    if later(i) or h >= 2:
                        v.wait_ge(s(f"stored{q}"), i * (16 * R // 2) + 16 * (h // 2))
                    if later(i) or h:
                        v.wait_ge(s("state"), i * R + h)
                    for k in range(J):
                        new = st[q][:, k * W01:(k + 1) * W01]
                        if k:
                            old = st[q][:, (k - 1) * W01:k * W01]
                        elif not later(i) and h == 0:
                            old = chunk_end[:, :]
                        else:
                            old = st[1 - q][:, (J - 1) * W01:J * W01]
                        n = (h + 1) % R
                        if k == J // 2 and more:
                            v.wait_ge(s(f"tb_in{n}"), (i + (h + 1) // R) * 16 + 16)
                            for m in same_src(n, tb[h][:, J - 1, TW - 1:TW]):
                                mc = c2.done(m)
                        if k in (J // 2 + 2, J // 2 + 4) and more:
                            v.wait_ge(c2.sem, c2.value(mc))
                            mc = c2.done(caps(n % 2, (k - J // 2) // 4))
                        if k:
                            v.wait_ge(c2.sem, c2.value(xk))
                        xk = c2.done(v.scalar_tensor_tensor(out=new[:, 0:WS], in0=old[:, 0:WS],
                                                            scalar=mask_blk[:, q, k:k + 1],
                                                            in1=tb[h][:, k, 0:WS], op0=ALU.mult, op1=ALU.add))
                        if k:
                            v.wait_ge(c2.sem, c2.value(mk))
                        ins = v.scalar_tensor_tensor(out=new[:, WS:W01], in0=old[:, WS:W01],
                                                     scalar=cap_blk[:, q, k:k + 1],
                                                     in1=tb[h][:, k, D:WS], op0=ALU.min, op1=ALU.max)
                        if k < J - 1:
                            mk = c2.done(ins)
                        else:
                            ins.then_inc(s("state"), 1)
                assert blocks < R or c2.k == c2.per, (c2.k, c2.per)

            turns(v, body, NB * 2 // R)
            body(NB * 2 // R, 2)

            def chunk_ends(g, w):
                v.wait_ge(s("state"), upto(g, "state") + NB * 2)
                link(v.tensor_copy(chunk_end[:, 0:w], st[1][:, (J - 1) * w:J * w]))

            chunk_ends("src", W01)
            link(v.tensor_tensor(flag[:, :], edge_ends[:, 1:2], edge_ends[:, 2:3], ALU.is_equal))
            link(v.tensor_tensor(edge_ends[:, 0:1], edge_ends[:, 0:1], edge_ends[:, 1:2], ALU.is_equal))
            link(v.tensor_tensor(flag[:, :], flag[:, :], edge_ends[:, 0:1], ALU.mult))
            fix_index("src", edge_ends[:, 0:1])
            link(v.tensor_scalar(diag[:, :], ident[:, :], flag[:, 0:1], None, ALU.mult))
            tell("flag")
            tell("chunk_end")
            v.wait_ge(s("flagrow"), upto("src", "flagrow") + 1)
            v.wait_ge(s("end_t"), upto("src", "end_t") + 1)
            link(v.tensor_copy(flagrow["src"][:, :], p_small[:, 128:256]))
            fr = flagrow["src"]
            link(v.memset(chunk_in_t[:, 0:1], 0.0))
            link(v.tensor_tensor_scan(chunk_in_t[0:WS, 1:P + 1], fr[0:WS, :], p_small[0:WS, 0:P], 0.0,
                                      ALU.mult, ALU.add))
            link(v.tensor_scalar(chunk_t1[WS:W01, :], fr[WS:W01, :], 2.0, -1.0, ALU.mult, ALU.add))
            link(v.tensor_scalar(chunk_t1[WS:W01, :], chunk_t1[WS:W01, :], HUGE, None, ALU.mult))
            link(v.tensor_tensor_scan(chunk_in_t[WS:W01, 1:P + 1], chunk_t1[WS:W01, :], p_small[WS:W01, 0:P], 0.0,
                                      ALU.min, ALU.max))
            tell("carry_t")
            v.wait_ge(s("carry"), upto("src", "carry") + 1)
            link(v.tensor_copy(chunk_in[:, :], p_small[:, 384:384 + W01]))

            v.wait_ge(s("fix_in"), 16)
            link(v.tensor_tensor(fix_rows[:, 0:WS], fix_rows[:, 0:WS], chunk_in[:, 0:WS], ALU.add))
            link(v.tensor_tensor(fix_rows[:, WS:W01], fix_rows[:, WS:W01], chunk_in[:, WS:W01], ALU.max))
            tell("fixed")

            def gathered(w, p):
                c0, c1 = columns(p)
                return arena_a[:, c0 * w:c1 * w].rearrange("p (k c) -> p k c", c=w)

            def part(t, p, w=D):
                c0, c1 = columns(p)
                return t[:, c0 * w:c1 * w].rearrange("p (k c) -> p k c", c=w)

            def local(name, p, w=D):
                c0, c1 = columns(p)
                return work[name][:, 0:(c1 - c0) * w].rearrange("p (k c) -> p k c", c=w)

            def per_node(t, p, n):
                c0, c1 = columns(p)
                return bc(t[:, c0:c1], n)

            def every(t, p):
                c0, c1 = columns(p)
                return bf(t[:, :], c1 - c0)

            norms = [0]

            def layer_norm(p, y3, z3):
                c0, c1 = columns(p)
                s3 = local("s", p)
                mean, var = stat1[:, c0:c1], stat2[:, c0:c1]
                link(v.tensor_reduce(mean, y3, AX.X, ALU.add))
                link(v.tensor_scalar(mean, mean, 1.0 / D, None, ALU.mult))
                link(v.tensor_tensor(z3, y3, bc(mean, D), ALU.subtract))
                link(v.tensor_tensor(s3, z3, z3, ALU.mult))
                link(v.tensor_reduce(var, s3, AX.X, ALU.add))
                link(v.tensor_scalar(var, var, 1.0 / D, 1e-5, ALU.mult, ALU.add))
                tell("var")
                norms[0] += 1
                v.wait_ge(s("root"), norms[0])
                link(v.reciprocal(var, var))
                link(v.tensor_tensor(z3, z3, bc(var, D), ALU.mult))

            v.wait_ge(s("weights_loaded"), 16 * 16)
            link(v.scalar_tensor_tensor(out=b1[:, :], in0=w1u[:, :], scalar=u0[:, 0:1], in1=b1[:, :],
                                        op0=ALU.mult, op1=ALU.add))
            tell("b1_ready")
            link(v.tensor_tensor(tmpk[:, :], nend["src"][:, :], nstart["src"][:, :], ALU.subtract))
            link(v.tensor_scalar(tmpk[:, :], tmpk[:, :], 1.0, None, ALU.max))
            link(v.reciprocal(tmpk[:, :], tmpk[:, :]))
            v.wait_ge(s("dinv_root"), 1)
            link(v.reciprocal(dinv[:, :], dinv[:, :]))

            def groups(g, p, fill, take):
                before_g = groups_before(g, p)

                def body(i, last_turn):
                    for h in range(2):
                        if h == 0:
                            fill(i * 2 + 1, 1)
                        elif not last_turn:
                            fill(i * 2 + 2, 0)
                        v.wait_ge(s("prod"), i * 2 + (before_g + h + 1))
                        take(i * 2 + h, bank[5 + h][:, 0:GT * D])

                fill(PARTS[p][0], 0)
                part_turns(v, body, p)
                v.wait_ge(s("out_read"), before_g + sum(PARTS[p]))

            def mlp(p):
                def fill(n, h):
                    src_rows = arena_a[:, bass.ds(n * (GT * W01), GT * W01)].rearrange("p (t c) -> p t c", c=W01)
                    hin = work[f"g{h}"].rearrange("p (t c) -> p t c", c=3 * E32)
                    v.tensor_copy(hin[:, :, 0:2 * E32], src_rows[:, :, D:W01])
                    v.tensor_tensor(hin[:, :, 2 * E32:], src_rows[:, :, D:D + E32],
                                    bc(tmpk[:, bass.ds(n * GT, GT)], E32), ALU.mult).then_inc(s("grp"), 1)

                def take(n, prod):
                    to = work["y"][:, bass.ds(n * (GT * D) - columns(p)[0] * D, GT * D)]
                    v.tensor_tensor(to, prod, x[:, bass.ds(n * (GT * D), GT * D)], ALU.add)\
                        .then_inc(s("out_read"), 1)

                groups("mlp", p, fill, take)
                link(v.tensor_tensor(local("y", p), local("y", p), every(b2, p), ALU.add))

            def dense(g, p, source):
                w, held = (W3, hrows) if g == "at" else (D, conv_rows)

                def fill(n, h):
                    v.tensor_copy(work[f"g{h}"][:, 0:GT * D], source[:, bass.ds(n * (GT * D), GT * D)])\
                        .then_inc(s("grp"), 1)

                def take(n, prod):
                    to = held[:, bass.ds(n * (GT * w), GT * w)].rearrange("p (t c) -> p t c", c=w)[:, :, 0:D]
                    prod = prod.rearrange("p (t c) -> p t c", c=D)
                    if g == "at":
                        ins = v.tensor_copy(to, prod)
                    else:
                        ins = v.tensor_tensor(to, prod, bc(dinv[:, bass.ds(n * GT, GT)], D), ALU.mult)
                    ins.then_inc(s("out_read"), 1)

                groups(g, p, fill, take)

            def nodes_in(g, p):
                c0, c1 = columns(p)
                v.wait_ge(s(f"nodes_in{p}"), (PASSES.index(g) + 1) * 16 * (c1 - c0))

            for p in range(len(PARTS)):
                nodes_in("src", p)
                got, xp = gathered(W01, p), part(x, p)
                link(v.tensor_tensor(got, got, per_node(has["src"], p, W01), ALU.mult))
                link(v.tensor_tensor(xp, xp, got[:, :, 0:D], ALU.add))
                layer_norm(p, xp, xp)
                mlp(p)
                layer_norm(p, local("y", p), xp)
                dense("c1", p, x)
                tell("table")

            def conv(g):
                link(v.memset(chunk_end[:, :], 0.0))
                cc = Steps(s("chain"), 2 * J, upto(g, "chain"))

                def body(i):
                    cc.turn(i)
                    for h in range(2):
                        if later(i):
                            v.wait_ge(s(f"stored{h}"), upto(g, f"stored{h}") + i * 16)
                        if later(i) or h:
                            v.wait_ge(s("state"), upto(g, "state") + i * 2 + h)
                        xk = cc.done(v.tensor_copy(mask_blk[:, h, :], same_dst[:, bass.ds(blk(i, h) * J, J)]))
                        v.wait_ge(s(f"gathered{h}"), upto(g, f"gathered{h}") + i * (16 * J) + 16 * J)
                        for k in range(J):
                            if k:
                                old = st[h][:, (k - 1) * D:k * D]
                            elif not later(i) and h == 0:
                                old = chunk_end[:, 0:D]
                            else:
                                old = st[1 - h][:, (J - 1) * D:J * D]
                            v.wait_ge(cc.sem, cc.value(xk))
                            ins = v.scalar_tensor_tensor(out=st[h][:, k * D:(k + 1) * D], in0=old,
                                                         scalar=mask_blk[:, h, k:k + 1],
                                                         in1=gb[h][:, k * D:(k + 1) * D], op0=ALU.mult, op1=ALU.add)
                            if k < J - 1:
                                xk = cc.done(ins)
                            else:
                                ins.then_inc(s("state"), 1)
                    assert cc.k == cc.per, (cc.k, cc.per)

                turns(v, body)
                chunk_ends(g, D)
                tell("chunk_end")
                v.wait_ge(s("end_t"), upto(g, "end_t") + 1)
                link(v.tensor_tensor_scan(chunk_in_t[0:D, 1:P + 1], flagrow["dst"][0:D, :], p_small[0:D, 0:P], 0.0,
                                          ALU.mult, ALU.add))
                tell("carry_t")
                v.wait_ge(s("carry"), upto(g, "carry") + 1)
                link(v.tensor_copy(chunk_in[:, 0:D], p_small[:, 384:384 + D]))
                v.wait_ge(s("fix_in"), upto(g, "fix_in") + 16)
                link(v.tensor_tensor(fix_rows[:, 0:D], fix_rows[:, 0:D], chunk_in[:, 0:D], ALU.add))
                tell("fixed")

            def conv_nodes(g, p):
                nodes_in(g, p)
                got, rows3 = gathered(D, p), part(conv_rows, p)
                link(v.tensor_tensor(got, got, per_node(has["dst"], p, D), ALU.mult))
                link(v.tensor_tensor(rows3, got, rows3, ALU.add))
                link(v.tensor_tensor(rows3, rows3, per_node(dinv, p, D), ALU.mult))
                link(v.tensor_tensor(rows3, rows3, every(bcv[g], p), ALU.add))
                link(v.tensor_scalar(rows3, rows3, 0.0, None, ALU.max))

            conv("c1")
            v.wait_ge(s("table_out"), upto("c2", "table_out"))
            for p in range(len(PARTS)):
                conv_nodes("c1", p)
                dense("c2", p, conv_rows)
                tell("table")
            conv("c2")
            v.wait_ge(s("table_out"), upto("at", "table_out"))
            for p in range(len(PARTS)):
                conv_nodes("c2", p)
                xp = part(x, p)
                link(v.tensor_tensor(xp, xp, part(conv_rows, p), ALU.add))
                layer_norm(p, xp, xp)
                dense("at", p, x)
                rows3 = part(hrows, p, W3)
                pr = local("s", p)
                for wv, to in ((asrc_w, rows3[:, :, D:W3]), (adst_w, part(work["adst"], p, HEADS))):
                    link(v.tensor_tensor(pr, rows3[:, :, 0:D], every(wv, p), ALU.mult))
                    link(v.tensor_reduce(to, pr.rearrange("p k (c d) -> p k c d", d=HD), AX.X, ALU.add))
                tell("table")

            v.wait_ge(s("adst_in"), 16)
            v.wait_ge(s("first_adst_in"), 16)
            adst = arena_b[:, 0:L * HEADS]
            adst_h = adst.rearrange("p (l c) -> p c l", c=HEADS)
            for hd in range(HEADS):
                link(v.tensor_tensor_scan(adst_h[:, hd, :], same_dst[:, :], adst_h[:, hd, :],
                                          first_adst[:, hd:hd + 1], ALU.mult, ALU.add))
            mx = late["mx"].rearrange("p (c j) -> p c j", j=J + 1)
            link(v.memset(mx[:, :, J:J + 1], 0.0))
            link(v.memset(chunk_end[:, :], 0.0))

            def hj(name):
                t = late[name]
                return t.rearrange("p (c j) -> p c j", j=J), t.rearrange("p (c j) -> p j c", j=J)

            (ex, ex_j), (lk, lk_j) = hj("ex"), hj("lk")
            sc = late["sc"]
            prod = late["prod"]
            prod4 = prod.rearrange("p (j c f) -> p j c f", c=HEADS, f=E16)
            wv4 = wedge[:, :].rearrange("p (o f c) -> p o c f", o=1, c=HEADS).to_broadcast([P, J, HEADS, E16])
            cf = late["cf"].rearrange("p (j w) -> p j w", w=W3)
            ca = Steps(s("chain"), 2 * (15 + HEADS + 2 * J), upto("at", "chain"))

            def per_head(ap3, n):
                return ap3.rearrange("p j (c o) -> p j c o", o=1).to_broadcast([P, J, HEADS, n])

            def body(i):
                ca.turn(i)

                def then(ins):
                    k = ca.done(ins)
                    v.wait_ge(ca.sem, ca.value(k))

                for h in range(2):
                    if later(i):
                        v.wait_ge(s(f"stored{h}"), upto("at", f"stored{h}") + i * 16)
                    if later(i) or h:
                        v.wait_ge(s("state"), upto("at", "state") + i * 2 + h)
                    m = mask_blk[:, h, :]
                    g3 = gb[h].rearrange("p (j w) -> p j w", w=W3)
                    ca.done(v.tensor_copy(m, same_dst[:, bass.ds(blk(i, h) * J, J)]))
                    ca.done(v.tensor_copy(mx[:, :, 0:1], mx[:, :, J:J + 1]))
                    v.wait_ge(s(f"a16_in{h}"), i * 16 + 16)
                    then(v.tensor_tensor(prod4, a16[h].rearrange("p j (o f) -> p j o f", o=1)
                                         .to_broadcast([P, J, HEADS, E16]), wv4, ALU.mult))
                    then(v.tensor_reduce(sc, prod.rearrange("p (a f) -> p a f", f=E16), AX.X, ALU.add))
                    then(v.tensor_tensor(sc, sc, adst[:, bass.ds(blk(i, h) * (J * HEADS), J * HEADS)], ALU.add))
                    v.wait_ge(s(f"gathered{h}"), upto("at", f"gathered{h}") + i * (16 * J) + 16 * J)
                    sc3 = sc.rearrange("p (j c) -> p j c", c=HEADS)
                    then(v.tensor_tensor(sc3, sc3, g3[:, :, D:W3], ALU.add))
                    then(v.scalar_tensor_tensor(out=lk_j, in0=sc3, scalar=0.2, in1=sc3, op0=ALU.mult, op1=ALU.max))
                    for hd in range(HEADS):
                        k = ca.done(v.tensor_tensor_scan(mx[:, hd, 1:J + 1], m, lk[:, hd, :], mx[:, hd, 0:1],
                                                         ALU.mult, ALU.max))
                    v.wait_ge(ca.sem, ca.value(k))
                    then(v.tensor_tensor(ex, mx[:, :, 0:J], bf(m, HEADS), ALU.mult))
                    then(v.tensor_tensor(ex, ex, mx[:, :, 1:J + 1], ALU.subtract))
                    then(v.tensor_tensor(lk, lk, mx[:, :, 1:J + 1], ALU.subtract))
                    v.sem_inc(s("at_args"), 1)
                    v.wait_ge(s("at_exp"), (i * 2 + h) * 2 + 2)
                    then(v.tensor_tensor(ex, ex, bf(m, HEADS), ALU.mult))
                    ca.done(v.tensor_copy(cf[:, :, 0:D].rearrange("p j (c d) -> p j c d", d=HD), per_head(ex_j, HD)))
                    ca.done(v.tensor_copy(cf[:, :, D:W3], ex_j))
                    hview = g3[:, :, 0:D].rearrange("p j (c d) -> p j c d", d=HD)
                    ca.done(v.tensor_tensor(hview, hview, per_head(lk_j, HD), ALU.mult))
                    ca.done(v.tensor_copy(g3[:, :, D:W3], lk_j))
                    s3 = st[h][:, 0:J * W3S].rearrange("p (j w) -> p j w", w=W3S)
                    then(v.tensor_copy(s3[:, :, W3:W3S], mx[:, :, 1:J + 1].rearrange("p c j -> p j c")))
                    for k in range(J):
                        if k:
                            old = s3[:, k - 1, 0:W3]
                        elif not later(i) and h == 0:
                            old = chunk_end[:, 0:W3]
                        else:
                            old = st[1 - h][:, (J - 1) * W3S:(J - 1) * W3S + W3]
                        tmp = late["tmp"][:, (k % 2) * W3:(k % 2 + 1) * W3]
                        then(v.tensor_tensor(tmp, old, cf[:, k, :], ALU.mult))
                        ins = v.tensor_tensor(s3[:, k, 0:W3], tmp, g3[:, k, :], ALU.add)
                        if k < J - 1:
                            then(ins)
                        else:
                            ins.then_inc(s("state"), 1)
                assert ca.k == ca.per

            turns(v, body)
            chunk_ends("at", W3S)
            link(v.tensor_copy(mrep[:, 0:D].rearrange("p (c d) -> p c d", d=HD), bc(chunk_end[:, W3:W3S], HD)))
            link(v.tensor_copy(mrep[:, D:W3], chunk_end[:, W3:W3S]))
            link(v.tensor_copy(mrep[:, W3:W3S], chunk_end[:, W3:W3S]))
            tell("chunk_end")
            v.wait_ge(s("end_t"), upto("at", "end_t") + 2)
            fr = flagrow["dst"][0:W3S, :]
            pm, psum_t = p_small[0:W3S, 256:384], p_small[0:W3S, 0:P]
            mo = chunk_max_t[0:W3S, :]
            t1, t2 = chunk_t1[0:W3S, :], chunk_t2[0:W3S, :]
            link(v.memset(chunk_max_t[:, 0:1], 0.0))
            link(v.tensor_tensor_scan(mo[:, 1:P + 1], fr, pm, 0.0, ALU.mult, ALU.max))
            link(v.tensor_tensor(t1, fr, mo[:, 0:P], ALU.mult))
            link(v.tensor_tensor(t1, t1, mo[:, 1:P + 1], ALU.subtract))
            link(v.tensor_tensor(t2, pm, mo[:, 1:P + 1], ALU.subtract))
            tell("at_chunk_args")
            v.wait_ge(s("at_chunk_exp"), 2)
            link(v.tensor_tensor(t1, t1, fr, ALU.mult))
            link(v.tensor_tensor(t2, t2, psum_t, ALU.mult))
            link(v.tensor_tensor_scan(chunk_in_t[0:W3S, 1:P + 1], t1, t2, 0.0, ALU.mult, ALU.add))
            tell("carry_t")
            v.wait_ge(s("carry"), upto("at", "carry") + 2)
            link(v.tensor_copy(chunk_in[:, 0:W3], p_small[:, 384:384 + W3]))
            link(v.tensor_copy(chunk_in[:, W3:W3S], p_small[:, W3:W3S]))
            v.wait_ge(s("fix_in"), upto("at", "fix_in") + 16)
            e_state, e_carry = fix_exp[:, 0:HEADS], fix_exp[:, HEADS:2 * HEADS]
            link(v.tensor_tensor(chunk_end[:, 0:HEADS], fix_rows[:, W3:W3S], chunk_in[:, W3:W3S], ALU.max))
            link(v.tensor_tensor(e_state, fix_rows[:, W3:W3S], chunk_end[:, 0:HEADS], ALU.subtract))
            link(v.tensor_tensor(e_carry, chunk_in[:, W3:W3S], chunk_end[:, 0:HEADS], ALU.subtract))
            tell("at_fix_args")
            v.wait_ge(s("at_fix_exp"), 1)
            for t, e in ((fix_rows, e_state), (chunk_in, e_carry)):
                by_head = t[:, 0:D].rearrange("p (c d) -> p c d", d=HD)
                link(v.tensor_tensor(by_head, by_head, bc(e, HD), ALU.mult))
                link(v.tensor_tensor(t[:, D:W3], t[:, D:W3], e, ALU.mult))
            link(v.tensor_tensor(fix_rows[:, 0:W3], fix_rows[:, 0:W3], chunk_in[:, 0:W3], ALU.add))
            tell("fixed")
            for p in range(len(PARTS)):
                nodes_in("at", p)
                got, y, xp = gathered(W3S, p), local("y", p), part(x, p)
                link(v.tensor_tensor(got[:, :, 0:W3], got[:, :, 0:W3], per_node(has["dst"], p, W3), ALU.mult))
                inv = local("e", p, HEADS)
                link(v.tensor_scalar(inv, got[:, :, D:W3], 1e-8, None, ALU.add))
                link(v.reciprocal(inv, inv))
                by_head = got[:, :, 0:D].rearrange("p k (c d) -> p k c d", d=HD)
                inv4 = inv.rearrange("p k (c o) -> p k c o", o=1).to_broadcast([P, by_head.shape[1], HEADS, HD])
                link(v.tensor_tensor(by_head, by_head, inv4, ALU.mult))
                link(v.tensor_tensor(y, got[:, :, 0:D], part(hrows, p, W3)[:, :, 0:D], ALU.add))
                layer_norm(p, y, y)
                link(v.tensor_tensor(y, y, every(gamma, p), ALU.mult))
                link(v.tensor_tensor(y, y, every(beta, p), ALU.add))
                link(v.tensor_tensor(xp, xp, y, ALU.add))
                layer_norm(p, xp, xp)
                tell("final")


_NAMES = {
    "x": "x", "src": "src", "dst": "dst", "a16": "edge_attr_16", "a32": "edge_attr_32", "w": "edge_weight",
    "u": "L1_gnn_u", "L1_W1": "L1_gnn_W1", "L1_b1": "L1_gnn_b1", "L1_W2": "L1_gnn_W2", "L1_b2": "L1_gnn_b2",
    "L2_W1": "L2_gnn_W1", "L2_b1": "L2_gnn_b1", "L2_W2": "L2_gnn_W2", "L2_b2": "L2_gnn_b2",
    "W_node": "L3_gnn_W_node", "W_edge": "L3_gnn_W_edge", "attn_src": "L3_gnn_attn_src",
    "attn_dst": "L3_gnn_attn_dst", "gamma": "L3_gnn_ln_gamma", "beta": "L3_gnn_ln_beta",
}


def kernel(**inputs):
    import numpy as np
    import concourse.bacc as bacc
    from concourse.bass_utils import run_bass_kernel_spmd

    nc = bacc.Bacc("TRN2", target_bir_lowering=False, num_devices=1)
    arrays, aps = {}, {}
    for short, name in _NAMES.items():
        v = np.asarray(inputs[name])
        rows_padded = {"x": NP, "src": EP, "dst": EP, "a16": EP, "a32": EP, "w": EP}.get(short)
        if rows_padded:
            full = np.full((rows_padded,) + v.shape[1:], N_NODES if short in ("src", "dst") else 0, v.dtype)
            full[:v.shape[0]] = v
            v = full
        v = np.ascontiguousarray(v)
        arrays[f"in_{short}"] = v
        aps[short] = nc.dram_tensor(f"in_{short}", v.shape, mybir.dt.from_np(v.dtype), kind="ExternalInput").ap()
    out = nc.dram_tensor("out_x", (NP, D), f32, kind="ExternalOutput").ap()
    program(nc, aps, out)
    r = run_bass_kernel_spmd(nc, [arrays], core_ids=[0])
    return r.results[0]["out_x"][:N_NODES]
```
